# Optimizing a Trainium2 kernel written in Bass

```python
import numpy as np
import jax
import jax.numpy as jnp

def _softmax(x, axis=-1):
    return jax.nn.softmax(x, axis=axis)

def _gelu(x):
    return jax.nn.gelu(x, approximate=True)

def _silu(x):
    return jax.nn.silu(x)

def _sigmoid(x):
    return jax.nn.sigmoid(x)

def _layernorm(x, axis=-1, eps=1e-05):
    m = jnp.mean(x, axis=axis, keepdims=True)
    v = jnp.var(x, axis=axis, keepdims=True)
    return (x - m) / jnp.sqrt(v + eps)

def _scatter_add(tgt, idx, src, axis=0):
    return tgt.at[idx].add(src)

def _segment_sum(src, seg, n):
    return jax.ops.segment_sum(src, seg, n)
kernel_name = 'mk_hybrid_d1_jaxref_r8_df8f7e'

def setup_inputs(seed: int=0):
    np.random.seed(seed)
    _w = jnp.asarray

    def _L0_attn_a_setup():
        import jax, jax.numpy as jnp
        import numpy as np

        def _gla_forward(hidden_state, Wq, bq, Wk, bk, Wv, bv, Wg, bg, Wo, bo):
            q = hidden_state @ Wq + bq
            k = jax.nn.sigmoid(hidden_state @ Wk + bk)
            g = jax.nn.sigmoid(hidden_state @ Wg + bg)
            v = hidden_state @ Wv + bv
            B = hidden_state.shape[0]
            K = Wq.shape[1]
            V = Wv.shape[1]
            state0 = jnp.zeros((B, K, V), dtype=hidden_state.dtype)

            def step(state, inp):
                q_t, k_t, g_t, v_t = inp
                state = state * g_t[:, :, None] + k_t[:, :, None] * v_t[:, None, :]
                out_t = jnp.einsum('bkv,bk->bv', state, q_t)
                return (state, out_t)
            xs = (jnp.swapaxes(q, 0, 1), jnp.swapaxes(k, 0, 1), jnp.swapaxes(g, 0, 1), jnp.swapaxes(v, 0, 1))
            final_state, outs = jax.lax.scan(step, state0, xs)
            out = jnp.swapaxes(outs, 0, 1)
            out = out @ Wo + bo
            return (out, final_state)

        def _reference_tuple_inner(hidden_state, Wq, bq, Wk, bk, Wv, bv, Wg, bg, Wo, bo):
            return _gla_forward(hidden_state, Wq, bq, Wk, bk, Wv, bv, Wg, bg, Wo, bo)
        key = jax.random.key(seed)
        ks = jax.random.split(key, 12)
        B, T, H, K, V, O = (8, 256, 128, 32, 32, 128)
        s = 0.02
        return {'hidden_state': jax.random.normal(ks[0], (B, T, H), dtype=jnp.float32), 'Wq': jax.random.normal(ks[1], (H, K), dtype=jnp.float32) * s, 'bq': jax.random.normal(ks[2], (K,), dtype=jnp.float32) * s, 'Wk': jax.random.normal(ks[3], (H, K), dtype=jnp.float32) * s, 'bk': jax.random.normal(ks[4], (K,), dtype=jnp.float32) * s, 'Wv': jax.random.normal(ks[5], (H, V), dtype=jnp.float32) * s, 'bv': jax.random.normal(ks[6], (V,), dtype=jnp.float32) * s, 'Wg': jax.random.normal(ks[7], (H, K), dtype=jnp.float32) * s, 'bg': jax.random.normal(ks[8], (K,), dtype=jnp.float32) * s, 'Wo': jax.random.normal(ks[9], (V, O), dtype=jnp.float32) * s, 'bo': jax.random.normal(ks[10], (O,), dtype=jnp.float32) * s}
    _L0_attn_a_in = _L0_attn_a_setup()

    def _L0_attn_b_setup():
        import jax, jax.numpy as jnp
        import numpy as np
        import math
        from jax import lax
        D_MODEL = 128
        D_STATE = 16
        D_CONV = 4
        EXPAND = 2
        D_INNER = EXPAND * D_MODEL
        DT_RANK = math.ceil(D_MODEL / 16)
        BATCH = 4
        SEQLEN = 256
        DT_MIN, DT_MAX = (0.001, 0.1)

        def _mamba_fwd(hidden_states, in_proj_w, conv_w, conv_b, x_proj_w, dt_proj_w, dt_proj_b, A_log, D_skip, out_proj_w):
            B, L, _ = hidden_states.shape
            xz = hidden_states @ in_proj_w
            x, z = jnp.split(xz, 2, axis=-1)
            p = D_CONV - 1
            x_ncl = jnp.transpose(x, (0, 2, 1))
            x_conv = lax.conv_general_dilated(x_ncl, conv_w[:, None, :], window_strides=(1,), padding=[(2 * p, p)], feature_group_count=D_INNER, dimension_numbers=('NCH', 'OIH', 'NCH'))[:, :, :L]
            x_conv = x_conv + conv_b[None, :, None]
            x_conv = jax.nn.silu(x_conv)
            x_bld = jnp.transpose(x_conv, (0, 2, 1))
            x_dbl = x_bld @ x_proj_w
            dt_low = x_dbl[..., :DT_RANK]
            Bc = x_dbl[..., DT_RANK:DT_RANK + D_STATE]
            Cc = x_dbl[..., DT_RANK + D_STATE:]
            dt = dt_low @ dt_proj_w + dt_proj_b
            delta = jax.nn.softplus(dt + dt_proj_b)
            A = -jnp.exp(A_log)

            def step(h, inp):
                d, u, b, c = inp
                dA = jnp.exp(d[..., None] * A)
                h = h * dA + (d * u)[..., None] * b[:, None, :]
                y = jnp.einsum('bdn,bn->bd', h, c)
                return (h, y)
            h0 = jnp.zeros((B, D_INNER, D_STATE), x_bld.dtype)
            inputs = (jnp.transpose(delta, (1, 0, 2)), jnp.transpose(x_bld, (1, 0, 2)), jnp.transpose(Bc, (1, 0, 2)), jnp.transpose(Cc, (1, 0, 2)))
            _, ys = lax.scan(step, h0, inputs)
            y = jnp.transpose(ys, (1, 0, 2)) + x_bld * D_skip
            y = y * jax.nn.silu(z)
            return y @ out_proj_w
        key = jax.random.key(seed)
        ks = jax.random.split(key, 9)
        hidden_states = jax.random.normal(ks[0], (BATCH, SEQLEN, D_MODEL), jnp.float32)
        in_proj_w = jax.random.normal(ks[1], (D_MODEL, 2 * D_INNER), jnp.float32) * D_MODEL ** (-0.5)
        conv_w = jax.random.normal(ks[2], (D_INNER, D_CONV), jnp.float32) * D_CONV ** (-0.5)
        conv_b = jax.random.normal(ks[3], (D_INNER,), jnp.float32) * 0.01
        x_proj_w = jax.random.normal(ks[4], (D_INNER, DT_RANK + 2 * D_STATE), jnp.float32) * D_INNER ** (-0.5)
        dt_std = DT_RANK ** (-0.5)
        dt_proj_w = jax.random.uniform(ks[5], (DT_RANK, D_INNER), jnp.float32, -dt_std, dt_std)
        dt = jnp.exp(jax.random.uniform(ks[6], (D_INNER,), jnp.float32) * (math.log(DT_MAX) - math.log(DT_MIN)) + math.log(DT_MIN))
        dt = jnp.clip(dt, 0.0001, None)
        dt_proj_b = dt + jnp.log(-jnp.expm1(-dt))
        A_log = jnp.log(jnp.tile(jnp.arange(1, D_STATE + 1, dtype=jnp.float32), (D_INNER, 1)))
        D_skip = jnp.ones((D_INNER,), jnp.float32)
        out_proj_w = jax.random.normal(ks[7], (D_INNER, D_MODEL), jnp.float32) * D_INNER ** (-0.5)
        return {'hidden_states': hidden_states, 'in_proj_w': in_proj_w, 'conv_w': conv_w, 'conv_b': conv_b, 'x_proj_w': x_proj_w, 'dt_proj_w': dt_proj_w, 'dt_proj_b': dt_proj_b, 'A_log': A_log, 'D_skip': D_skip, 'out_proj_w': out_proj_w}
    _L0_attn_b_in = _L0_attn_b_setup()

    def _L0_ffn_setup():
        import jax, jax.numpy as jnp
        import numpy as np
        DIM = 128
        DEPTH = 6
        HEADS = 16
        DIM_HEAD = 64
        WINDOW = 32
        INNER = HEADS * DIM_HEAD
        DIM_INNER = int(DIM * 4 * 2 / 3)
        QK_SCALE = 8.0

        def shift_tokens(t):
            a, s = jnp.split(t, 2, -1)
            s = jnp.pad(s, ((0, 0), (1, 0), (0, 0)))[:, :-1]
            return jnp.concatenate([a, s], -1)

        def l2norm(t):
            return t / jnp.maximum(jnp.linalg.norm(t, axis=-1, keepdims=True), 1e-12)

        def rotate_half(x):
            x1, x2 = jnp.split(x, 2, -1)
            return jnp.concatenate([-x2, x1], -1)

        def rotary_tables(n):
            half = jnp.arange(0, DIM_HEAD, 2, dtype=jnp.float32)
            inv_freq = 1.0 / 10000.0 ** (half / DIM_HEAD)
            t = jnp.arange(n, dtype=jnp.float32)
            freqs = t[:, None] * inv_freq[None, :]
            freqs = jnp.concatenate([freqs, freqs], -1)
            base_scale = (half + 0.4 * DIM_HEAD) / (1.4 * DIM_HEAD)
            power = (t - n // 2) / (WINDOW // 2)
            scale = base_scale[None, :] ** power[:, None]
            scale = jnp.concatenate([scale, scale], -1)
            return (freqs, scale)

        def local_attention(q, k, v):
            b, h, n, d = q.shape
            w = WINDOW
            nw = n // w
            bq = q.reshape(b, h, nw, w, d)
            bk = k.reshape(b, h, nw, w, d)
            bv = v.reshape(b, h, nw, w, d)

            def look(t):
                p = jnp.pad(t, ((0, 0), (0, 0), (1, 0), (0, 0), (0, 0)))
                return jnp.concatenate([p[:, :, :nw], p[:, :, 1:]], axis=3)
            bk2, bv2 = (look(bk), look(bv))
            seq = jnp.arange(n).reshape(nw, w)
            seq_p = jnp.pad(seq, ((1, 0), (0, 0)), constant_values=-1)
            jt = jnp.concatenate([seq_p[:nw], seq_p[1:]], axis=1)
            it = seq[:, :, None]
            jb = jt[:, None, :]
            mask = (it < jb) | (it > jb + w) | (jb == -1)
            sim = jnp.einsum('bhwie,bhwje->bhwij', bq, bk2) * QK_SCALE
            sim = jnp.where(mask, -jnp.finfo(sim.dtype).max, sim)
            attn = jax.nn.softmax(sim, -1)
            out = jnp.einsum('bhwij,bhwje->bhwie', attn, bv2)
            return out.reshape(b, h, n, d)

        def attn_layer(x, Wqkv, qs, ksc, Wo):
            b, n, _ = x.shape
            qkv = x @ Wqkv
            q, k, v = jnp.split(qkv, 3, -1)
            sh = lambda t: t.reshape(b, n, HEADS, DIM_HEAD).transpose(0, 2, 1, 3)
            q, k, v = (sh(q), sh(k), sh(v))
            q = l2norm(q) * qs
            k = l2norm(k) * ksc
            freqs, scale = rotary_tables(n)
            cos, sin = (jnp.cos(freqs), jnp.sin(freqs))
            q = q * cos * scale + rotate_half(q) * sin * scale
            inv = 1.0 / scale
            k = k * cos * inv + rotate_half(k) * sin * inv
            out = local_attention(q, k, v)
            out = out.transpose(0, 2, 1, 3).reshape(b, n, INNER)
            return out @ Wo

        def ffn_layer(x, g, bln, W1, b1, W2, b2):
            mu = x.mean(-1, keepdims=True)
            var = ((x - mu) ** 2).mean(-1, keepdims=True)
            xn = (x - mu) / jnp.sqrt(var + 1e-05) * g + bln
            hg = xn @ W1 + b1
            a, gate = jnp.split(hg, 2, -1)
            return a * jax.nn.gelu(gate, approximate=False) @ W2 + b2
        key = jax.random.key(seed)
        ks = jax.random.split(key, 8)
        B, N = (2, 256)
        init = lambda k, shape: jax.random.normal(k, shape, jnp.float32) * 0.02
        return {'x': jax.random.normal(ks[0], (B, N, DIM), jnp.float32), 'Wqkv': init(ks[1], (DEPTH, DIM, 3 * INNER)), 'q_scale': jnp.ones((DEPTH, DIM_HEAD), jnp.float32), 'k_scale': jnp.ones((DEPTH, DIM_HEAD), jnp.float32), 'Wo': init(ks[2], (DEPTH, INNER, DIM)), 'ln_g': jnp.ones((DEPTH, DIM), jnp.float32), 'ln_b': jnp.zeros((DEPTH, DIM), jnp.float32), 'W1': init(ks[3], (DEPTH, DIM, 2 * DIM_INNER)), 'b1': jnp.zeros((DEPTH, 2 * DIM_INNER), jnp.float32), 'W2': init(ks[4], (DEPTH, DIM_INNER, DIM)), 'b2': jnp.zeros((DEPTH, DIM), jnp.float32)}
    _L0_ffn_in = _L0_ffn_setup()
    _d = {'L0_attn_a_hidden_state': _L0_attn_a_in['hidden_state'], 'L0_attn_a_Wq': _L0_attn_a_in['Wq'], 'L0_attn_a_bq': _L0_attn_a_in['bq'], 'L0_attn_a_Wk': _L0_attn_a_in['Wk'], 'L0_attn_a_bk': _L0_attn_a_in['bk'], 'L0_attn_a_Wv': _L0_attn_a_in['Wv'], 'L0_attn_a_bv': _L0_attn_a_in['bv'], 'L0_attn_a_Wg': _L0_attn_a_in['Wg'], 'L0_attn_a_bg': _L0_attn_a_in['bg'], 'L0_attn_a_Wo': _L0_attn_a_in['Wo'], 'L0_attn_a_bo': _L0_attn_a_in['bo'], 'L0_attn_b_in_proj_w': _L0_attn_b_in['in_proj_w'], 'L0_attn_b_conv_w': _L0_attn_b_in['conv_w'], 'L0_attn_b_conv_b': _L0_attn_b_in['conv_b'], 'L0_attn_b_x_proj_w': _L0_attn_b_in['x_proj_w'], 'L0_attn_b_dt_proj_w': _L0_attn_b_in['dt_proj_w'], 'L0_attn_b_dt_proj_b': _L0_attn_b_in['dt_proj_b'], 'L0_attn_b_A_log': _L0_attn_b_in['A_log'], 'L0_attn_b_D_skip': _L0_attn_b_in['D_skip'], 'L0_attn_b_out_proj_w': _L0_attn_b_in['out_proj_w'], 'L0_ffn_Wqkv': _L0_ffn_in['Wqkv'], 'L0_ffn_q_scale': _L0_ffn_in['q_scale'], 'L0_ffn_k_scale': _L0_ffn_in['k_scale'], 'L0_ffn_Wo': _L0_ffn_in['Wo'], 'L0_ffn_ln_g': _L0_ffn_in['ln_g'], 'L0_ffn_ln_b': _L0_ffn_in['ln_b'], 'L0_ffn_W1': _L0_ffn_in['W1'], 'L0_ffn_b1': _L0_ffn_in['b1'], 'L0_ffn_W2': _L0_ffn_in['W2'], 'L0_ffn_b2': _L0_ffn_in['b2']}
    _x0 = _d['L0_attn_a_hidden_state']
    _d['L0_attn_a_hidden_state'] = jax.random.normal(jax.random.fold_in(jax.random.key(seed), 1), (4, 512, 128), dtype=_x0.dtype)
    del _x0
    return _d

def reference(L0_attn_a_hidden_state, L0_attn_a_Wq, L0_attn_a_bq, L0_attn_a_Wk, L0_attn_a_bk, L0_attn_a_Wv, L0_attn_a_bv, L0_attn_a_Wg, L0_attn_a_bg, L0_attn_a_Wo, L0_attn_a_bo, L0_attn_b_in_proj_w, L0_attn_b_conv_w, L0_attn_b_conv_b, L0_attn_b_x_proj_w, L0_attn_b_dt_proj_w, L0_attn_b_dt_proj_b, L0_attn_b_A_log, L0_attn_b_D_skip, L0_attn_b_out_proj_w, L0_ffn_Wqkv, L0_ffn_q_scale, L0_ffn_k_scale, L0_ffn_Wo, L0_ffn_ln_g, L0_ffn_ln_b, L0_ffn_W1, L0_ffn_b1, L0_ffn_W2, L0_ffn_b2):

    def _L0_attn_a_ref(hidden_state, Wq, bq, Wk, bk, Wv, bv, Wg, bg, Wo, bo):
        import jax, jax.numpy as jnp
        import numpy as np

        def _gla_forward(hidden_state, Wq, bq, Wk, bk, Wv, bv, Wg, bg, Wo, bo):
            q = hidden_state @ Wq + bq
            k = jax.nn.sigmoid(hidden_state @ Wk + bk)
            g = jax.nn.sigmoid(hidden_state @ Wg + bg)
            v = hidden_state @ Wv + bv
            B = hidden_state.shape[0]
            K = Wq.shape[1]
            V = Wv.shape[1]
            state0 = jnp.zeros((B, K, V), dtype=hidden_state.dtype)

            def step(state, inp):
                q_t, k_t, g_t, v_t = inp
                state = state * g_t[:, :, None] + k_t[:, :, None] * v_t[:, None, :]
                out_t = jnp.einsum('bkv,bk->bv', state, q_t)
                return (state, out_t)
            xs = (jnp.swapaxes(q, 0, 1), jnp.swapaxes(k, 0, 1), jnp.swapaxes(g, 0, 1), jnp.swapaxes(v, 0, 1))
            final_state, outs = jax.lax.scan(step, state0, xs)
            out = jnp.swapaxes(outs, 0, 1)
            out = out @ Wo + bo
            return (out, final_state)

        def _reference_tuple_inner(hidden_state, Wq, bq, Wk, bk, Wv, bv, Wg, bg, Wo, bo):
            return _gla_forward(hidden_state, Wq, bq, Wk, bk, Wv, bv, Wg, bg, Wo, bo)
        return _reference_tuple_inner(hidden_state, Wq, bq, Wk, bk, Wv, bv, Wg, bg, Wo, bo)[0]

    def _L0_attn_b_ref(hidden_states, in_proj_w, conv_w, conv_b, x_proj_w, dt_proj_w, dt_proj_b, A_log, D_skip, out_proj_w):
        import jax, jax.numpy as jnp
        import numpy as np
        import math
        from jax import lax
        D_MODEL = 128
        D_STATE = 16
        D_CONV = 4
        EXPAND = 2
        D_INNER = EXPAND * D_MODEL
        DT_RANK = math.ceil(D_MODEL / 16)
        BATCH = 4
        SEQLEN = 256
        DT_MIN, DT_MAX = (0.001, 0.1)

        def _mamba_fwd(hidden_states, in_proj_w, conv_w, conv_b, x_proj_w, dt_proj_w, dt_proj_b, A_log, D_skip, out_proj_w):
            B, L, _ = hidden_states.shape
            xz = hidden_states @ in_proj_w
            x, z = jnp.split(xz, 2, axis=-1)
            p = D_CONV - 1
            x_ncl = jnp.transpose(x, (0, 2, 1))
            x_conv = lax.conv_general_dilated(x_ncl, conv_w[:, None, :], window_strides=(1,), padding=[(2 * p, p)], feature_group_count=D_INNER, dimension_numbers=('NCH', 'OIH', 'NCH'))[:, :, :L]
            x_conv = x_conv + conv_b[None, :, None]
            x_conv = jax.nn.silu(x_conv)
            x_bld = jnp.transpose(x_conv, (0, 2, 1))
            x_dbl = x_bld @ x_proj_w
            dt_low = x_dbl[..., :DT_RANK]
            Bc = x_dbl[..., DT_RANK:DT_RANK + D_STATE]
            Cc = x_dbl[..., DT_RANK + D_STATE:]
            dt = dt_low @ dt_proj_w + dt_proj_b
            delta = jax.nn.softplus(dt + dt_proj_b)
            A = -jnp.exp(A_log)

            def step(h, inp):
                d, u, b, c = inp
                dA = jnp.exp(d[..., None] * A)
                h = h * dA + (d * u)[..., None] * b[:, None, :]
                y = jnp.einsum('bdn,bn->bd', h, c)
                return (h, y)
            h0 = jnp.zeros((B, D_INNER, D_STATE), x_bld.dtype)
            inputs = (jnp.transpose(delta, (1, 0, 2)), jnp.transpose(x_bld, (1, 0, 2)), jnp.transpose(Bc, (1, 0, 2)), jnp.transpose(Cc, (1, 0, 2)))
            _, ys = lax.scan(step, h0, inputs)
            y = jnp.transpose(ys, (1, 0, 2)) + x_bld * D_skip
            y = y * jax.nn.silu(z)
            return y @ out_proj_w
        return _mamba_fwd(hidden_states, in_proj_w, conv_w, conv_b, x_proj_w, dt_proj_w, dt_proj_b, A_log, D_skip, out_proj_w)

    def _L0_ffn_ref(x, Wqkv, q_scale, k_scale, Wo, ln_g, ln_b, W1, b1, W2, b2):
        import jax, jax.numpy as jnp
        import numpy as np
        DIM = 128
        DEPTH = 6
        HEADS = 16
        DIM_HEAD = 64
        WINDOW = 32
        INNER = HEADS * DIM_HEAD
        DIM_INNER = int(DIM * 4 * 2 / 3)
        QK_SCALE = 8.0

        def shift_tokens(t):
            a, s = jnp.split(t, 2, -1)
            s = jnp.pad(s, ((0, 0), (1, 0), (0, 0)))[:, :-1]
            return jnp.concatenate([a, s], -1)

        def l2norm(t):
            return t / jnp.maximum(jnp.linalg.norm(t, axis=-1, keepdims=True), 1e-12)

        def rotate_half(x):
            x1, x2 = jnp.split(x, 2, -1)
            return jnp.concatenate([-x2, x1], -1)

        def rotary_tables(n):
            half = jnp.arange(0, DIM_HEAD, 2, dtype=jnp.float32)
            inv_freq = 1.0 / 10000.0 ** (half / DIM_HEAD)
            t = jnp.arange(n, dtype=jnp.float32)
            freqs = t[:, None] * inv_freq[None, :]
            freqs = jnp.concatenate([freqs, freqs], -1)
            base_scale = (half + 0.4 * DIM_HEAD) / (1.4 * DIM_HEAD)
            power = (t - n // 2) / (WINDOW // 2)
            scale = base_scale[None, :] ** power[:, None]
            scale = jnp.concatenate([scale, scale], -1)
            return (freqs, scale)

        def local_attention(q, k, v):
            b, h, n, d = q.shape
            w = WINDOW
            nw = n // w
            bq = q.reshape(b, h, nw, w, d)
            bk = k.reshape(b, h, nw, w, d)
            bv = v.reshape(b, h, nw, w, d)

            def look(t):
                p = jnp.pad(t, ((0, 0), (0, 0), (1, 0), (0, 0), (0, 0)))
                return jnp.concatenate([p[:, :, :nw], p[:, :, 1:]], axis=3)
            bk2, bv2 = (look(bk), look(bv))
            seq = jnp.arange(n).reshape(nw, w)
            seq_p = jnp.pad(seq, ((1, 0), (0, 0)), constant_values=-1)
            jt = jnp.concatenate([seq_p[:nw], seq_p[1:]], axis=1)
            it = seq[:, :, None]
            jb = jt[:, None, :]
            mask = (it < jb) | (it > jb + w) | (jb == -1)
            sim = jnp.einsum('bhwie,bhwje->bhwij', bq, bk2) * QK_SCALE
            sim = jnp.where(mask, -jnp.finfo(sim.dtype).max, sim)
            attn = jax.nn.softmax(sim, -1)
            out = jnp.einsum('bhwij,bhwje->bhwie', attn, bv2)
            return out.reshape(b, h, n, d)

        def attn_layer(x, Wqkv, qs, ksc, Wo):
            b, n, _ = x.shape
            qkv = x @ Wqkv
            q, k, v = jnp.split(qkv, 3, -1)
            sh = lambda t: t.reshape(b, n, HEADS, DIM_HEAD).transpose(0, 2, 1, 3)
            q, k, v = (sh(q), sh(k), sh(v))
            q = l2norm(q) * qs
            k = l2norm(k) * ksc
            freqs, scale = rotary_tables(n)
            cos, sin = (jnp.cos(freqs), jnp.sin(freqs))
            q = q * cos * scale + rotate_half(q) * sin * scale
            inv = 1.0 / scale
            k = k * cos * inv + rotate_half(k) * sin * inv
            out = local_attention(q, k, v)
            out = out.transpose(0, 2, 1, 3).reshape(b, n, INNER)
            return out @ Wo

        def ffn_layer(x, g, bln, W1, b1, W2, b2):
            mu = x.mean(-1, keepdims=True)
            var = ((x - mu) ** 2).mean(-1, keepdims=True)
            xn = (x - mu) / jnp.sqrt(var + 1e-05) * g + bln
            hg = xn @ W1 + b1
            a, gate = jnp.split(hg, 2, -1)
            return a * jax.nn.gelu(gate, approximate=False) @ W2 + b2
        for i in range(DEPTH):
            x = attn_layer(shift_tokens(x), Wqkv[i], q_scale[i], k_scale[i], Wo[i]) + x
            x = ffn_layer(shift_tokens(x), ln_g[i], ln_b[i], W1[i], b1[i], W2[i], b2[i]) + x
        return x
    x = L0_attn_a_hidden_state
    x = x + _L0_attn_a_ref(_layernorm(x, axis=-1), L0_attn_a_Wq, L0_attn_a_bq, L0_attn_a_Wk, L0_attn_a_bk, L0_attn_a_Wv, L0_attn_a_bv, L0_attn_a_Wg, L0_attn_a_bg, L0_attn_a_Wo, L0_attn_a_bo)
    x = x + _L0_ffn_ref(_layernorm(x, axis=-1), L0_ffn_Wqkv, L0_ffn_q_scale, L0_ffn_k_scale, L0_ffn_Wo, L0_ffn_ln_g, L0_ffn_ln_b, L0_ffn_W1, L0_ffn_b1, L0_ffn_W2, L0_ffn_b2)
    x = x + _L0_attn_b_ref(_layernorm(x, axis=-1), L0_attn_b_in_proj_w, L0_attn_b_conv_w, L0_attn_b_conv_b, L0_attn_b_x_proj_w, L0_attn_b_dt_proj_w, L0_attn_b_dt_proj_b, L0_attn_b_A_log, L0_attn_b_D_skip, L0_attn_b_out_proj_w)
    x = x + _L0_ffn_ref(_layernorm(x, axis=-1), L0_ffn_Wqkv, L0_ffn_q_scale, L0_ffn_k_scale, L0_ffn_Wo, L0_ffn_ln_g, L0_ffn_ln_b, L0_ffn_W1, L0_ffn_b1, L0_ffn_W2, L0_ffn_b2)
    return x

_drawn_inputs = setup_inputs


def setup_inputs(seed=0):
    import zlib

    import numpy as np

    out = dict(_drawn_inputs(seed))
    spreads = {'L0_attn_b_D_skip': (1.0, 0.2),
     'L0_ffn_q_scale': (1.0, 0.6),
     'L0_ffn_k_scale': (1.0, 0.6),
     'L0_ffn_ln_g': (1.0, 0.6),
     'L0_ffn_ln_b': (0.0, 0.8),
     'L0_ffn_b1': (0.0, 0.581),
     'L0_ffn_b2': (0.0, 0.1)}
    factors = {'L0_attn_a_Wq': 2.754,
     'L0_attn_a_bq': 8.0,
     'L0_attn_a_Wk': 8.0,
     'L0_attn_a_bk': 8.0,
     'L0_attn_a_Wv': 2.903,
     'L0_attn_a_bv': 8.0,
     'L0_attn_a_Wg': 8.0,
     'L0_attn_a_bg': 8.0,
     'L0_attn_a_Wo': 2.908,
     'L0_attn_b_conv_b': 8.0,
     'L0_attn_b_x_proj_w': 7.212,
     'L0_attn_b_dt_proj_w': 8.0,
     'L0_attn_b_dt_proj_b': 8.0,
     'L0_attn_b_A_log': 8.0}
    for name, (base, spread) in spreads.items():
        noise = np.random.default_rng([zlib.crc32(name.encode()), seed]).standard_normal(out[name].shape)
        drawn = base * np.exp(spread * noise) if base else spread * noise
        out[name] = jnp.asarray(drawn.astype(out[name].dtype))
    for name, factor in factors.items():
        out[name] = (out[name] * factor).astype(out[name].dtype)
    return out
```

```python
import numpy as np
import concourse.bass as bass
from concourse import mybir
from contextlib import ExitStack

F32 = mybir.dt.float32
F32R = mybir.dt.float32r
BF16 = mybir.dt.bfloat16
I32 = mybir.dt.int32
ALU = mybir.AluOpType
ACT = mybir.ActivationFunctionType
AX = mybir.AxisListType

P = 128
B, T, D = 4, 512, 128
EPS = 1e-5
DEPTH, HEADS, DH, WIN = 6, 16, 64, 32
INNER = HEADS * DH
HP = HEADS // 2
QK_SCALE = 8.0
DI = int(D * 4 * 2 / 3)
DT_TILES = [(0, 128), (128, 128), (256, DI - 256)]
TILES = T // P
WPT = P // WIN
CH = 512
NCH = 3 * INNER // CH
HC = CH // DH
QKC = 2 * INNER // CH
WQ = 3 * INNER // 4
PHASE = DEPTH * B
NEWTON = 3
MAGIC = 0x5F3759DF
MASKED = -1e30
NVEC = 9
GK = 32
NST, DIN, RANK, CONV = 16, 256, 8, 4
XPW = RANK + 2 * NST
SHIFT = 2 * (CONV - 1)
LOG1P = [float(c) for c in np.polynomial.chebyshev.Chebyshev.interpolate(
    lambda e: np.log1p(e) / e, 11, domain=[0, 1]).convert(kind=np.polynomial.Polynomial).coef]


def cnt(it, per_unit, j, k=0):
    return it * (TILES * per_unit) + (per_unit * j + k)


def wait(eng, sem, value):
    if isinstance(value, int) and value <= 0:
        return
    eng.wait_ge(sem, value)


def build(nc, a):
    ctx = ExitStack()
    with ctx:
        def sb(name, shape, dt=F32):
            return ctx.enter_context(nc.sbuf_tensor(name, shape, dt))

        def sem(name):
            return ctx.enter_context(nc.semaphore(name))

        xm = sb("x_main", [P, B, T])
        xf = sb("x_ffn", [P, B, T + 1])
        ident = sb("ident", [P, P])
        center = sb("center", [P, P])
        mean = sb("mean", [P, P])
        onehot = sb("onehot", [64, 2, P], BF16)
        maskrow = sb("maskrow", [64, CH], BF16)
        eps_t = sb("eps_t", [P, 1])
        CONSTS = ((ident, "ident"), (center, "center"), (mean, "mean"), (onehot, "onehot"), (maskrow, "maskrow"))
        ln_xc = sb("ln_xc", [P, T])
        hidden = sb("hidden", [P, 3, T])
        gelu = sb("gelu", [P, 2, T])
        mlp_xs = hidden[:, 0, :]
        ln_sq = hidden[:, 1, :]
        ln_std = gelu[:, 0, :]
        ln_rstd = gelu[:, 1, :]

        psum = ctx.enter_context(nc.psum_tensor("psum", [P, 8, CH], F32))
        proj_ps = [psum[:, 0, :], psum[:, 1, :]]
        tr_ps = [psum[:, 2, :], psum[:, 3, :]]
        s_ps = [psum[:, 4, :], psum[:, 5, :]]
        o_ps = [psum[:, 6, :], psum[:, 7, :]]

        consts = sem("consts")
        rot_in = sem("rot_in")
        zeroed = sem("zeroed")
        x_in = sem("x_in")
        x_tr = sem("x_tr")
        x_ready = sem("x_ready")
        lnc_mm, lnx_ev, lnv_mm, lnstd_done, ln_rs = (
            sem(n) for n in ("lnc_mm", "lnx_ev", "lnv_mm", "lnstd_done", "ln_rs"))
        out_tr, out_ev, out_st = sem("out_tr"), sem("out_ev"), sem("out_st")
        added = sem("added")

        wqkv_hi = sb("wqkv_hi", [P, 2, 3 * INNER], F32R)
        wqkv_lo = sb("wqkv_lo", [P, 2, 3 * INNER], F32R)
        wqkv_staged = sb("wqkv_staged", [P, 1, WQ])
        fctx = ctx.enter_context(ExitStack())

        def fsb(name, shape, dt=F32):
            return fctx.enter_context(nc.sbuf_tensor(name, shape, dt))

        def ffn_buffers():
            m = {}
            m["wh"], m["wl"], m["wst"] = wqkv_hi, wqkv_lo, wqkv_staged
            m["wo"] = fsb("wo", [P, HP, D])
            m["w1"] = fsb("w1", [P, 2 * DI])
            m["w2"] = fsb("w2", [P, 3, D])
            m["vec"] = fsb("layer_vectors", [P, NVEC])
            m["rot"] = fsb("rot_base", [P, TILES, 4 * DH])
            m["rots"] = fsb("rot_scaled", [P, TILES, 4 * DH])
            m["qks"] = fsb("qk_scale", [P, 4 * DH])
            m["xh"] = fsb("xs_hi", [P, 2, P], F32R)
            m["xl"] = fsb("xs_lo", [P, 2, P], F32R)
            m["sq"] = fsb("squares", [P, 2, CH])
            m["ma"] = fsb("rot_cos", [P, 2, CH])
            m["mb"] = fsb("rot_sin", [P, 2, CH])
            m["qk"] = fsb("qk_rows", [P, 2, 2 * INNER])
            m["ss"] = fsb("sumsq", [P, 2 * HEADS])
            m["ny"] = fsb("newton_y", [P, 2 * HEADS])
            m["nt"] = fsb("newton_t", [P, 2 * HEADS])
            m["rn"] = fsb("rnorm", [P, 2, 2 * HEADS])
            m["v"] = fsb("v_rows", [P, 2, 2, HP * DH])
            m["vp"] = fsb("v_pairs", [P, 2, WPT, HP * DH])
            m["qt"] = fsb("q_t", [P, HP, P])
            m["kt"] = fsb("k_t", [P, HP, WIN + T])
            m["mx"] = fsb("row_max", [P, 2, HP])
            m["p"] = fsb("probs", [P, HP, 2, 2 * WIN])
            m["d"] = m["p"]
            m["pt"] = fsb("probs_t", [P, HP, P])
            m["den"] = fsb("den", [P, 2, HP])
            m["rden"] = fsb("rden", [P, 2, 2, HP])
            m["o"] = fsb("o_rows", [P, HP, 2, DH])
            m["ot"] = fsb("o_t", [P, HP, T])
            m["xn"] = fsb("xn_mlp", [P, T])
            m["gl"], m["h"], m["xs"] = gelu, hidden, mlp_xs
            return m

        m = ffn_buffers()
        fctx.close()

        def gla_buffers():
            gb = {}
            gb["w"] = fsb("gla_w", [P, 4, GK])
            gb["b"] = fsb("gla_b", [P, 4])
            gb["wo"] = fsb("gla_wo", [P, B, D])
            gb["bo"] = fsb("gla_bo", [P, 1])
            gb["pick"] = fsb("gla_pick", [P, 4 * (2 * GK - 1)])
            gb["q"] = fsb("gla_q", [P, T])
            gb["k"] = fsb("gla_k", [P, T])
            gb["g"] = fsb("gla_g", [P, T])
            gb["v"] = fsb("gla_v", [P, T])
            gb["zero"] = fsb("gla_zero", [P, P])
            gb["spread"] = fsb("gla_spread", [P, 2, B, GK])
            gb["gather"] = fsb("gla_gather", [P, 2, P])
            gb["kv"] = fsb("gla_kv", [P, 2, T])
            gb["st"] = fsb("gla_state", [P, 2, T])
            gb["sq"] = fsb("gla_state_q", [P, 2, T])
            gb["o"] = fsb("gla_out", [P, T])
            return gb

        gb = gla_buffers()
        fctx.close()

        def mamba_buffers():
            mb = {}
            mb["win"] = fsb("mb_in_w", [P, 2 * DIN])
            mb["conv"] = fsb("mb_conv", [P, 2, CONV])
            mb["cols"] = fsb("mb_cols", [P, 2, 3])
            mb["xw"] = fsb("mb_x_w", [P, 2, 3 * XPW])
            mb["dtw"] = fsb("mb_dt_w", [RANK, DIN])
            mb["alog"] = fsb("mb_alog", [P, 2, NST])
            mb["a"] = fsb("mb_a", [P, 2, NST])
            mb["wout"] = fsb("mb_out_w", [P, 2, D])
            mb["part"] = fsb("mb_part", [3 * XPW, 3])
            mb["bc"] = fsb("mb_bc_pick", [3 * XPW, 2 * NST, P], BF16)
            mb["xp"] = fsb("mb_x", [P, 2, SHIFT + T])
            mb["zs"] = fsb("mb_z", [P, 2, T])
            mb["cv"] = fsb("mb_conv_out", [P, 2, T])
            mb["u"] = fsb("mb_u", [P, 2, T])
            mb["xd"] = fsb("mb_xdbl", [3 * XPW, T])
            mb["hi"] = fsb("mb_hi", [3 * XPW, T], BF16)
            mb["mid"] = fsb("mb_mid", [3 * XPW, T], BF16)
            mb["r1"] = fsb("mb_rest", [3 * XPW, T])
            mb["r2"] = fsb("mb_rest2", [3 * XPW, T])
            mb["pa"] = fsb("mb_parts_a", [3 * XPW, T])
            mb["pb"] = fsb("mb_parts_b", [3 * XPW, T])
            mb["parts"] = fsb("mb_parts", [3 * XPW, T], BF16)
            mb["y"] = fsb("mb_dt", [P, 2, T])
            mb["ab"] = fsb("mb_dt_abs", [P, 2, T])
            mb["e"] = fsb("mb_dt_exp", [P, 2, T])
            mb["pl"] = fsb("mb_poly", [P, 2, T])
            mb["dl"] = fsb("mb_delta", [P, 2, T])
            mb["du"] = fsb("mb_du", [P, 2, T])
            mb["da"] = fsb("mb_decay", [P, 2, T])
            mb["bu"] = fsb("mb_bu", [P, 2, T])
            mb["h"] = fsb("mb_h", [P, 2, T])
            mb["c"] = fsb("mb_c", [P, 2, T])
            mb["hc"] = fsb("mb_hc", [P, 2, T])
            mb["yo"] = fsb("mb_y", [P, 2, T])
            return mb

        mb = mamba_buffers()
        gs = {n: sem("g_" + n) for n in (
            "in", "zero", "proj_mm", "proj_ev", "sel", "vb_mm", "kv", "st", "sq", "sum_mm", "o_ev", "out_mm")}
        ms = {n: sem("m_" + n) for n in (
            "in", "zero", "a1", "a2", "in_mm", "x_ev", "z_ev", "conv", "u_ev", "xd_mm", "xd_ev", "split", "dt_mm",
            "dt_ev", "abs", "exp", "poly", "du", "da", "b_mm", "c_mm", "bu", "h", "c_ev", "hc", "y_mm", "yo",
            "out_mm", "added")}
        S = {n: sem(n) for n in (
            "xs_hi", "xs_lo", "wstaged", "whi_done", "wconv", "qkv_mm", "sq_done", "m_done", "red_done",
            "newton", "add_done", "rot_done", "v_ev", "vp0", "vp1", "oT_mm", "oT_ev", "qkT_mm",
            "qkT_ev", "s_mm", "max_done", "sub_done", "exp_done", "den_sum", "den_done", "pT_mm", "pT_ev",
            "o_mm", "o_ev", "wo_in", "w1_in", "w2_in", "vec_in", "qks_in", "rots_done", "d1_mm", "d1_ev",
            "mlp_xs", "d2_mm", "xc_ev", "d3_mm", "std_done", "rstd_done", "xn1", "xn2", "d4_mm",
            "gelu_done", "h_done", "hidden_done", "d5_mm", "stream")}
        ln_done = [sem("ln0_done"), S["stream"], sem("ln2_done"), sem("ln3_done")]
        vp_sem = [S["vp0"], S["vp1"]]

        def pe_proj(it, u):
            j, e = u, (it + (u // TILES))
            par = (e // B) % 2
            nc.tensor.wait_ge(S["xs_lo"], cnt(it, 1, j, 1))
            nc.tensor.wait_ge(S["wconv"], (e // B) * B + B)
            for c in range(NCH):
                if c < 2:
                    wait(nc.tensor, S["v_ev"], cnt(it, 2, j, c - 1))
                else:
                    wait(nc.tensor, S["sq_done"], cnt(it, QKC, j, c - 1))
                    wait(nc.tensor, S["m_done"], cnt(it, QKC, j, c - 1))
                cols = slice(c * CH, (c + 1) * CH)
                xh, xl = m["xh"][:, u % 2, :], m["xl"][:, u % 2, :]
                wh, wl = m["wh"][:, par, cols], m["wl"][:, par, cols]
                out = proj_ps[c % 2]
                nc.tensor.matmul(out, xh, wh, start=True, stop=False)
                nc.tensor.matmul(out, xh, wl, start=False, stop=False)
                nc.tensor.matmul(out, xl, wh, start=False, stop=True).then_inc(S["qkv_mm"], 1)

        def pe_out_t(it, u):
            for g in range(2):
                nc.tensor.wait_ge(S["o_ev"], cnt(it, 2, u, 2))
                wait(nc.tensor, S["pT_ev"], cnt(it, 2, u, g + 1))
                for i in range(4):
                    hp = 4 * g + i
                    last = nc.tensor.transpose(tr_ps[g][:, i * P:(i + 1) * P],
                                               m["o"][:, hp, :, :].rearrange("p a e -> p (a e)"),
                                               ident[:, :])
                last.then_inc(S["oT_mm"], 1)

        def pe_qk_t(it, u, after):
            for g in range(4):
                nc.tensor.wait_ge(S["rot_done"], cnt(it, QKC, u, g + 1))
                if g >= 2:
                    nc.tensor.wait_ge(S["qkT_ev"], cnt(it, 4, u, g - 1))
                elif after:
                    wait(nc.tensor, S["oT_ev"], cnt(it, 2, u - 2, g + 1))
                for i in range(4):
                    last = nc.tensor.transpose(tr_ps[g % 2][:, i * P:(i + 1) * P],
                                               m["qk"][:, u % 2, (4 * g + i) * P:(4 * g + i + 1) * P],
                                               ident[:, :])
                last.then_inc(S["qkT_mm"], 1)

        def pe_probs_t(it, u, qk_after, out_before):
            nc.tensor.wait_ge(vp_sem[u % 2], it * 512 + 256 * (u // 2 + 1))
            for g in range(2):
                nc.tensor.wait_ge(S["exp_done"], cnt(it, 2, u, 2))
                if qk_after:
                    nc.tensor.wait_ge(S["qkT_ev"], cnt(it, 4, u + 1, g + 3))
                elif out_before:
                    nc.tensor.wait_ge(S["oT_ev"], cnt(it, 2, u - 1, g + 1))
                for i in range(4):
                    hp = 4 * g + i
                    last = nc.tensor.transpose(tr_ps[g][:, i * P:(i + 1) * P],
                                               m["p"][:, hp, :, :].rearrange("p a k -> p (a k)"),
                                               ident[:, :])
                last.then_inc(S["pT_mm"], 1)

        def pe_scores(it, u):
            t = u % TILES
            nc.tensor.wait_ge(S["qkT_ev"], cnt(it, 4, u, 4))
            for g in range(2):
                wait(nc.tensor, S["sub_done"], cnt(it, 2, u - 1, g + 1))
                nc.tensor.matmul(s_ps[g], onehot[:, 1 if t == 0 else 0, :], maskrow[:, :], start=True, stop=False,
                                 skip_group_check=True)
            for hp in range(HP):
                for par in range(2):
                    rows = slice(64 * par, 64 * par + 64)
                    for w in range(WPT):
                        last = nc.tensor.matmul(
                            s_ps[par][WIN * w:WIN * w + WIN, 64 * hp:64 * hp + 64],
                            m["qt"][rows, hp, WIN * w:WIN * w + WIN],
                            m["kt"][rows, hp, t * P + WIN * w:t * P + WIN * w + 2 * WIN],
                            start=False, stop=True, skip_group_check=True)
                    if hp == HP - 1:
                        last.then_inc(S["s_mm"], 1)

        def pe_pv(it, u):
            nc.tensor.wait_ge(S["pT_ev"], cnt(it, 2, u, 2))
            wait(nc.tensor, S["o_ev"], cnt(it, 2, u))
            for hp in range(HP):
                for par in range(2):
                    rows = slice(64 * par, 64 * par + 64)
                    for w in range(WPT):
                        last = nc.tensor.matmul(
                            o_ps[par][WIN * w:WIN * w + WIN, 64 * hp:64 * hp + 64],
                            m["pt"][rows, hp, WIN * w:WIN * w + WIN],
                            m["vp"][rows, u % 2, w, DH * hp:DH * hp + DH],
                            start=True, stop=True)
                    if hp == HP - 1:
                        last.then_inc(S["o_mm"], 1)

        def pe_wo(e):
            nc.tensor.wait_ge(S["wo_in"], (e + 1) * 16)
            nc.tensor.wait_ge(S["oT_ev"], (e + 1) * 8)
            nc.tensor.wait_ge(S["o_ev"], (e + 1) * 8 - 1)
            for hp in range(HP):
                last = nc.tensor.matmul(o_ps[0], m["wo"][:, hp, :], m["ot"][:, hp, :],
                                        start=(hp == 0), stop=(hp == HP - 1))
            last.then_inc(S["d1_mm"], 1)

        def pe_center(e, o_free):
            wait(nc.tensor, S["o_ev"], o_free)
            nc.tensor.wait_ge(S["mlp_xs"], e + 1)
            nc.tensor.matmul(o_ps[0], center[:, :], m["xs"][:, :], start=True, stop=True).then_inc(S["d2_mm"], 1)

        def pe_var(e, o_free):
            wait(nc.tensor, S["o_ev"], o_free)
            nc.tensor.wait_ge(S["xc_ev"], 2 * (e + 1))
            nc.tensor.matmul(o_ps[1], mean[:, :], ln_sq[:, :], start=True, stop=True).then_inc(S["d3_mm"], 1)

        def pe_up(e, j, o_free):
            if j == 0:
                wait(nc.tensor, S["o_ev"], o_free)
                nc.tensor.wait_ge(S["w1_in"], (e + 1) * 16)
                nc.tensor.wait_ge(S["xn2"], e + 1)
            else:
                nc.tensor.wait_ge(S["h_done"], 2 * e + j)
                nc.tensor.wait_ge(S["gelu_done"], 3 * e + j)
            at, n = DT_TILES[j]
            nc.tensor.matmul(o_ps[1][:n, :], m["w1"][:, DI + at:DI + at + n], m["xn"][:, :], start=True, stop=True)
            nc.tensor.matmul(o_ps[0][:n, :], m["w1"][:, at:at + n], m["xn"][:, :],
                             start=True, stop=True).then_inc(S["d4_mm"], 1)

        def pe_down(e, o_free):
            wait(nc.tensor, S["o_ev"], o_free)
            nc.tensor.wait_ge(S["w2_in"], (e + 1) * 32)
            nc.tensor.wait_ge(S["hidden_done"], e + 1)
            for j, (_, n) in enumerate(DT_TILES):
                last = nc.tensor.matmul(o_ps[0], m["w2"][:n, j, :], m["h"][:n, j, :], start=(j == 0), stop=(j == 2))
            last.then_inc(S["d5_mm"], 1)

        def pe_pv_banks(e, u):
            if u == 0:
                nc.tensor.wait_ge(S["d1_ev"], e + 1)
            elif u == 1:
                nc.tensor.wait_ge(S["xc_ev"], 2 * (e + 1))
                nc.tensor.wait_ge(S["std_done"], e + 1)
            elif u == 2:
                nc.tensor.wait_ge(S["hidden_done"], e + 1)
            else:
                nc.tensor.wait_ge(S["stream"], B + e + 1)

        def pe_body(it, mlp, ahead, attn=True):
            for u in range(TILES):
                o_free = cnt(it, 2, u)
                if ahead or u + 2 < TILES:
                    pe_proj(it, u + 2)
                if mlp and u == 1:
                    pe_center(it - 1, o_free)
                if mlp and u == 2:
                    pe_up(it - 1, 0, o_free)
                if mlp and u == 3:
                    pe_down(it - 1, o_free)
                if mlp or u > 0:
                    pe_out_t(it, u - 1)
                nxt = ahead or u + 1 < TILES
                if nxt:
                    pe_qk_t(it, u + 1, mlp or u > 0)
                if mlp and u == 0:
                    pe_wo(it - 1)
                if mlp and u == 1:
                    pe_var(it - 1, o_free)
                if mlp and u == 2:
                    pe_up(it - 1, 1, o_free)
                pe_probs_t(it, u, nxt, mlp or u > 0)
                if mlp and u == 2:
                    pe_up(it - 1, 2, o_free)
                if mlp and u == 3:
                    pe_pv_banks(it - 1, u)
                if nxt:
                    pe_scores(it, u + 1)
                nc.tensor.wait_ge(consts, 16 * len(CONSTS))
                if mlp and u < 3:
                    pe_pv_banks(it - 1, u)
                pe_pv(it, u)

        def pe_ffn(first):
            last = first + PHASE - 1
            pe_proj(first, 0)
            pe_proj(first, 1)
            pe_qk_t(first, 0, False)
            pe_scores(first, 0)
            pe_body(first, False, True)
            if first == 0:
                pe_body(1, True, True)
            with nc.tensor.Fori(max(first + 1, 2), last) as it:
                pe_body(it, True, True)
            pe_body(last, True, False)
            pe_out_t(last, 3)
            pe_wo(last)
            pe_center(last, 0)
            pe_var(last, 0)
            for j in range(3):
                pe_up(last, j, 0)
            pe_down(last, 0)

        def act_proj(it, u):
            for c in range(QKC):
                nc.scalar.wait_ge(S["qkv_mm"], cnt(it, NCH, u, c + 1))
                wait(nc.scalar, S["red_done"], cnt(it, QKC, u, c - 1))
                nc.scalar.activation(m["sq"][:, c % 2, :], proj_ps[c % 2], ACT.Square).then_inc(S["sq_done"], 1)
            for c in range(2):
                nc.scalar.wait_ge(S["qkv_mm"], cnt(it, NCH, u, QKC + c + 1))
                if c == 0:
                    wait(nc.scalar, vp_sem[u % 2], it * 512 + 256 * (u // 2))
                    wait(nc.scalar, vp_sem[(u + 1) % 2], it * 512 + 256 * ((u - 1) // 2 + 1))
                nc.scalar.activation(
                    m["v"][:, u % 2, :, 256 * c:256 * c + 256].rearrange("p a (i e) -> p i a e", e=DH),
                    proj_ps[c % 2].rearrange("p (i a e) -> p i a e", a=2, e=DH), ACT.Copy).then_inc(S["v_ev"], 1)

        def act_out_t(it, u):
            t = u % TILES
            for g in range(2):
                nc.scalar.wait_ge(S["oT_mm"], cnt(it, 2, u, g + 1))
                if t == 0:
                    wait(nc.scalar, S["d1_mm"], it + u // TILES)
                nc.scalar.activation(m["ot"][:, 4 * g:4 * g + 4, t * P:(t + 1) * P],
                                     tr_ps[g].rearrange("p (i q) -> p i q", i=4), ACT.Copy).then_inc(S["oT_ev"], 1)

        def act_qk_t(it, u):
            t = u % TILES
            wait(nc.scalar, S["s_mm"], cnt(it, 2, u))
            for g in range(4):
                nc.scalar.wait_ge(S["qkT_mm"], cnt(it, 4, u, g + 1))
                hp = 4 * (g % 2)
                out = (m["qt"][:, hp:hp + 4, :] if g < 2
                       else m["kt"][:, hp:hp + 4, WIN + t * P:WIN + (t + 1) * P])
                nc.scalar.activation(out, tr_ps[g % 2].rearrange("p (i q) -> p i q", i=4), ACT.Copy)\
                    .then_inc(S["qkT_ev"], 1)

        def act_probs_t(it, u):
            for g in range(2):
                nc.scalar.wait_ge(S["pT_mm"], cnt(it, 2, u, g + 1))
                wait(nc.scalar, S["o_mm"], cnt(it, 2, u - 1, g + 1))
                nc.scalar.activation(m["pt"][:, 4 * g:4 * g + 4, :], tr_ps[g].rearrange("p (i q) -> p i q", i=4),
                                     ACT.Copy).then_inc(S["pT_ev"], 1)

        def act_exp(it, u):
            for g in range(2):
                nc.scalar.wait_ge(S["sub_done"], cnt(it, 2, u, g + 1))
                nc.scalar.activation(m["p"][:, :, g, :], m["d"][:, :, g, :], ACT.Exp,
                                     scale=QK_SCALE).then_inc(S["exp_done"], 1)

        def act_center(e):
            nc.scalar.wait_ge(S["d2_mm"], e + 1)
            wait(nc.scalar, S["xn1"], e)
            nc.scalar.activation(ln_xc[:, :], o_ps[0], ACT.Copy).then_inc(S["xc_ev"], 1)
            wait(nc.scalar, S["d3_mm"], e)
            nc.scalar.activation(ln_sq[:, :], o_ps[0], ACT.Square).then_inc(S["xc_ev"], 1)

        def act_std(e):
            nc.scalar.wait_ge(S["d3_mm"], e + 1)
            wait(nc.scalar, S["rstd_done"], e)
            nc.scalar.activation(ln_std[:, :], o_ps[1], ACT.Sqrt, bias=eps_t[:, :]).then_inc(S["std_done"], 1)

        def act_gelu(e, j):
            n = DT_TILES[j][1]
            nc.scalar.wait_ge(S["d4_mm"], 3 * e + j + 1)
            if j == 0:
                nc.scalar.wait_ge(S["vec_in"], (e + 1) * 16)
            if j == 0:
                wait(nc.scalar, S["hidden_done"], e)
            if j == 2:
                nc.scalar.wait_ge(S["h_done"], 2 * e + 1)
            nc.scalar.activation(m["gl"][:n, j % 2, :], o_ps[1][:n, :], ACT.Gelu,
                                 bias=m["vec"][:n, 5 + j:6 + j]).then_inc(S["gelu_done"], 1)

        def act_body(it, mlp, ahead):
            for u in range(TILES):
                if ahead or u + 2 < TILES:
                    act_proj(it, u + 2)
                if mlp and u == 1:
                    act_center(it - 1)
                if mlp and u == 2:
                    act_gelu(it - 1, 0)
                if mlp or u > 0:
                    act_out_t(it, u - 1)
                nxt = ahead or u + 1 < TILES
                if nxt:
                    act_qk_t(it, u + 1)
                if mlp and u == 1:
                    act_std(it - 1)
                if mlp and u == 2:
                    act_gelu(it - 1, 1)
                act_probs_t(it, u)
                if mlp and u == 2:
                    act_gelu(it - 1, 2)
                if nxt:
                    act_exp(it, u + 1)

        def act_ffn(first):
            last = first + PHASE - 1
            act_proj(first, 0)
            act_proj(first, 1)
            act_qk_t(first, 0)
            act_exp(first, 0)
            act_body(first, False, True)
            if first == 0:
                act_body(1, True, True)
            with nc.scalar.Fori(max(first + 1, 2), last) as it:
                act_body(it, True, True)
            act_body(last, True, False)
            act_out_t(last, 3)
            act_center(last)
            act_std(last)
            for j in range(3):
                act_gelu(last, j)

        V = nc.vector

        def dve_xs(it, u):
            t, b = u % TILES, (it + u // TILES) % B
            wait(V, S["qkv_mm"], cnt(it, NCH, u - 1))
            V.wait_ge(S["stream"], it + u // TILES + 1)
            halves = [(slice(0, 64), xf[0:64, b, 1 + t * P:1 + (t + 1) * P]),
                      (slice(64, 128), xf[64:128, b, t * P:(t + 1) * P])]
            for rows, src in halves:
                V.tensor_scalar(m["xh"][rows, u % 2, :], src, 1.0, None, ALU.mult).then_inc(S["xs_hi"], 1)
            V.wait_ge(S["xs_hi"], cnt(it, 2, u, 2))
            for rows, src in halves:
                last_ = V.tensor_tensor(m["xl"][rows, u % 2, :], src, m["xh"][rows, u % 2, :].bitcast(F32), ALU.subtract)
            last_.then_inc(S["xs_lo"], 1)

        def dve_tables(e):
            V.wait_ge(S["qks_in"], (e + 1) * 16)
            wait(V, S["m_done"], e * (TILES * QKC))
            V.tensor_tensor(m["rots"][:, :, :], m["rot"][:, :, :],
                            m["qks"][:, :].unsqueeze(1).to_broadcast([P, TILES, 4 * DH]), ALU.mult)\
                .then_inc(S["rots_done"], 1)

        def dve_rotate(it, u):
            t = u % TILES
            if t == 0:
                V.wait_ge(S["rots_done"], it + u // TILES + 1)
            for c in range(QKC):
                o = 2 * DH * (c // 2)
                ps = proj_ps[c % 2].rearrange("p (h e) -> p h e", e=DH)
                ma = m["ma"][:, c % 2, :].rearrange("p (h e) -> p h e", e=DH)
                mb = m["mb"][:, c % 2, :].rearrange("p (h e) -> p h e", e=DH)
                cos = m["rots"][:, t, o:o + DH].unsqueeze(1).to_broadcast([P, HC, DH])
                sin = m["rots"][:, t, o + DH:o + 2 * DH].unsqueeze(1).to_broadcast([P, HC, DH])
                V.wait_ge(S["sq_done"], cnt(it, QKC, u, c + 1))
                wait(V, S["add_done"], cnt(it, QKC, u, c - 1))
                V.tensor_tensor(ma, ps, cos, ALU.mult)
                V.tensor_tensor(mb[:, :, 0:32], ps[:, :, 32:64], sin[:, :, 0:32], ALU.mult)
                V.tensor_tensor(mb[:, :, 32:64], ps[:, :, 0:32], sin[:, :, 32:64], ALU.mult).then_inc(S["m_done"], 1)
                V.tensor_reduce(m["ss"][:, HC * c:HC * c + HC],
                                m["sq"][:, c % 2, :].rearrange("p (h e) -> p h e", e=DH), AX.X, ALU.add)\
                    .then_inc(S["red_done"], 1)

        NLINK = 4 + 3 * NEWTON

        def dve_rnorm(it, u):
            n = [0]

            def link(ins):
                n[0] += 1
                ins.then_inc(S["newton"], 1)
                V.wait_ge(S["newton"], cnt(it, NLINK, u, n[0]))

            ss, y, t_ = m["ss"][:, :], m["ny"][:, :], m["nt"][:, :]
            V.wait_ge(S["red_done"], cnt(it, QKC, u, QKC))
            link(V.tensor_scalar(ss, ss, 1e-24, None, ALU.max))
            link(V.tensor_scalar(t_.bitcast(I32), ss.bitcast(I32), 1, None, ALU.logical_shift_right))
            link(V.tensor_scalar(y.bitcast(I32), t_.bitcast(I32), -1.0, float(MAGIC), ALU.mult, ALU.add))
            for i in range(NEWTON):
                link(V.tensor_tensor(t_, y, y, ALU.mult))
                link(V.scalar_tensor_tensor(t_, t_, -0.5, ss, ALU.mult, ALU.mult))
                link(V.scalar_tensor_tensor(y, t_, 1.5, y, ALU.add, ALU.mult))
            wait(V, S["rot_done"], cnt(it, QKC, u - 1))
            link(V.tensor_copy(m["rn"][:, u % 2, :], y))


        def dve_softmax_in(it, u):
            for g in range(2):
                V.wait_ge(S["s_mm"], cnt(it, 2, u, g + 1))
                wait(V, S["sub_done"], cnt(it, 2, u - 1, g + 1))
                s = s_ps[g].rearrange("p (h k) -> p h k", k=2 * WIN)
                V.tensor_reduce(m["mx"][:, g, :], s, AX.X, ALU.max).then_inc(S["max_done"], 1)
                V.wait_ge(S["max_done"], cnt(it, 2, u, g + 1))
                wait(V, S["pT_mm"], cnt(it, 2, u))
                wait(V, S["den_sum"], cnt(it, 1, u - 1, 1))
                V.tensor_tensor(m["d"][:, :, g, :], s,
                                m["mx"][:, g, :].unsqueeze(2).to_broadcast([P, 8, 2 * WIN]),
                                ALU.subtract).then_inc(S["sub_done"], 1)

        def dve_den(it, u):
            V.wait_ge(S["exp_done"], cnt(it, 2, u, 2))
            V.tensor_reduce(m["den"][:, :, :], m["p"][:, :, :, :].rearrange("p h a k -> p a h k"), AX.X, ALU.add).then_inc(S["den_sum"], 1)
            V.wait_ge(S["den_sum"], cnt(it, 1, u, 1))
            wait(V, S["o_ev"], cnt(it, 2, u - 1))
            V.reciprocal(m["rden"][:, u % 2, :, :], m["den"][:, :, :]).then_inc(S["den_done"], 1)

        def dve_out(it, u):
            V.wait_ge(S["den_done"], cnt(it, 1, u, 1))
            for g in range(2):
                V.wait_ge(S["o_mm"], cnt(it, 2, u, g + 1))
                wait(V, S["oT_mm"], cnt(it, 2, u))
                V.tensor_tensor(m["o"][:, :, g, :], o_ps[g].rearrange("p (h e) -> p h e", e=DH),
                                m["rden"][:, u % 2, g, :].unsqueeze(2).to_broadcast([P, 8, DH]),
                                ALU.mult).then_inc(S["o_ev"], 1)

        def dve_wo(e):
            b = e % B
            V.wait_ge(S["d1_mm"], e + 1)
            V.tensor_tensor(xf[:, b, 1:1 + T], o_ps[0], xf[:, b, 1:1 + T], ALU.add).then_inc(S["d1_ev"], 1)
            V.wait_ge(S["d1_ev"], e + 1)
            wait(V, S["d2_mm"], e)
            V.tensor_scalar(m["xs"][0:64, :], xf[0:64, b, 1:1 + T], 1.0, None, ALU.mult)
            V.tensor_scalar(m["xs"][64:128, :], xf[64:128, b, 0:T], 1.0, None, ALU.mult).then_inc(S["mlp_xs"], 1)

        def dve_norm(e):
            V.wait_ge(S["std_done"], e + 1)
            V.wait_ge(S["vec_in"], (e + 1) * 16)
            V.reciprocal(ln_rstd[:, :], ln_std[:, :]).then_inc(S["rstd_done"], 1)
            V.wait_ge(S["rstd_done"], e + 1)
            wait(V, S["d4_mm"], 3 * e)
            V.scalar_tensor_tensor(m["xn"][:, :], ln_xc[:, :], m["vec"][:, 0:1], ln_rstd[:, :], ALU.mult, ALU.mult)\
                .then_inc(S["xn1"], 1)
            V.wait_ge(S["xn1"], e + 1)
            V.tensor_scalar(m["xn"][:, :], m["xn"][:, :], m["vec"][:, 1:2], None, ALU.add).then_inc(S["xn2"], 1)

        def dve_hidden(e, j):
            n = DT_TILES[j][1]
            V.wait_ge(S["gelu_done"], 3 * e + j + 1)
            wait(V, S["d5_mm"], e)
            V.scalar_tensor_tensor(m["h"][:n, j, :], o_ps[0][:n, :], m["vec"][:n, 2 + j:3 + j], m["gl"][:n, j % 2, :],
                                   ALU.add, ALU.mult).then_inc(S["hidden_done" if j == 2 else "h_done"], 1)

        def dve_down(e):
            b = e % B
            V.wait_ge(S["d5_mm"], e + 1)
            V.wait_ge(S["d1_ev"], e + 1)
            V.scalar_tensor_tensor(xf[:, b, 1:1 + T], o_ps[0], m["vec"][:, 8:9], xf[:, b, 1:1 + T], ALU.add, ALU.add)\
                .then_inc(S["stream"], 1)

        def dve_body(it, mlp, ahead, more):
            for u in range(TILES):
                if ahead or u + 3 < TILES:
                    dve_xs(it, u + 3)
                if u == 0 and more:
                    dve_weights(it)
                if u == 2 and ahead:
                    dve_tables(it + 1)
                if ahead or u + 2 < TILES:
                    dve_rotate(it, u + 2)
                if mlp and u == 2:
                    dve_hidden(it - 1, 0)
                if mlp and u == 3:
                    dve_down(it - 1)
                if ahead or u + 2 < TILES:
                    dve_rnorm(it, u + 2)
                if mlp and u == 0:
                    dve_wo(it - 1)
                if mlp and u == 2:
                    dve_hidden(it - 1, 1)
                    dve_hidden(it - 1, 2)
                if ahead or u + 1 < TILES:
                    dve_softmax_in(it, u + 1)
                dve_out(it, u)
                if ahead or u + 1 < TILES:
                    dve_den(it, u + 1)
                if mlp and u == 1:
                    dve_norm(it - 1)

        def dve_weights(it):
            k = it + B
            par, at = (k // 4) % 2, (k % 4) * WQ
            V.wait_ge(S["wstaged"], (k + 1) * 16)
            hi = m["wh"][:, par, bass.ds(at, WQ)]
            V.tensor_scalar(hi, m["wst"][:, 0, :], 1.0, None, ALU.mult).then_inc(S["whi_done"], 1)
            V.wait_ge(S["whi_done"], k + 1)
            V.tensor_tensor(m["wl"][:, par, bass.ds(at, WQ)], m["wst"][:, 0, :], hi.bitcast(F32), ALU.subtract)\
                .then_inc(S["wconv"], 1)

        def dve_ffn(first):
            last = first + PHASE - 1
            dve_tables(first)
            if first == 0:
                for k in range(-B, 0):
                    dve_weights(k)
            dve_xs(first, 0)
            dve_xs(first, 1)
            dve_rotate(first, 0)
            dve_rnorm(first, 0)
            dve_xs(first, 2)
            dve_rotate(first, 1)
            dve_rnorm(first, 1)
            dve_softmax_in(first, 0)
            dve_den(first, 0)
            dve_body(first, False, True, True)
            if first == 0:
                dve_body(1, True, True, True)
            with nc.vector.Fori(max(first + 1, 2), last) as it:
                dve_body(it, True, True, True)
            dve_body(last, True, False, first == 0)
            dve_wo(last)
            dve_norm(last)
            for j in range(3):
                dve_hidden(last, j)
            dve_down(last)

        G = nc.gpsimd

        def pool_rotate(it, u):
            qk = m["qk"][:, u % 2, :]
            wait(G, S["qkT_mm"], cnt(it, 4, u - 1))
            for c in range(QKC):
                G.wait_ge(S["m_done"], cnt(it, QKC, u, c + 1))
                G.tensor_tensor(qk[:, c * CH:(c + 1) * CH], m["ma"][:, c % 2, :], m["mb"][:, c % 2, :], ALU.add)\
                    .then_inc(S["add_done"], 1)
            G.wait_ge(S["newton"], cnt(it, NLINK, u, NLINK))
            for c in range(QKC):
                G.wait_ge(S["add_done"], cnt(it, QKC, u, c + 1))
                part = qk[:, c * CH:(c + 1) * CH].rearrange("p (h e) -> p h e", e=DH)
                G.tensor_tensor(part, part, m["rn"][:, u % 2, HC * c:HC * c + HC].unsqueeze(2)
                                .to_broadcast([P, HC, DH]), ALU.mult).then_inc(S["rot_done"], 1)

        def pool_ffn(first):
            last = first + PHASE - 1
            for u in range(2):
                pool_rotate(first, u)
            with nc.gpsimd.Fori(first, last) as it:
                for u in range(TILES):
                    pool_rotate(it, u + 2)
            for u in range(2):
                pool_rotate(last, u + 2)

        SP = nc.sync

        def sp_pairs(it, u):
            t = u % TILES
            SP.wait_ge(S["v_ev"], cnt(it, 2, u, 2))
            wait(SP, S["o_mm"], (it * TILES + (u - 1)) * 2)
            for par in range(2):
                for half in range(2):
                    for w in range(WPT):
                        slot, src_w = u % 2, w if half else w - 1
                        if src_w < 0:
                            slot, src_w = ((u - 1) % 2, WPT - 1) if t else (slot, 0)
                        at = 64 * par + 32 * half
                        SP.dma_start(m["vp"][at:at + WIN, u % 2, w, :],
                                     m["v"][WIN * src_w:WIN * src_w + WIN, slot, par, :])\
                            .then_inc(vp_sem[u % 2], 16)

        def sp_weights(k):
            wait(SP, S["wconv"], k)
            SP.dma_start(m["wst"][:, 0, :], a["Wqkv"][(k // 4) % DEPTH, :, bass.ds((k % 4) * WQ, WQ)])\
                .then_inc(S["wstaged"], 16)

        def sp_scales(e):
            wait(SP, S["rots_done"], e)
            SP.dma_start(m["qks"][:, :], a["qk_scale"][(e // B) % DEPTH, :, :].to_broadcast([P, 4 * DH]))\
                .then_inc(S["qks_in"], 16)

        def sp_wo(e):
            wait(SP, S["d1_mm"], e)
            SP.dma_start(m["wo"][:, :, :], a["Wo"][(e // B) % DEPTH, :, :].rearrange("(h p) n -> p h n", p=P))\
                .then_inc(S["wo_in"], 16)

        def sp_w1(e):
            wait(SP, S["d4_mm"], 3 * e)
            SP.dma_start(m["w1"][:, :], a["W1"][(e // B) % DEPTH, :, :]).then_inc(S["w1_in"], 16)

        def sp_w2(e):
            l = (e // B) % DEPTH
            wait(SP, S["d5_mm"], e)
            SP.dma_start(m["w2"][:, 0:2, :], a["W2"][l, 0:2 * P, :].rearrange("(j p) n -> p j n", p=P))\
                .then_inc(S["w2_in"], 16)
            SP.dma_start(m["w2"][0:DI - 2 * P, 2, :], a["W2"][l, 2 * P:DI, :]).then_inc(S["w2_in"], 16)
            SP.wait_ge(S["stream"], B + e)
            SP.dma_start(m["vec"][:, :], a["vectors"][l, :, :]).then_inc(S["vec_in"], 16)

        def sp_ffn(first):
            last = first + PHASE - 1
            sp_scales(first)
            if first == 0:
                for k in range(0, B + 1):
                    sp_weights(k)
            sp_wo(first)
            sp_w1(first)
            sp_w2(first)
            for u in range(2):
                sp_pairs(first, u)

            def body(it, mlp, ahead, more):
                for u in range(TILES):
                    if u == 0:
                        if ahead:
                            sp_scales(it + 1)
                        if more:
                            sp_weights(it + B + 1)
                    if ahead or u + 2 < TILES:
                        sp_pairs(it, u + 2)
                    if mlp and u == 1:
                        sp_wo(it)
                    if mlp and u == 3:
                        sp_w1(it)
                if mlp:
                    sp_w2(it)

            body(first, False, True, True)
            if first == 0:
                body(1, True, True, True)
            with nc.sync.Fori(max(first + 1, 2), last) as it:
                body(it, True, True, True)
            body(last, True, False, first == 0)

        def pe_ln(stage):
            for b in range(B):
                n = stage * B + b
                nc.tensor.wait_ge(x_ready, B * stage + B)
                wait(nc.tensor, lnx_ev, 2 * n)
                nc.tensor.matmul(o_ps[0], center[:, :], xm[:, b, :], start=True, stop=True).then_inc(lnc_mm, 1)
                nc.tensor.wait_ge(lnx_ev, 2 * n + 2)
                wait(nc.tensor, lnstd_done, n)
                nc.tensor.matmul(o_ps[1], mean[:, :], ln_sq[:, :], start=True, stop=True).then_inc(lnv_mm, 1)

        def act_ln(stage):
            for b in range(B):
                n = stage * B + b
                nc.scalar.wait_ge(lnc_mm, n + 1)
                wait(nc.scalar, ln_done[stage], b)
                nc.scalar.activation(ln_xc[:, :], o_ps[0], ACT.Copy).then_inc(lnx_ev, 1)
                wait(nc.scalar, lnv_mm, n)
                nc.scalar.activation(ln_sq[:, :], o_ps[0], ACT.Square).then_inc(lnx_ev, 1)
                nc.scalar.wait_ge(lnv_mm, n + 1)
                nc.scalar.activation(ln_std[:, :], o_ps[1], ACT.Sqrt, bias=eps_t[:, :]).then_inc(lnstd_done, 1)

        def dve_ln(stage):
            for b in range(B):
                n = stage * B + b
                V.wait_ge(lnstd_done, n + 1)
                V.reciprocal(ln_rstd[:, :], ln_std[:, :]).then_inc(ln_rs, 1)
                V.wait_ge(ln_rs, n + 1)
                V.tensor_tensor(xf[:, b, 1:1 + T], ln_xc[:, :], ln_rstd[:, :], ALU.mult).then_inc(ln_done[stage], 1)

        def dve_add(stage):
            V.wait_ge(S["stream"], B + PHASE * stage)
            for b in range(B):
                V.tensor_tensor(xm[:, b, :], xm[:, b, :], xf[:, b, 1:1 + T], ALU.add).then_inc(x_ready, 1)

        def sp_gla(sp):
            for dst, name in (("w", "gla_w"), ("b", "gla_b"), ("wo", "gla_wo"), ("bo", "gla_bo"), ("pick", "gla_pick")):
                sp.dma_start(gb[dst][:], a[name]).then_inc(gs["in"], 16)

        def pe_gla():
            nc.tensor.wait_ge(gs["in"], 5 * 16)
            nc.tensor.wait_ge(ln_done[0], B)
            banks = [proj_ps[0], proj_ps[1], tr_ps[0], tr_ps[1]]
            for j in range(4):
                for b in range(B):
                    last = nc.tensor.matmul(banks[j][GK * b:GK * b + GK, :], gb["w"][:, j, :], xf[:, b, 1:1 + T],
                                            start=True, stop=True)
                last.then_inc(gs["proj_mm"], 1)
            nc.tensor.wait_ge(gs["zero"], 1)
            nc.tensor.wait_ge(gs["proj_ev"], 4)
            nc.tensor.matmul(s_ps[0], gb["zero"][:, :], gb["v"][:, :], start=True, stop=False)

            def gather(v, r):
                nc.tensor.wait_ge(gs["sq"], v + 1)
                nc.tensor.matmul(s_ps[0], gb["gather"][:, r, :], gb["sq"][:, r, :], start=False, stop=False)\
                    .then_inc(gs["sum_mm"], 1)

            def spread(v, r, first=False):
                nc.tensor.wait_ge(gs["sel"], v + 1)
                if not first:
                    nc.tensor.wait_ge(gs["kv"], v - 1)
                nc.tensor.matmul(proj_ps[r], gb["spread"][:, r, :, :].rearrange("p b k -> p (b k)"), gb["v"][:, :],
                                 start=True, stop=True).then_inc(gs["vb_mm"], 1)

            spread(0, 0, True)
            spread(1, 1, True)
            with nc.tensor.Fori(0, GK // 2 - 1) as i:
                for r in range(2):
                    gather(2 * i + r, r)
                    spread(2 * i + (r + 2), r)
            for r in range(2):
                gather(GK - 2 + r, r)
            nc.tensor.matmul(s_ps[0], gb["zero"][:, :], gb["v"][:, :], start=False, stop=True).then_inc(gs["sum_mm"], 1)
            nc.tensor.wait_ge(gs["o_ev"], 1)
            for b in range(B):
                if b >= 2:
                    nc.tensor.wait_ge(x_ready, B + b - 1)
                nc.tensor.matmul(tr_ps[b % 2], gb["wo"][:, b, :], gb["o"][:, :], start=True, stop=True)\
                    .then_inc(gs["out_mm"], 1)

        def act_gla():
            nc.scalar.wait_ge(gs["in"], 5 * 16)
            banks = [proj_ps[0], proj_ps[1], tr_ps[0], tr_ps[1]]
            for j, (dst, func) in enumerate((("q", ACT.Identity), ("k", ACT.Sigmoid), ("g", ACT.Sigmoid),
                                             ("v", ACT.Identity))):
                nc.scalar.wait_ge(gs["proj_mm"], j + 1)
                nc.scalar.activation(gb[dst][:, :], banks[j], func, bias=gb["b"][:, j:j + 1]).then_inc(gs["proj_ev"], 1)

            def select(v, r, first=False):
                if not first:
                    nc.scalar.wait_ge(gs["sum_mm"], v - 1)
                nc.scalar.activation(gb["spread"][:, r, :, :],
                                     ident[:, :].rearrange("p (b v) -> p b v", v=GK)[:, :, bass.ds(v, 1)]
                                     .to_broadcast([P, B, GK]), ACT.Copy)
                nc.scalar.activation(gb["gather"][:, r, :], gb["pick"][:, bass.ds(4 * (GK - 1) - 4 * v, P)], ACT.Copy)\
                    .then_inc(gs["sel"], 1)

            nc.scalar.wait_ge(consts, 5 * 16)
            select(0, 0, True)
            select(1, 1, True)
            with nc.scalar.Fori(1, GK // 2) as i:
                for r in range(2):
                    select(2 * i + r, r)
            nc.scalar.wait_ge(gs["sum_mm"], GK + 1)
            nc.scalar.activation(gb["o"][:, :], s_ps[0], ACT.Copy).then_inc(gs["o_ev"], 1)

        def dve_gla():
            V.memset(gb["zero"][:, :], 0.0).then_inc(gs["zero"], 1)
            V.wait_ge(gs["proj_ev"], 4)

            def one(v, r, first=False):
                V.wait_ge(gs["vb_mm"], v + 1)
                if not first:
                    V.wait_ge(gs["st"], v - 1)
                V.tensor_tensor(gb["kv"][:, r, :], proj_ps[r], gb["k"][:, :], ALU.mult).then_inc(gs["kv"], 1)
                V.wait_ge(gs["kv"], v + 1)
                if not first:
                    V.wait_ge(gs["sq"], v - 1)
                V.tensor_tensor_scan(gb["st"][:, r, :], gb["g"][:, :], gb["kv"][:, r, :], 0.0, ALU.mult, ALU.add)\
                    .then_inc(gs["st"], 1)

            one(0, 0, True)
            one(1, 1, True)
            with nc.vector.Fori(1, GK // 2) as i:
                for r in range(2):
                    one(2 * i + r, r)
            for b in range(B):
                V.wait_ge(gs["out_mm"], b + 1)
                V.scalar_tensor_tensor(xm[:, b, :], tr_ps[b % 2], gb["bo"][:, :], xm[:, b, :], ALU.add, ALU.add)\
                    .then_inc(x_ready, 1)

        def pool_gla():
            G.wait_ge(gs["proj_ev"], 4)

            def one(v, r, first=False):
                G.wait_ge(gs["st"], v + 1)
                if not first:
                    G.wait_ge(gs["sum_mm"], v - 1)
                G.tensor_tensor(gb["sq"][:, r, :], gb["st"][:, r, :], gb["q"][:, :], ALU.mult).then_inc(gs["sq"], 1)

            one(0, 0, True)
            one(1, 1, True)
            with nc.gpsimd.Fori(1, GK // 2) as i:
                for r in range(2):
                    one(2 * i + r, r)

        MB_IN = (("win", "mb_in_w"), ("conv", "mb_conv"), ("cols", "mb_cols"), ("xw", "mb_x_w"), ("dtw", "mb_dt_w"),
                 ("alog", "mb_alog"), ("wout", "mb_out_w"), ("part", "mb_part"), ("bc", "mb_bc_pick"))

        def sp_mamba(sp):
            sp.wait_ge(x_ready, 3 * B)
            for dst, name in MB_IN:
                sp.dma_start(mb[dst][:], a[name]).then_inc(ms["in"], 16)

        def pe_mamba():
            T_ = nc.tensor
            T_.wait_ge(ms["in"], len(MB_IN) * 16)
            T_.wait_ge(ln_done[2], B)

            def batch(b, first):
                if not first:
                    T_.wait_ge(ms["bu"], 32 * b)
                    T_.wait_ge(ms["c_ev"], 16 * b)
                for j in range(4):
                    last = T_.matmul(psum[:, j, :], mb["win"][:, P * j:P * j + P], xf[:, b, 1:1 + T],
                                     start=True, stop=True)
                    last.then_inc(ms["in_mm"], 1)
                T_.wait_ge(ms["u_ev"], b + 1)
                for j in range(2):
                    last = T_.matmul(psum[0:3 * XPW, 6, :], mb["xw"][:, j, :], mb["u"][:, j, :],
                                     start=(j == 0), stop=(j == 1))
                last.then_inc(ms["xd_mm"], 1)
                T_.wait_ge(ms["xd_ev"], b + 1)
                T_.wait_ge(ms["x_ev"], b + 1)
                for j in range(2):
                    last = T_.matmul(psum[:, j, :], mb["dtw"][:, P * j:P * j + P], mb["xd"][0:RANK, :],
                                     start=True, stop=True)
                last.then_inc(ms["dt_mm"], 1)
                T_.wait_ge(ms["split"], 6 * b + 6)
                T_.wait_ge(ms["dt_ev"], b + 1)
                T_.wait_ge(ms["z_ev"], b + 1)

                def spread(n):
                    if n >= 2:
                        T_.wait_ge(ms["bu"], 32 * b + 2 * (n - 1))
                        T_.wait_ge(ms["c_ev"], 16 * b + (n - 1))
                    T_.matmul(psum[:, n % 2, :], mb["bc"][:, n, :], mb["parts"][:, :], start=True, stop=True)\
                        .then_inc(ms["b_mm"], 1)
                    T_.matmul(psum[:, 2 + n % 2, :], mb["bc"][:, NST + n, :], mb["parts"][:, :], start=True, stop=True)\
                        .then_inc(ms["c_mm"], 1)

                spread(0)
                for n in range(NST):
                    if n + 1 < NST:
                        spread(n + 1)
                    for j in range(2):
                        T_.wait_ge(ms["hc"], 32 * b + 2 * n + j + 1)
                        if n == 0 and not first:
                            T_.wait_ge(ms["yo"], 4 * b)
                        T_.matmul(psum[:, 4 + j, :], ident[:, :], mb["hc"][:, j, :], start=(n == 0), stop=(n == NST - 1))\
                            .then_inc(ms["y_mm"], 1)
                T_.wait_ge(ms["yo"], 4 * b + 4)
                if not first:
                    T_.wait_ge(x_ready, b + 3 * B)
                for j in range(2):
                    last = T_.matmul(psum[:, 7, :], mb["wout"][:, j, :], mb["yo"][:, j, :], start=(j == 0), stop=(j == 1))
                last.then_inc(ms["out_mm"], 1)

            batch(0, True)
            with T_.Fori(1, B) as b:
                batch(b, False)

        def act_mamba():
            A_ = nc.scalar
            A_.wait_ge(ms["in"], len(MB_IN) * 16)
            A_.activation(mb["a"][:, :, :], mb["alog"][:, :, :], ACT.Exp).then_inc(ms["a1"], 1)

            def batch(b, first):
                A_.wait_ge(ms["in_mm"], 4 * b + 2)
                if not first:
                    A_.wait_ge(ms["conv"], 8 * b)
                A_.activation(mb["xp"][:, :, SHIFT:], psum[:, 0:2, :], ACT.Copy).then_inc(ms["x_ev"], 1)
                A_.wait_ge(ms["in_mm"], 4 * b + 4)
                if not first:
                    A_.wait_ge(ms["yo"], 4 * b)
                A_.activation(mb["zs"][:, :, :], psum[:, 2:4, :], ACT.Silu).then_inc(ms["z_ev"], 1)
                A_.wait_ge(ms["conv"], 8 * b + 8)
                for j in range(2):
                    last = A_.activation(mb["u"][:, j, :], mb["cv"][:, j, :], ACT.Silu, bias=mb["cols"][:, j, 0:1])
                last.then_inc(ms["u_ev"], 1)
                A_.wait_ge(ms["xd_mm"], b + 1)
                if not first:
                    A_.wait_ge(ms["dt_mm"], b)
                    A_.wait_ge(ms["split"], 6 * b)
                A_.activation(mb["xd"][:, :], psum[0:3 * XPW, 6, :], ACT.Copy).then_inc(ms["xd_ev"], 1)
                A_.wait_ge(ms["dt_ev"], b + 1)
                A_.activation(mb["ab"][:, :, :], mb["y"][:, :, :], ACT.Abs).then_inc(ms["abs"], 1)
                A_.wait_ge(ms["abs"], b + 1)
                A_.activation(mb["e"][:, :, :], mb["ab"][:, :, :], ACT.Exp, scale=-1.0).then_inc(ms["exp"], 1)
                A_.wait_ge(ms["poly"], (len(LOG1P) + 2) * b + (len(LOG1P) + 2))
                A_.wait_ge(ms["a2"], 1)
                for n in range(NST):
                    for j in range(2):
                        if not (first and n == 0):
                            A_.wait_ge(ms["h"], 32 * b + 2 * n + j - 1)
                        A_.activation(mb["da"][:, j, :], mb["dl"][:, j, :], ACT.Exp, scale=mb["a"][:, j, n:n + 1])\
                            .then_inc(ms["da"], 1)
                    A_.wait_ge(ms["c_mm"], 16 * b + n + 1)
                    if not (first and n < 2):
                        A_.wait_ge(ms["hc"], 32 * b + 2 * (n - 1))
                    A_.activation(mb["c"][:, n % 2, :], psum[:, 2 + n % 2, :], ACT.Copy).then_inc(ms["c_ev"], 1)

            batch(0, True)
            with A_.Fori(1, B) as b:
                batch(b, False)

        def dve_mamba():
            V.wait_ge(ms["in"], len(MB_IN) * 16)
            V.memset(mb["xp"][:, :, 0:SHIFT], 0.0).then_inc(ms["zero"], 1)
            V.wait_ge(ms["a1"], 1)
            V.tensor_scalar(mb["a"][:, :, :], mb["a"][:, :, :], -1.0, None, ALU.mult).then_inc(ms["a2"], 1)
            V.wait_ge(ms["zero"], 1)
            NP_ = len(LOG1P) + 2

            def batch(b, first):
                V.wait_ge(ms["x_ev"], b + 1)
                if not first:
                    V.wait_ge(ms["u_ev"], b)
                for k in range(CONV):
                    for j in range(2):
                        src, tap = mb["xp"][:, j, k:k + T], mb["conv"][:, j, k:k + 1]
                        if k == 0:
                            V.tensor_scalar(mb["cv"][:, j, :], src, tap, None, ALU.mult).then_inc(ms["conv"], 1)
                        else:
                            V.wait_ge(ms["conv"], 8 * b + (2 * (k - 1) + j + 1))
                            V.scalar_tensor_tensor(mb["cv"][:, j, :], src, tap, mb["cv"][:, j, :], ALU.mult, ALU.add)\
                                .then_inc(ms["conv"], 1)
                V.wait_ge(ms["xd_ev"], b + 1)
                part = mb["part"]
                if not first:
                    V.wait_ge(ms["c_mm"], 16 * b)
                V.tensor_copy(mb["hi"][:, :], mb["xd"][:, :]).then_inc(ms["split"], 1)
                V.wait_ge(ms["split"], 6 * b + 1)
                V.tensor_tensor(mb["r1"][:, :], mb["xd"][:, :], mb["hi"][:, :], ALU.subtract).then_inc(ms["split"], 1)
                V.wait_ge(ms["split"], 6 * b + 2)
                V.tensor_copy(mb["mid"][:, :], mb["r1"][:, :]).then_inc(ms["split"], 1)
                V.tensor_scalar(mb["pa"][:, :], mb["hi"][:, :], part[:, 0:1], None, ALU.mult)
                V.wait_ge(ms["split"], 6 * b + 3)
                V.tensor_tensor(mb["r2"][:, :], mb["r1"][:, :], mb["mid"][:, :], ALU.subtract).then_inc(ms["split"], 1)
                V.wait_ge(ms["split"], 6 * b + 4)
                V.scalar_tensor_tensor(mb["pb"][:, :], mb["mid"][:, :], part[:, 1:2], mb["pa"][:, :], ALU.mult, ALU.add)\
                    .then_inc(ms["split"], 1)
                V.wait_ge(ms["split"], 6 * b + 5)
                V.scalar_tensor_tensor(mb["parts"][:, :], mb["r2"][:, :], part[:, 2:3], mb["pb"][:, :],
                                       ALU.mult, ALU.add).then_inc(ms["split"], 1)
                V.wait_ge(ms["dt_mm"], b + 1)
                for j in range(2):
                    bias = mb["cols"][:, j, 1:2]
                    last = V.tensor_scalar(mb["y"][:, j, :], psum[:, j, :], bias, bias, ALU.add, ALU.add)
                last.then_inc(ms["dt_ev"], 1)
                V.wait_ge(ms["exp"], b + 1)
                if not first:
                    V.wait_ge(ms["da"], 32 * b)
                e, pl = mb["e"][:, :, :], mb["pl"][:, :, :]
                V.tensor_scalar(pl, e, LOG1P[-1], None, ALU.mult).then_inc(ms["poly"], 1)
                for i, c in enumerate(LOG1P[-2::-1]):
                    V.wait_ge(ms["poly"], NP_ * b + (i + 1))
                    V.scalar_tensor_tensor(pl, pl, c, e, ALU.add, ALU.mult).then_inc(ms["poly"], 1)
                V.wait_ge(ms["poly"], NP_ * b + (NP_ - 2))
                V.scalar_tensor_tensor(mb["dl"][:, :, :], mb["y"][:, :, :], 0.0, pl, ALU.max, ALU.add)\
                    .then_inc(ms["poly"], 1)
                V.wait_ge(ms["poly"], NP_ * b + (NP_ - 1))
                V.tensor_tensor(mb["du"][:, :, :], mb["dl"][:, :, :], mb["u"][:, :, :], ALU.mult).then_inc(ms["poly"], 1)
                V.wait_ge(ms["poly"], NP_ * b + NP_)
                for n in range(NST):
                    V.wait_ge(ms["b_mm"], 16 * b + n + 1)
                    for j in range(2):
                        k = 2 * n + j
                        if not (first and n == 0):
                            V.wait_ge(ms["h"], 32 * b + k - 1)
                        V.tensor_tensor(mb["bu"][:, j, :], psum[:, n % 2, :], mb["du"][:, j, :], ALU.mult)\
                            .then_inc(ms["bu"], 1)
                    for j in range(2):
                        k = 2 * n + j
                        V.wait_ge(ms["bu"], 32 * b + k + 1)
                        V.wait_ge(ms["da"], 32 * b + k + 1)
                        if not (first and n == 0):
                            V.wait_ge(ms["hc"], 32 * b + k - 1)
                        V.tensor_tensor_scan(mb["h"][:, j, :], mb["da"][:, j, :], mb["bu"][:, j, :], 0.0,
                                             ALU.mult, ALU.add).then_inc(ms["h"], 1)
                V.wait_ge(ms["y_mm"], 32 * b + 32)
                if not first:
                    V.wait_ge(ms["out_mm"], b)
                for j in range(2):
                    V.scalar_tensor_tensor(mb["yo"][:, j, :], mb["u"][:, j, :], mb["cols"][:, j, 2:3],
                                           psum[:, 4 + j, :], ALU.mult, ALU.add).then_inc(ms["yo"], 1)
                V.wait_ge(ms["z_ev"], b + 1)
                for j in range(2):
                    V.wait_ge(ms["yo"], 4 * b + (j + 1))
                    V.tensor_tensor(mb["yo"][:, j, :], mb["yo"][:, j, :], mb["zs"][:, j, :], ALU.mult)\
                        .then_inc(ms["yo"], 1)
                V.wait_ge(ms["out_mm"], b + 1)
                V.tensor_tensor(xm[:, b, :], xm[:, b, :], psum[:, 7, :], ALU.add).then_inc(x_ready, 1)

            batch(0, True)
            with nc.vector.Fori(1, B) as b:
                batch(b, False)

        def pool_mamba():
            def batch(b, first):
                for n in range(NST):
                    G.wait_ge(ms["c_ev"], 16 * b + n + 1)
                    for j in range(2):
                        k = 2 * n + j
                        G.wait_ge(ms["h"], 32 * b + k + 1)
                        if not (first and n == 0):
                            G.wait_ge(ms["y_mm"], 32 * b + k - 1)
                        G.tensor_tensor(mb["hc"][:, j, :], mb["h"][:, j, :], mb["c"][:, n % 2, :], ALU.mult)\
                            .then_inc(ms["hc"], 1)

            batch(0, True)
            with nc.gpsimd.Fori(1, B) as b:
                batch(b, False)

        block = ctx.enter_context(nc.Block())
        xin = a["x"].rearrange("b (t p) c -> p (b t) c", p=P)
        xout = a["out"].rearrange("b (t p) c -> p (b t) c", p=P)
        xrows = m["qk"][:, :, :].rearrange("p u n -> p (u n)")[:, 0:2 * 1024].rearrange("p (n c) -> p n c", c=D)

        @block.sync
        def _(sp):
            sp.dma_start(xrows, xin).then_inc(x_in, 16)
            for dst, name in CONSTS:
                sp.dma_start(dst[:], a[name]).then_inc(consts, 16)
            sp_gla(sp)
            sp.wait_ge(x_ready, 2 * B)
            sp.dma_start(m["rot"][:], a["rot"]).then_inc(rot_in, 16)
            sp_ffn(0)
            sp_mamba(sp)
            sp.wait_ge(x_ready, 4 * B)
            sp.dma_start(m["rot"][:], a["rot"]).then_inc(rot_in, 16)
            sp_ffn(PHASE)
            sp.wait_ge(out_ev, 4)
            sp.dma_start(xout, xrows).then_inc(out_st, 16)
            sp.wait_ge(out_st, 16)

        @block.tensor
        def _(pe):
            pe.wait_ge(consts, 16 * len(CONSTS))
            pe.wait_ge(x_in, 16)
            for g in range(B):
                if g >= 2:
                    pe.wait_ge(x_ready, g - 1)
                for i in range(4):
                    last = nc.tensor.transpose(tr_ps[g % 2][:, i * P:(i + 1) * P], xrows[:, 4 * g + i, :], ident[:, :])
                last.then_inc(x_tr, 1)
            pe_ln(0)
            pe_gla()
            pe_ln(1)
            pe_ffn(0)
            pe_ln(2)
            pe_mamba()
            pe_ln(3)
            pe_ffn(PHASE)
            for g in range(B):
                pe.wait_ge(x_ready, 4 * B + g + 1)
                if g >= 2:
                    pe.wait_ge(out_ev, g - 1)
                for i in range(4):
                    last = nc.tensor.transpose(tr_ps[g % 2][:, i * P:(i + 1) * P], xm[:, g, i * P:(i + 1) * P], ident[:, :])
                last.then_inc(out_tr, 1)

        @block.scalar
        def _(act):
            act.wait_ge(zeroed, 2)
            act_ln(0)
            act_gla()
            act_ln(1)
            act_ffn(0)
            act_ln(2)
            act_mamba()
            act_ln(3)
            act_ffn(PHASE)
            for g in range(B):
                act.wait_ge(out_tr, g + 1)
                nc.scalar.activation(xrows[:, 4 * g:4 * g + 4, :], tr_ps[g % 2].rearrange("p (i c) -> p i c", i=4),
                                     ACT.Copy).then_inc(out_ev, 1)

        def dve_ffn_start(n, stage):
            V.memset(m["kt"][:, :, 0:WIN], 0.0).then_inc(zeroed, 1)
            V.wait_ge(rot_in, 16 * n)
            V.wait_ge(ln_done[stage], B)
            V.wait_ge(zeroed, 2 + n)

        @block.vector
        def _(dve):
            V.memset(xf[:, :, 0:1], 0.0).then_inc(zeroed, 1)
            V.memset(eps_t[:, :], EPS).then_inc(zeroed, 1)
            for g in range(B):
                V.wait_ge(x_tr, g + 1)
                V.tensor_copy(xm[:, g, :], tr_ps[g % 2]).then_inc(x_ready, 1)
            dve_ln(0)
            dve_gla()
            dve_ln(1)
            dve_ffn_start(1, 1)
            dve_ffn(0)
            dve_add(1)
            dve_ln(2)
            dve_mamba()
            dve_ln(3)
            dve_ffn_start(2, 3)
            dve_ffn(PHASE)
            dve_add(2)

        @block.gpsimd
        def _(pool):
            pool_gla()
            pool_ffn(0)
            pool_mamba()
            pool_ffn(PHASE)


def constants():
    half = np.arange(0, DH, 2, dtype=np.float32)
    inv_freq = (1.0 / np.power(np.float32(10000.0), half / np.float32(DH))).astype(np.float32)
    t = np.arange(T, dtype=np.float32)
    freqs = t[:, None] * inv_freq[None, :]
    base = (half + np.float32(0.4 * DH)) / np.float32(1.4 * DH)
    power = (t - T // 2) / np.float32(WIN // 2)
    scale = np.power(base[None, :], power[:, None]).astype(np.float32)
    cos, sin = np.cos(freqs), np.sin(freqs)
    inv = np.float32(1.0) / scale

    def two(x, y):
        return np.concatenate([x, y], -1)

    rot = np.concatenate([two(cos * scale, cos * scale), two(-sin * scale, sin * scale),
                          two(cos * inv, cos * inv), two(-sin * inv, sin * inv)], -1).astype(np.float32)
    rot = rot.reshape(TILES, P, 4 * DH).transpose(1, 0, 2)
    tau = np.arange(WIN)
    prev = np.where(tau[:, None] > tau[None, :], MASKED, 0.0)
    own = np.where(tau[:, None] < tau[None, :], MASKED, 0.0)
    maskrow = np.zeros((64, HC, 2 * WIN), np.float32)
    maskrow[:WIN] = np.concatenate([prev, own], 1)[:, None, :]
    maskrow[WIN, :, :WIN] = MASKED
    onehot = np.zeros((64, 2, P), np.float32)
    onehot[:WIN] = np.tile(np.eye(WIN), (1, WPT))[:, None, :]
    onehot[WIN, 1, :WIN] = 1.0
    bf = mybir.dt.np(BF16)
    pick = np.zeros((P, 4 * (2 * GK - 1)), np.float32)
    pick[np.arange(P), 4 * (GK - 1) + np.arange(P) // GK] = 1.0
    bc = np.zeros((3 * XPW, 2 * NST, P), np.float32)
    part = np.zeros((3 * XPW, 3), np.float32)
    for i in range(3):
        part[i * XPW:(i + 1) * XPW, i] = 1.0
        for n in range(2 * NST):
            bc[i * XPW + RANK + n, n, :] = 1.0
    return {"gla_pick": pick, "mb_part": part, "mb_bc_pick": bc.astype(bf), "rot": np.ascontiguousarray(rot), "maskrow": maskrow.reshape(64, CH).astype(bf),
            "onehot": onehot.astype(bf), "ident": np.eye(P, dtype=np.float32),
            "center": (np.eye(P) - 1.0 / P).astype(np.float32), "mean": np.full((P, P), 1.0 / P, np.float32)}


def layout(inputs):
    f = {k: np.asarray(v) for k, v in inputs.items()}
    r = {"x": f["L0_attn_a_hidden_state"], "Wqkv": f["L0_ffn_Wqkv"], "Wo": f["L0_ffn_Wo"], "W1": f["L0_ffn_W1"],
         "W2": f["L0_ffn_W2"]}
    qs, ks = f["L0_ffn_q_scale"], f["L0_ffn_k_scale"]
    swap = np.concatenate([np.arange(DH // 2, DH), np.arange(DH // 2)])
    r["qk_scale"] = np.concatenate([qs, qs[:, swap], ks, ks[:, swap]], -1)[:, None, :]
    vec = np.zeros((DEPTH, P, NVEC), np.float32)
    vec[:, :, 0] = f["L0_ffn_ln_g"]
    vec[:, :, 1] = f["L0_ffn_ln_b"]
    for j, (at, n) in enumerate(DT_TILES):
        vec[:, :n, 2 + j] = f["L0_ffn_b1"][:, at:at + n]
        vec[:, :n, 5 + j] = f["L0_ffn_b1"][:, DI + at:DI + at + n]
    vec[:, :, 8] = f["L0_ffn_b2"]
    r["vectors"] = vec

    def chan(x):
        return x.reshape(2, P, -1).transpose(1, 0, 2)

    g = {n: f["L0_attn_a_" + n] for n in ("Wq", "bq", "Wk", "bk", "Wv", "bv", "Wg", "bg", "Wo", "bo")}
    r["gla_w"] = np.stack([g["Wq"], g["Wk"], g["Wg"], g["Wv"]], 1)
    r["gla_b"] = np.tile(np.stack([g["bq"], g["bk"], g["bg"], g["bv"]], 1), (B, 1))
    wo = np.zeros((GK, B, B, D), np.float32)
    for b in range(B):
        wo[:, b, b, :] = g["Wo"]
    r["gla_wo"] = wo.reshape(P, B, D)
    r["gla_bo"] = g["bo"][:, None]
    h = {n: f["L0_attn_b_" + n] for n in ("in_proj_w", "conv_w", "conv_b", "x_proj_w", "dt_proj_w", "dt_proj_b",
                                          "A_log", "D_skip", "out_proj_w")}
    r["mb_in_w"] = h["in_proj_w"]
    r["mb_conv"] = chan(h["conv_w"])
    r["mb_cols"] = chan(np.stack([h["conv_b"], h["dt_proj_b"], h["D_skip"]], 1))
    r["mb_x_w"] = chan(np.concatenate([h["x_proj_w"]] * 3, 1))
    r["mb_dt_w"] = h["dt_proj_w"]
    r["mb_alog"] = chan(h["A_log"])
    r["mb_out_w"] = chan(h["out_proj_w"])
    return {k: np.ascontiguousarray(v) for k, v in (r | constants()).items()}


def kernel(**inputs):
    import numpy as np
    import concourse.bacc as bacc
    from concourse import mybir
    from concourse.bass_utils import run_bass_kernel_spmd

    arrays = {"in_" + name: value for name, value in layout(inputs).items()}
    nc = bacc.Bacc("TRN2", target_bir_lowering=False, num_devices=1)
    tensors = {name[3:]: nc.dram_tensor(name, value.shape, mybir.dt.from_np(value.dtype), kind="ExternalInput").ap()
               for name, value in arrays.items()}
    tensors["out"] = nc.dram_tensor("out_x", (B, T, D), F32, kind="ExternalOutput").ap()
    build(nc, tensors)
    result = run_bass_kernel_spmd(nc, [arrays], core_ids=[0])
    return result.results[0]["out_x"]
```

```python
import numpy as np
import concourse.bass as bass
from concourse import mybir
from contextlib import ExitStack

F32 = mybir.dt.float32
F32R = mybir.dt.float32r
BF16 = mybir.dt.bfloat16
I32 = mybir.dt.int32
ALU = mybir.AluOpType
ACT = mybir.ActivationFunctionType
AX = mybir.AxisListType

P = 128
B, T, D = 4, 512, 128
EPS = 1e-5
DEPTH, HEADS, DH, WIN = 6, 16, 64, 32
INNER = HEADS * DH
HP = HEADS // 2
QK_SCALE = 8.0
DI = int(D * 4 * 2 / 3)
DT_TILES = [(0, 128), (128, 128), (256, DI - 256)]
TILES = T // P
WPT = P // WIN
CH = 512
NCH = 3 * INNER // CH
HC = CH // DH
QKC = 2 * INNER // CH
WQ = 3 * INNER // 4
PHASE = DEPTH * B
NEWTON = 3
MAGIC = 0x5F3759DF
MASKED = -1e30
NVEC = 9
GK = 32
NST, DIN, RANK, CONV = 16, 256, 8, 4
XPW = RANK + 2 * NST
SHIFT = 2 * (CONV - 1)
LOG1P = [float(c) for c in np.polynomial.chebyshev.Chebyshev.interpolate(
    lambda e: np.log1p(e) / e, 11, domain=[0, 1]).convert(kind=np.polynomial.Polynomial).coef]


def cnt(it, per_unit, j, k=0):
    return it * (TILES * per_unit) + (per_unit * j + k)


def wait(eng, sem, value):
    if isinstance(value, int) and value <= 0:
        return
    eng.wait_ge(sem, value)


def build(nc, a):
    ctx = ExitStack()
    with ctx:
        def sb(name, shape, dt=F32):
            return ctx.enter_context(nc.sbuf_tensor(name, shape, dt))

        def sem(name):
            return ctx.enter_context(nc.semaphore(name))

        xm = sb("x_main", [P, B, T])
        xf = sb("x_ffn", [P, B, T + 1])
        ident = sb("ident", [P, P])
        center = sb("center", [P, P])
        mean = sb("mean", [P, P])
        onehot = sb("onehot", [64, 2, P], BF16)
        maskrow = sb("maskrow", [64, CH], BF16)
        eps_t = sb("eps_t", [P, 1])
        three_halves = sb("three_halves", [P, 2 * HEADS])
        CONSTS = ((ident, "ident"), (center, "center"), (mean, "mean"), (onehot, "onehot"), (maskrow, "maskrow"))
        ln_xc = sb("ln_xc", [P, T])
        hidden = sb("hidden", [P, 3, T])
        gelu = sb("gelu", [P, 2, T])
        mlp_xs = hidden[:, 0, :]
        ln_sq = hidden[:, 1, :]
        ln_std = gelu[:, 0, :]
        ln_rstd = gelu[:, 1, :]
        ln_diag = gelu[:, 1, :].rearrange("p (t q) -> p t q", t=TILES)
        ln_col_std = sb("ln_col_std", [P, TILES])
        ln_col_rstd = sb("ln_col_rstd", [P, TILES])

        psum = ctx.enter_context(nc.psum_tensor("psum", [P, 8, CH], F32))
        proj_ps = [psum[:, 0, :], psum[:, 1, :]]
        tr_ps = [psum[:, 2, :], psum[:, 3, :]]
        s_ps = [psum[:, 4, :], psum[:, 5, :]]
        o_ps = [psum[:, 6, :], psum[:, 7, :]]

        consts = sem("consts")
        rot_in = sem("rot_in")
        zeroed = sem("zeroed")
        x_in = sem("x_in")
        x_tr = sem("x_tr")
        x_ready = sem("x_ready")
        lnc_mm, lnx_ev, lnv_mm, lnstd_done, ln_rs = (
            sem(n) for n in ("lnc_mm", "lnx_ev", "lnv_mm", "lnstd_done", "ln_rs"))
        out_tr, out_ev, out_st = sem("out_tr"), sem("out_ev"), sem("out_st")
        added = sem("added")

        wqkv_hi = sb("wqkv_hi", [P, 2, 3 * INNER], F32R)
        wqkv_lo = sb("wqkv_lo", [P, 2, 3 * INNER], F32R)
        wqkv_staged = sb("wqkv_staged", [P, 1, WQ])
        fctx = ctx.enter_context(ExitStack())

        def fsb(name, shape, dt=F32):
            return fctx.enter_context(nc.sbuf_tensor(name, shape, dt))

        def ffn_buffers():
            m = {}
            m["wh"], m["wl"], m["wst"] = wqkv_hi, wqkv_lo, wqkv_staged
            m["wo"] = fsb("wo", [P, HP, D])
            m["w1"] = fsb("w1", [P, 2 * DI])
            m["w2"] = fsb("w2", [P, 3, D])
            m["vec"] = fsb("layer_vectors", [P, NVEC])
            m["rot"] = fsb("rot_base", [P, TILES, 4 * DH])
            m["rots"] = fsb("rot_scaled", [P, TILES, 4 * DH])
            m["qks"] = fsb("qk_scale", [P, 4 * DH])
            m["xh"] = fsb("xs_hi", [P, 2, P], F32R)
            m["xl"] = fsb("xs_lo", [P, 2, P], F32R)
            m["sq"] = fsb("squares", [P, 2, CH])
            m["ma"] = fsb("rot_cos", [P, 2, CH])
            m["mb"] = fsb("rot_sin", [P, 2, CH])
            m["qk"] = fsb("qk_rows", [P, 2, 2 * INNER])
            m["ss"] = fsb("sumsq", [P, 2 * HEADS])
            m["ny"] = fsb("newton_y", [P, 2 * HEADS])
            m["nt"] = fsb("newton_t", [P, 2 * HEADS])
            m["hs"] = fsb("minus_half_sumsq", [P, 2 * HEADS])
            m["rn"] = fsb("rnorm", [P, 2, 2 * HEADS])
            m["v"] = fsb("v_rows", [P, 2, 2, HP * DH])
            m["vp"] = fsb("v_pairs", [P, 2, WPT, HP * DH])
            m["qt"] = fsb("q_t", [P, HP, P])
            m["kt"] = fsb("k_t", [P, HP, WIN + T])
            m["mx"] = fsb("row_max", [P, 2, HP])
            m["p"] = fsb("probs", [P, HP, 2, 2 * WIN])
            m["d"] = m["p"]
            m["pt"] = fsb("probs_t", [P, HP, P])
            m["den"] = fsb("den", [P, 2, HP])
            m["rden"] = fsb("rden", [P, 2, 2, HP])
            m["o"] = fsb("o_rows", [P, HP, 2, DH])
            m["ot"] = fsb("o_t", [P, HP, T])
            m["xn"] = fsb("xn_mlp", [P, T])
            m["gl"], m["h"], m["xs"] = gelu, hidden, mlp_xs
            return m

        m = ffn_buffers()
        fctx.close()

        def gla_buffers():
            gb = {}
            gb["w"] = fsb("gla_w", [P, 4, GK])
            gb["b"] = fsb("gla_b", [P, 4])
            gb["wo"] = fsb("gla_wo", [P, B, D])
            gb["bo"] = fsb("gla_bo", [P, 1])
            gb["pick"] = fsb("gla_pick", [P, 4 * (2 * GK - 1)])
            gb["q"] = fsb("gla_q", [P, T])
            gb["k"] = fsb("gla_k", [P, T])
            gb["g"] = fsb("gla_g", [P, T])
            gb["v"] = fsb("gla_v", [P, T])
            gb["zero"] = fsb("gla_zero", [P, P])
            gb["spread"] = fsb("gla_spread", [P, 2, B, GK])
            gb["gather"] = fsb("gla_gather", [P, 2, P])
            gb["kv"] = fsb("gla_kv", [P, 2, T])
            gb["st"] = fsb("gla_state", [P, 2, T])
            gb["sq"] = fsb("gla_state_q", [P, 2, T])
            gb["o"] = fsb("gla_out", [P, T])
            return gb

        gb = gla_buffers()
        fctx.close()

        def mamba_buffers():
            mb = {}
            mb["win"] = fsb("mb_in_w", [P, 2 * DIN])
            mb["conv"] = fsb("mb_conv", [P, 2, CONV])
            mb["cols"] = fsb("mb_cols", [P, 2, 3])
            mb["xw"] = fsb("mb_x_w", [P, 2, 3 * XPW])
            mb["dtw"] = fsb("mb_dt_w", [RANK, DIN])
            mb["alog"] = fsb("mb_alog", [P, 2, NST])
            mb["a"] = fsb("mb_a", [P, 2, NST])
            mb["wout"] = fsb("mb_out_w", [P, 2, D])
            mb["part"] = fsb("mb_part", [3 * XPW, 3])
            mb["bc"] = fsb("mb_bc_pick", [3 * XPW, 2 * NST, P], BF16)
            mb["xp"] = fsb("mb_x", [P, 2, SHIFT + T])
            mb["zs"] = fsb("mb_z", [P, 2, T])
            mb["cv"] = fsb("mb_conv_out", [P, 2, T])
            mb["u"] = fsb("mb_u", [P, 2, T])
            mb["xd"] = fsb("mb_xdbl", [3 * XPW, T])
            mb["hi"] = fsb("mb_hi", [3 * XPW, T], BF16)
            mb["mid"] = fsb("mb_mid", [3 * XPW, T], BF16)
            mb["r1"] = fsb("mb_rest", [3 * XPW, T])
            mb["r2"] = fsb("mb_rest2", [3 * XPW, T])
            mb["pa"] = fsb("mb_parts_a", [3 * XPW, T])
            mb["pb"] = fsb("mb_parts_b", [3 * XPW, T])
            mb["parts"] = fsb("mb_parts", [3 * XPW, T], BF16)
            mb["y"] = fsb("mb_dt", [P, 2, T])
            mb["ab"] = fsb("mb_dt_abs", [P, 2, T])
            mb["e"] = fsb("mb_dt_exp", [P, 2, T])
            mb["pl"] = fsb("mb_poly", [P, 2, T])
            mb["dl"] = fsb("mb_delta", [P, 2, T])
            mb["du"] = fsb("mb_du", [P, 2, T])
            mb["da"] = fsb("mb_decay", [P, 2, T])
            mb["bu"] = fsb("mb_bu", [P, 2, T])
            mb["h"] = fsb("mb_h", [P, 2, T])
            mb["c"] = fsb("mb_c", [P, 2, T])
            mb["hc"] = fsb("mb_hc", [P, 2, T])
            mb["yo"] = fsb("mb_y", [P, 2, T])
            return mb

        mb = mamba_buffers()
        gs = {n: sem("g_" + n) for n in (
            "in", "zero", "proj_mm", "proj_ev", "sel", "vb_mm", "kv", "st", "sq", "sum_mm", "o_ev", "out_mm")}
        ms = {n: sem("m_" + n) for n in (
            "in", "zero", "a1", "a2", "in_mm", "x_ev", "z_ev", "conv", "u_ev", "xd_mm", "xd_ev", "split", "dt_mm",
            "dt_ev", "abs", "exp", "poly", "du", "da", "b_mm", "c_mm", "bu", "h", "c_ev", "hc", "y_mm", "yo",
            "out_mm", "added")}
        S = {n: sem(n) for n in (
            "xs_hi", "xs_lo", "wstaged", "whi_done", "wconv", "qkv_mm", "sq_done", "m_done", "red_done",
            "seed", "newton", "add_done", "rot_done", "v_ev", "vp0", "vp1", "oT_mm", "oT_ev", "qkT_mm",
            "qkT_ev", "s_mm", "max_done", "sub_done", "exp_done", "den_sum", "den_done", "pT_mm", "pT_ev",
            "o_mm", "o_ev", "wo_in", "w1_in", "w2_in", "vec_in", "qks_in", "rots_done", "d1_mm", "d1_ev",
            "mlp_xs", "d2_mm", "xc_ev", "d3_mm", "std_done", "rstd_done", "diag_done", "d6_mm", "xn1", "xn2", "d4_mm",
            "gelu_done", "h_done", "hidden_done", "d5_mm", "stream")}
        ln_done = [sem("ln0_done"), S["stream"], sem("ln2_done"), sem("ln3_done")]
        vp_sem = [S["vp0"], S["vp1"]]

        def pe_proj(it, u, c):
            layer = (it + u // TILES) // B
            if c == 0:
                nc.tensor.wait_ge(S["xs_lo"], cnt(it, 1, u, 1))
                nc.tensor.wait_ge(S["wconv"], layer * B + B)
            if c < 2:
                wait(nc.tensor, S["v_ev"], cnt(it, 2, u, c - 1))
            else:
                wait(nc.tensor, S["sq_done"], cnt(it, QKC, u, c - 1))
                wait(nc.tensor, S["m_done"], cnt(it, QKC, u, c - 1))
            cols = slice(c * CH, (c + 1) * CH)
            xh, xl = m["xh"][:, u % 2, :], m["xl"][:, u % 2, :]
            wh, wl = m["wh"][:, layer % 2, cols], m["wl"][:, layer % 2, cols]
            nc.tensor.matmul(proj_ps[c % 2], xh, wh, start=True, stop=False)
            nc.tensor.matmul(proj_ps[c % 2], xh, wl, start=False, stop=False)
            nc.tensor.matmul(proj_ps[c % 2], xl, wh, start=False, stop=True).then_inc(S["qkv_mm"], 1)

        def pe_out_t(it, u, qk_after):
            for g in range(2):
                nc.tensor.wait_ge(S["o_ev"], cnt(it, 2, u, 2))
                if qk_after:
                    nc.tensor.wait_ge(S["qkT_ev"], cnt(it, 4, u + 2, g + 3))
                else:
                    nc.tensor.wait_ge(S["pT_ev"], cnt(it, 2, u, g + 1))
                for i in range(4):
                    hp = 4 * g + i
                    last = nc.tensor.transpose(tr_ps[g][:, i * P:(i + 1) * P],
                                               m["o"][:, hp, :, :].rearrange("p a e -> p (a e)"),
                                               ident[:, :])
                last.then_inc(S["oT_mm"], 1)

        def pe_qk_t(it, u, after, groups):
            for g in groups:
                nc.tensor.wait_ge(S["rot_done"], cnt(it, QKC, u, g + 1))
                if g >= 2:
                    nc.tensor.wait_ge(S["qkT_ev"], cnt(it, 4, u, g - 1))
                elif after:
                    nc.tensor.wait_ge(S["pT_ev"], cnt(it, 2, u - 2, g + 1))
                for i in range(4):
                    last = nc.tensor.transpose(tr_ps[g % 2][:, i * P:(i + 1) * P],
                                               m["qk"][:, u % 2, (4 * g + i) * P:(4 * g + i + 1) * P],
                                               ident[:, :])
                last.then_inc(S["qkT_mm"], 1)

        def pe_probs_t(it, u, qk_after, out_before):
            for g in range(2):
                nc.tensor.wait_ge(S["exp_done"], cnt(it, 2, u, 2))
                if out_before:
                    nc.tensor.wait_ge(S["oT_ev"], cnt(it, 2, u - 1, g + 1))
                elif qk_after:
                    nc.tensor.wait_ge(S["qkT_ev"], cnt(it, 4, u + 1, g + 3))
                for i in range(4):
                    hp = 4 * g + i
                    last = nc.tensor.transpose(tr_ps[g][:, i * P:(i + 1) * P],
                                               m["p"][:, hp, :, :].rearrange("p a k -> p (a k)"),
                                               ident[:, :])
                last.then_inc(S["pT_mm"], 1)

        def pe_scores(it, u, half):
            t = u % TILES
            if half == 0:
                nc.tensor.wait_ge(S["qkT_ev"], cnt(it, 4, u, 4))
                for g in range(2):
                    wait(nc.tensor, S["sub_done"], cnt(it, 2, u - 1, g + 1))
                    nc.tensor.matmul(s_ps[g], onehot[:, 1 if t == 0 else 0, :], maskrow[:, :], start=True, stop=False,
                                     skip_group_check=True)
            for hp in range(4 * half, 4 * half + 4):
                for par in range(2):
                    rows = slice(64 * par, 64 * par + 64)
                    for w in range(WPT):
                        last = nc.tensor.matmul(
                            s_ps[par][WIN * w:WIN * w + WIN, 64 * hp:64 * hp + 64],
                            m["qt"][rows, hp, WIN * w:WIN * w + WIN],
                            m["kt"][rows, hp, t * P + WIN * w:t * P + WIN * w + 2 * WIN],
                            start=False, stop=True, skip_group_check=True)
                    if hp == HP - 1:
                        last.then_inc(S["s_mm"], 1)

        def pe_pv(it, u, half):
            for hp in range(4 * half, 4 * half + 4):
                for par in range(2):
                    rows = slice(64 * par, 64 * par + 64)
                    for w in range(WPT):
                        last = nc.tensor.matmul(
                            o_ps[par][WIN * w:WIN * w + WIN, 64 * hp:64 * hp + 64],
                            m["pt"][rows, hp, WIN * w:WIN * w + WIN],
                            m["vp"][rows, u % 2, w, DH * hp:DH * hp + DH],
                            start=True, stop=True)
                    if hp == HP - 1:
                        last.then_inc(S["o_mm"], 1)

        def pe_pv_ready(it, u, mlp):
            nc.tensor.wait_ge(vp_sem[u % 2], it * 512 + 256 * (u // 2 + 1))
            nc.tensor.wait_ge(S["pT_ev"], cnt(it, 2, u, 2))
            wait(nc.tensor, S["o_ev"], cnt(it, 2, u))
            if mlp:
                pe_pv_banks(it - 1, u)

        def pe_wo(e, half):
            if half == 0:
                nc.tensor.wait_ge(S["wo_in"], (e + 1) * 16)
                nc.tensor.wait_ge(S["oT_ev"], (e + 1) * 8)
                nc.tensor.wait_ge(S["o_ev"], (e + 1) * 8 - 1)
            for hp in range(4 * half, 4 * half + 4):
                last = nc.tensor.matmul(o_ps[0], m["wo"][:, hp, :], m["ot"][:, hp, :],
                                        start=(hp == 0), stop=(hp == HP - 1))
            if half == 1:
                last.then_inc(S["d1_mm"], 1)

        def pe_center(e, o_free):
            wait(nc.tensor, S["o_ev"], o_free)
            nc.tensor.wait_ge(S["mlp_xs"], e + 1)
            nc.tensor.matmul(o_ps[0], center[:, :], m["xs"][:, :], start=True, stop=True).then_inc(S["d2_mm"], 1)

        def pe_var(e, o_free):
            wait(nc.tensor, S["o_ev"], o_free)
            nc.tensor.wait_ge(S["xc_ev"], 2 * (e + 1))
            for t in range(TILES):
                last = nc.tensor.matmul(o_ps[1][:, t:t + 1], ln_sq[:, t * P:(t + 1) * P], mean[:, 0:1],
                                        start=True, stop=True)
            last.then_inc(S["d3_mm"], 1)

        def pe_rstd(e, o_free):
            wait(nc.tensor, S["o_ev"], o_free)
            nc.tensor.wait_ge(S["diag_done"], e + 1)
            nc.tensor.matmul(o_ps[1], mean[:, :], ln_rstd[:, :], start=True, stop=True).then_inc(S["d6_mm"], 1)

        def pe_up(e, j, o_free):
            if j < 2:
                wait(nc.tensor, S["o_ev"], o_free)
            if j == 0:
                nc.tensor.wait_ge(S["w1_in"], (e + 1) * 16)
                nc.tensor.wait_ge(S["xn2"], e + 1)
            if j > 0:
                nc.tensor.wait_ge(S["h_done"], 2 * e + j)
                nc.tensor.wait_ge(S["gelu_done"], 3 * e + j)
            at, n = DT_TILES[j]
            nc.tensor.matmul(o_ps[1][:n, :], m["w1"][:, DI + at:DI + at + n], m["xn"][:, :], start=True, stop=True)
            nc.tensor.matmul(o_ps[0][:n, :], m["w1"][:, at:at + n], m["xn"][:, :],
                             start=True, stop=True).then_inc(S["d4_mm"], 1)

        def pe_down(e, o_free):
            wait(nc.tensor, S["o_ev"], o_free)
            nc.tensor.wait_ge(S["w2_in"], (e + 1) * 32)
            nc.tensor.wait_ge(S["hidden_done"], e + 1)
            for j, (_, n) in enumerate(DT_TILES):
                last = nc.tensor.matmul(o_ps[0], m["w2"][:n, j, :], m["h"][:n, j, :], start=(j == 0), stop=(j == 2))
            last.then_inc(S["d5_mm"], 1)

        def pe_pv_banks(e, u):
            if u == 0:
                nc.tensor.wait_ge(S["d1_ev"], e + 1)
            elif u == 1:
                nc.tensor.wait_ge(S["xc_ev"], 2 * (e + 1))
                nc.tensor.wait_ge(S["std_done"], e + 1)
            elif u == 2:
                nc.tensor.wait_ge(S["h_done"], 2 * e + 1)
            else:
                nc.tensor.wait_ge(S["stream"], B + e + 1)

        def pe_body(it, mlp, ahead):
            for u in range(TILES):
                o_free = cnt(it, 2, u)
                proj, nxt, prev = ahead or u + 2 < TILES, ahead or u + 1 < TILES, mlp or u > 0
                if proj:
                    pe_proj(it, u + 2, 1)
                if nxt:
                    pe_qk_t(it, u + 1, prev, (0, 1))
                if mlp and u == 1:
                    pe_center(it - 1, o_free)
                if mlp and u == 3:
                    pe_up(it - 1, 1, o_free)
                if nxt:
                    pe_qk_t(it, u + 1, prev, (2, 3))
                if mlp and u == 2:
                    pe_rstd(it - 1, o_free)
                if proj:
                    pe_proj(it, u + 2, 2)
                if prev:
                    pe_out_t(it, u - 1, nxt)
                if mlp and u == 3:
                    pe_up(it - 1, 2, o_free)
                if proj:
                    pe_proj(it, u + 2, 3)
                if mlp and u == 0:
                    pe_wo(it - 1, 0)
                if mlp and u == 1:
                    pe_var(it - 1, o_free)
                if mlp and u == 2:
                    pe_up(it - 1, 0, o_free)
                pe_probs_t(it, u, nxt, prev)
                if nxt:
                    pe_scores(it, u + 1, 0)
                if proj:
                    pe_proj(it, u + 2, 4)
                if mlp and u == 0:
                    pe_wo(it - 1, 1)
                if mlp and u == 3:
                    pe_down(it - 1, o_free)
                if nxt:
                    pe_scores(it, u + 1, 1)
                pe_pv_ready(it, u, mlp)
                if proj:
                    pe_proj(it, u + 2, 5)
                pe_pv(it, u, 0)
                if ahead or u + 3 < TILES:
                    pe_proj(it, u + 3, 0)
                pe_pv(it, u, 1)

        def pe_ffn(first):
            last = first + PHASE - 1
            for u in range(2):
                for c in range(NCH):
                    pe_proj(first, u, c)
            pe_qk_t(first, 0, False, range(4))
            pe_scores(first, 0, 0)
            pe_scores(first, 0, 1)
            pe_proj(first, 2, 0)
            pe_body(first, False, True)
            if first == 0:
                pe_body(1, True, True)
            with nc.tensor.Fori(max(first + 1, 2), last) as it:
                pe_body(it, True, True)
            pe_body(last, True, False)
            pe_out_t(last, 3, False)
            pe_wo(last, 0)
            pe_wo(last, 1)
            pe_center(last, 0)
            pe_var(last, 0)
            nc.tensor.wait_ge(S["std_done"], last + 1)
            pe_rstd(last, 0)
            for j in range(3):
                pe_up(last, j, 0)
            pe_down(last, 0)

        def act_square(it, u, c):
            nc.scalar.wait_ge(S["qkv_mm"], cnt(it, NCH, u, c + 1))
            wait(nc.scalar, S["red_done"], cnt(it, QKC, u, c - 1))
            nc.scalar.activation(m["sq"][:, c % 2, :], proj_ps[c % 2], ACT.Square).then_inc(S["sq_done"], 1)

        def act_v(it, u, c):
            nc.scalar.wait_ge(S["qkv_mm"], cnt(it, NCH, u, QKC + c + 1))
            if c == 0:
                wait(nc.scalar, vp_sem[u % 2], it * 512 + 256 * (u // 2))
                wait(nc.scalar, vp_sem[(u + 1) % 2], it * 512 + 256 * ((u - 1) // 2 + 1))
            nc.scalar.activation(
                m["v"][:, u % 2, :, 256 * c:256 * c + 256].rearrange("p a (i e) -> p i a e", e=DH),
                proj_ps[c % 2].rearrange("p (i a e) -> p i a e", a=2, e=DH), ACT.Copy).then_inc(S["v_ev"], 1)

        def act_out_t(it, u):
            t = u % TILES
            for g in range(2):
                nc.scalar.wait_ge(S["oT_mm"], cnt(it, 2, u, g + 1))
                if t == 0:
                    wait(nc.scalar, S["d1_mm"], it + u // TILES)
                nc.scalar.activation(m["ot"][:, 4 * g:4 * g + 4, t * P:(t + 1) * P],
                                     tr_ps[g].rearrange("p (i q) -> p i q", i=4), ACT.Copy).then_inc(S["oT_ev"], 1)

        def act_qk_t(it, u, groups):
            t = u % TILES
            wait(nc.scalar, S["s_mm"], cnt(it, 2, u))
            for g in groups:
                nc.scalar.wait_ge(S["qkT_mm"], cnt(it, 4, u, g + 1))
                hp = 4 * (g % 2)
                out = (m["qt"][:, hp:hp + 4, :] if g < 2
                       else m["kt"][:, hp:hp + 4, WIN + t * P:WIN + (t + 1) * P])
                nc.scalar.activation(out, tr_ps[g % 2].rearrange("p (i q) -> p i q", i=4), ACT.Copy)\
                    .then_inc(S["qkT_ev"], 1)

        def act_probs_t(it, u):
            for g in range(2):
                nc.scalar.wait_ge(S["pT_mm"], cnt(it, 2, u, g + 1))
                wait(nc.scalar, S["o_mm"], cnt(it, 2, u - 1, g + 1))
                nc.scalar.activation(m["pt"][:, 4 * g:4 * g + 4, :], tr_ps[g].rearrange("p (i q) -> p i q", i=4),
                                     ACT.Copy).then_inc(S["pT_ev"], 1)

        def act_exp(it, u):
            for g in range(2):
                nc.scalar.wait_ge(S["sub_done"], cnt(it, 2, u, g + 1))
                nc.scalar.activation(m["p"][:, :, g, :], m["d"][:, :, g, :], ACT.Exp,
                                     scale=QK_SCALE).then_inc(S["exp_done"], 1)

        def act_center(e):
            nc.scalar.wait_ge(S["d2_mm"], e + 1)
            wait(nc.scalar, S["xn1"], e)
            nc.scalar.activation(ln_xc[:, :], o_ps[0], ACT.Copy).then_inc(S["xc_ev"], 1)
            wait(nc.scalar, S["d3_mm"], e)
            nc.scalar.activation(ln_sq[:, :], o_ps[0], ACT.Square).then_inc(S["xc_ev"], 1)

        def act_std(e):
            nc.scalar.wait_ge(S["d3_mm"], e + 1)
            wait(nc.scalar, S["rstd_done"], e)
            nc.scalar.activation(ln_col_std[:, :], o_ps[1][:, 0:TILES], ACT.Sqrt, bias=eps_t[:, :])\
                .then_inc(S["std_done"], 1)

        def act_gelu(e, j):
            n = DT_TILES[j][1]
            nc.scalar.wait_ge(S["d4_mm"], 3 * e + j + 1)
            if j == 0:
                nc.scalar.wait_ge(S["vec_in"], (e + 1) * 16)
            if j == 0:
                wait(nc.scalar, S["hidden_done"], e)
            if j == 2:
                nc.scalar.wait_ge(S["h_done"], 2 * e + 1)
            nc.scalar.activation(m["gl"][:n, j % 2, :], o_ps[1][:n, :], ACT.Gelu,
                                 bias=m["vec"][:n, 5 + j:6 + j]).then_inc(S["gelu_done"], 1)

        def act_body(it, mlp, ahead):
            for u in range(TILES):
                proj, nxt, prev = ahead or u + 2 < TILES, ahead or u + 1 < TILES, mlp or u > 0
                if proj:
                    act_square(it, u + 2, 0)
                    act_square(it, u + 2, 1)
                if nxt:
                    act_qk_t(it, u + 1, (0, 1))
                if mlp and u == 3:
                    act_gelu(it - 1, 1)
                if nxt:
                    act_qk_t(it, u + 1, (2, 3))
                if mlp and u == 1:
                    act_center(it - 1)
                if proj:
                    act_square(it, u + 2, 2)
                if prev:
                    act_out_t(it, u - 1)
                if proj:
                    act_square(it, u + 2, 3)
                if mlp and u == 1:
                    act_std(it - 1)
                if mlp and u == 2:
                    act_gelu(it - 1, 0)
                if mlp and u == 3:
                    act_gelu(it - 1, 2)
                act_probs_t(it, u)
                if proj:
                    act_v(it, u + 2, 0)
                if proj:
                    act_v(it, u + 2, 1)
                if nxt:
                    act_exp(it, u + 1)

        def act_ffn(first):
            last = first + PHASE - 1
            for u in range(2):
                for c in range(QKC):
                    act_square(first, u, c)
                for c in range(2):
                    act_v(first, u, c)
            act_qk_t(first, 0, range(4))
            act_exp(first, 0)
            act_body(first, False, True)
            if first == 0:
                act_body(1, True, True)
            with nc.scalar.Fori(max(first + 1, 2), last) as it:
                act_body(it, True, True)
            act_body(last, True, False)
            act_out_t(last, 3)
            act_center(last)
            act_std(last)
            for j in range(3):
                act_gelu(last, j)

        V = nc.vector

        def dve_xs(it, u):
            t, b = u % TILES, (it + u // TILES) % B
            wait(V, S["qkv_mm"], cnt(it, NCH, u - 1))
            V.wait_ge(S["stream"], it + u // TILES + 1)
            halves = [(slice(0, 64), xf[0:64, b, 1 + t * P:1 + (t + 1) * P]),
                      (slice(64, 128), xf[64:128, b, t * P:(t + 1) * P])]
            for rows, src in halves:
                V.tensor_scalar(m["xh"][rows, u % 2, :], src, 1.0, None, ALU.mult).then_inc(S["xs_hi"], 1)
            V.wait_ge(S["xs_hi"], cnt(it, 2, u, 2))
            for rows, src in halves:
                last_ = V.tensor_tensor(m["xl"][rows, u % 2, :], src, m["xh"][rows, u % 2, :].bitcast(F32), ALU.subtract)
            last_.then_inc(S["xs_lo"], 1)

        def dve_tables(e, half):
            V.wait_ge(S["qks_in"], (e + 1) * 16)
            tiles = slice(2 * half, 2 * half + 2)
            wait(V, S["m_done"], (e - 1) * (TILES * QKC) + (2 * half + 2) * QKC)
            V.tensor_tensor(m["rots"][:, tiles, :], m["rot"][:, tiles, :],
                            m["qks"][:, :].unsqueeze(1).to_broadcast([P, 2, 4 * DH]), ALU.mult)\
                .then_inc(S["rots_done"], 1)

        def dve_rotate(it, u, chunks):
            t = u % TILES
            if t % 2 == 0 and chunks[0] == 0:
                V.wait_ge(S["rots_done"], 2 * it + (2 * (u // TILES) + t // 2 + 1))
            for c in chunks:
                o = 2 * DH * (c // 2)
                ps = proj_ps[c % 2].rearrange("p (h e) -> p h e", e=DH)
                ma = m["ma"][:, c % 2, :].rearrange("p (h e) -> p h e", e=DH)
                mb = m["mb"][:, c % 2, :].rearrange("p (h e) -> p h e", e=DH)
                cos = m["rots"][:, t, o:o + DH].unsqueeze(1).to_broadcast([P, HC, DH])
                sin = m["rots"][:, t, o + DH:o + 2 * DH].unsqueeze(1).to_broadcast([P, HC, DH])
                V.wait_ge(S["sq_done"], cnt(it, QKC, u, c + 1))
                wait(V, S["add_done"], cnt(it, QKC, u, c - 1))
                V.tensor_tensor(ma, ps, cos, ALU.mult)
                V.tensor_tensor(mb[:, :, 0:32], ps[:, :, 32:64], sin[:, :, 0:32], ALU.mult)
                V.tensor_tensor(mb[:, :, 32:64], ps[:, :, 0:32], sin[:, :, 32:64], ALU.mult).then_inc(S["m_done"], 1)
                V.tensor_reduce(m["ss"][:, HC * c:HC * c + HC],
                                m["sq"][:, c % 2, :].rearrange("p (h e) -> p h e", e=DH), AX.X, ALU.add)\
                    .then_inc(S["red_done"], 1)

        SEED, STEPS = 7, 4 * (NEWTON - 1)

        def dve_rnorm(it, u):
            n = [0]

            def link(ins):
                n[0] += 1
                ins.then_inc(S["seed"], 1)
                V.wait_ge(S["seed"], cnt(it, SEED, u, n[0]))

            ss, y, t_ = m["ss"][:, :], m["ny"][:, :], m["nt"][:, :]
            V.wait_ge(S["red_done"], cnt(it, QKC, u, QKC))
            wait(V, S["newton"], cnt(it, STEPS, u))
            link(V.tensor_scalar(ss, ss, 1e-24, None, ALU.max))
            link(V.tensor_scalar(t_.bitcast(I32), ss.bitcast(I32), 1, None, ALU.logical_shift_right))
            link(V.tensor_scalar(m["hs"][:, :], ss, -0.5, None, ALU.mult))
            link(V.tensor_scalar(y.bitcast(I32), t_.bitcast(I32), -1.0, float(MAGIC), ALU.mult, ALU.add))
            link(V.tensor_tensor(t_, y, y, ALU.mult))
            link(V.tensor_tensor(t_, t_, m["hs"][:, :], ALU.mult))
            V.scalar_tensor_tensor(y, t_, 1.5, y, ALU.add, ALU.mult).then_inc(S["seed"], 1)

        def dve_softmax_in(it, u):
            for g in range(2):
                V.wait_ge(S["s_mm"], cnt(it, 2, u, g + 1))
                wait(V, S["sub_done"], cnt(it, 2, u - 1, g + 1))
                s = s_ps[g].rearrange("p (h k) -> p h k", k=2 * WIN)
                V.tensor_reduce(m["mx"][:, g, :], s, AX.X, ALU.max).then_inc(S["max_done"], 1)
                V.wait_ge(S["max_done"], cnt(it, 2, u, g + 1))
                wait(V, S["pT_mm"], cnt(it, 2, u))
                wait(V, S["den_sum"], cnt(it, 1, u - 1, 1))
                V.tensor_tensor(m["d"][:, :, g, :], s,
                                m["mx"][:, g, :].unsqueeze(2).to_broadcast([P, 8, 2 * WIN]),
                                ALU.subtract).then_inc(S["sub_done"], 1)

        def dve_den(it, u):
            V.wait_ge(S["exp_done"], cnt(it, 2, u, 2))
            V.tensor_reduce(m["den"][:, :, :], m["p"][:, :, :, :].rearrange("p h a k -> p a h k"), AX.X, ALU.add).then_inc(S["den_sum"], 1)
            V.wait_ge(S["den_sum"], cnt(it, 1, u, 1))
            wait(V, S["o_ev"], cnt(it, 2, u - 1))
            V.reciprocal(m["rden"][:, u % 2, :, :], m["den"][:, :, :]).then_inc(S["den_done"], 1)

        def dve_out(it, u):
            V.wait_ge(S["den_done"], cnt(it, 1, u, 1))
            for g in range(2):
                V.wait_ge(S["o_mm"], cnt(it, 2, u, g + 1))
                wait(V, S["oT_mm"], cnt(it, 2, u))
                V.tensor_tensor(m["o"][:, :, g, :], o_ps[g].rearrange("p (h e) -> p h e", e=DH),
                                m["rden"][:, u % 2, g, :].unsqueeze(2).to_broadcast([P, 8, DH]),
                                ALU.mult).then_inc(S["o_ev"], 1)

        def dve_wo(e):
            b = e % B
            V.wait_ge(S["d1_mm"], e + 1)
            V.tensor_tensor(xf[:, b, 1:1 + T], o_ps[0], xf[:, b, 1:1 + T], ALU.add).then_inc(S["d1_ev"], 1)
            V.wait_ge(S["d1_ev"], e + 1)
            wait(V, S["d2_mm"], e)
            V.tensor_scalar(m["xs"][0:64, :], xf[0:64, b, 1:1 + T], 1.0, None, ALU.mult)
            V.tensor_scalar(m["xs"][64:128, :], xf[64:128, b, 0:T], 1.0, None, ALU.mult).then_inc(S["mlp_xs"], 1)

        def dve_rstd(e):
            V.wait_ge(S["std_done"], e + 1)
            wait(V, S["diag_done"], e)
            V.reciprocal(ln_col_rstd[:, :], ln_col_std[:, :]).then_inc(S["rstd_done"], 1)
            V.wait_ge(S["rstd_done"], e + 1)
            wait(V, S["hidden_done"], e)
            V.scalar_tensor_tensor(ln_diag, ident[:, :].unsqueeze(1).to_broadcast([P, TILES, P]), float(P),
                                   ln_col_rstd[:, :].unsqueeze(2).to_broadcast([P, TILES, P]), ALU.mult, ALU.mult)\
                .then_inc(S["diag_done"], 1)

        def dve_norm(e):
            V.wait_ge(S["vec_in"], (e + 1) * 16)
            V.wait_ge(S["d6_mm"], e + 1)
            wait(V, S["d4_mm"], 3 * e)
            V.scalar_tensor_tensor(m["xn"][:, :], ln_xc[:, :], m["vec"][:, 0:1], o_ps[1], ALU.mult, ALU.mult)\
                .then_inc(S["xn1"], 1)
            V.wait_ge(S["xn1"], e + 1)
            V.tensor_scalar(m["xn"][:, :], m["xn"][:, :], m["vec"][:, 1:2], None, ALU.add).then_inc(S["xn2"], 1)

        def dve_hidden(e, j):
            n = DT_TILES[j][1]
            V.wait_ge(S["gelu_done"], 3 * e + j + 1)
            wait(V, S["d5_mm"], e)
            V.scalar_tensor_tensor(m["h"][:n, j, :], o_ps[0][:n, :], m["vec"][:n, 2 + j:3 + j], m["gl"][:n, j % 2, :],
                                   ALU.add, ALU.mult).then_inc(S["hidden_done" if j == 2 else "h_done"], 1)

        def dve_down(e):
            b = e % B
            V.wait_ge(S["d5_mm"], e + 1)
            V.wait_ge(S["d1_ev"], e + 1)
            V.scalar_tensor_tensor(xf[:, b, 1:1 + T], o_ps[0], m["vec"][:, 8:9], xf[:, b, 1:1 + T], ALU.add, ALU.add)\
                .then_inc(S["stream"], 1)

        def dve_body(it, mlp, ahead, more):
            for u in range(TILES):
                proj, nxt = ahead or u + 2 < TILES, ahead or u + 1 < TILES
                if proj:
                    dve_rotate(it, u + 2, (0, 1))
                if mlp and u == 3:
                    dve_hidden(it - 1, 1)
                if mlp and u == 2:
                    dve_norm(it - 1)
                if ahead or u + 3 < TILES:
                    dve_xs(it, u + 3)
                if proj:
                    dve_rotate(it, u + 2, (2,))
                if mlp and u == 3:
                    dve_hidden(it - 1, 2)
                if proj:
                    dve_rotate(it, u + 2, (3,))
                if mlp and u == 2:
                    dve_hidden(it - 1, 0)
                if proj:
                    dve_rnorm(it, u + 2)
                if mlp and u == 3:
                    dve_down(it - 1)
                if u == 0 and more:
                    dve_weights(it)
                if u == 0 and ahead:
                    dve_tables(it + 1, 0)
                if mlp and u == 0:
                    dve_wo(it - 1)
                if u == 3 and ahead:
                    dve_tables(it + 1, 1)
                if nxt:
                    dve_softmax_in(it, u + 1)
                if mlp and u == 1:
                    dve_rstd(it - 1)
                if nxt:
                    dve_den(it, u + 1)
                dve_out(it, u)

        def dve_weights(it):
            k = it + B
            par, at = (k // 4) % 2, (k % 4) * WQ
            V.wait_ge(S["wstaged"], (k + 1) * 16)
            hi = m["wh"][:, par, bass.ds(at, WQ)]
            V.tensor_scalar(hi, m["wst"][:, 0, :], 1.0, None, ALU.mult).then_inc(S["whi_done"], 1)
            V.wait_ge(S["whi_done"], k + 1)
            V.tensor_tensor(m["wl"][:, par, bass.ds(at, WQ)], m["wst"][:, 0, :], hi.bitcast(F32), ALU.subtract)\
                .then_inc(S["wconv"], 1)

        def dve_ffn(first):
            last = first + PHASE - 1
            dve_tables(first, 0)
            dve_tables(first, 1)
            if first == 0:
                for k in range(-B, 0):
                    dve_weights(k)
            dve_xs(first, 0)
            dve_xs(first, 1)
            dve_rotate(first, 0, range(QKC))
            dve_rnorm(first, 0)
            dve_xs(first, 2)
            dve_rotate(first, 1, range(QKC))
            dve_rnorm(first, 1)
            dve_softmax_in(first, 0)
            dve_den(first, 0)
            dve_body(first, False, True, True)
            if first == 0:
                dve_body(1, True, True, True)
            with nc.vector.Fori(max(first + 1, 2), last) as it:
                dve_body(it, True, True, True)
            dve_body(last, True, False, first == 0)
            dve_wo(last)
            dve_rstd(last)
            dve_norm(last)
            for j in range(3):
                dve_hidden(last, j)
            dve_down(last)

        G = nc.gpsimd

        def pool_newton(it, u):
            n = [0]

            def link(out, in0, in1, op):
                n[0] += 1
                G.tensor_tensor(out, in0, in1, op).then_inc(S["newton"], 1)
                G.wait_ge(S["newton"], cnt(it, STEPS, u, n[0]))

            y, t_ = m["ny"][:, :], m["nt"][:, :]
            G.wait_ge(S["seed"], cnt(it, SEED, u, SEED))
            wait(G, S["rot_done"], cnt(it, QKC, u - 1))
            for i in range(NEWTON - 1):
                link(t_, y, y, ALU.mult)
                link(t_, t_, m["hs"][:, :], ALU.mult)
                link(t_, t_, three_halves[:, :], ALU.add)
                link(m["rn"][:, u % 2, :] if i == NEWTON - 2 else y, y, t_, ALU.mult)

        def pool_rotate(it, u):
            qk = m["qk"][:, u % 2, :]
            wait(G, S["qkT_mm"], cnt(it, 4, u - 1))
            for c in range(QKC):
                G.wait_ge(S["m_done"], cnt(it, QKC, u, c + 1))
                G.tensor_tensor(qk[:, c * CH:(c + 1) * CH], m["ma"][:, c % 2, :], m["mb"][:, c % 2, :], ALU.add)\
                    .then_inc(S["add_done"], 1)
            pool_newton(it, u)
            for c in range(QKC):
                G.wait_ge(S["add_done"], cnt(it, QKC, u, c + 1))
                part = qk[:, c * CH:(c + 1) * CH].rearrange("p (h e) -> p h e", e=DH)
                G.tensor_tensor(part, part, m["rn"][:, u % 2, HC * c:HC * c + HC].unsqueeze(2)
                                .to_broadcast([P, HC, DH]), ALU.mult).then_inc(S["rot_done"], 1)

        def pool_ffn(first):
            last = first + PHASE - 1
            G.wait_ge(zeroed, 3)
            for u in range(2):
                pool_rotate(first, u)
            with nc.gpsimd.Fori(first, last) as it:
                for u in range(TILES):
                    pool_rotate(it, u + 2)
            for u in range(2):
                pool_rotate(last, u + 2)

        SP = nc.sync

        def sp_pairs(it, u):
            t = u % TILES
            SP.wait_ge(S["v_ev"], cnt(it, 2, u, 2))
            wait(SP, S["o_mm"], (it * TILES + (u - 1)) * 2)
            for par in range(2):
                for half in range(2):
                    for w in range(WPT):
                        slot, src_w = u % 2, w if half else w - 1
                        if src_w < 0:
                            slot, src_w = ((u - 1) % 2, WPT - 1) if t else (slot, 0)
                        at = 64 * par + 32 * half
                        SP.dma_start(m["vp"][at:at + WIN, u % 2, w, :],
                                     m["v"][WIN * src_w:WIN * src_w + WIN, slot, par, :])\
                            .then_inc(vp_sem[u % 2], 16)

        def sp_weights(k):
            wait(SP, S["wconv"], k)
            SP.dma_start(m["wst"][:, 0, :], a["Wqkv"][(k // 4) % DEPTH, :, bass.ds((k % 4) * WQ, WQ)])\
                .then_inc(S["wstaged"], 16)

        def sp_scales(e):
            wait(SP, S["rots_done"], 2 * e)
            SP.dma_start(m["qks"][:, :], a["qk_scale"][(e // B) % DEPTH, :, :].to_broadcast([P, 4 * DH]))\
                .then_inc(S["qks_in"], 16)

        def sp_wo(e):
            wait(SP, S["d1_mm"], e)
            SP.dma_start(m["wo"][:, :, :], a["Wo"][(e // B) % DEPTH, :, :].rearrange("(h p) n -> p h n", p=P))\
                .then_inc(S["wo_in"], 16)

        def sp_w1(e):
            wait(SP, S["d4_mm"], 3 * e)
            SP.dma_start(m["w1"][:, :], a["W1"][(e // B) % DEPTH, :, :]).then_inc(S["w1_in"], 16)

        def sp_w2(e):
            l = (e // B) % DEPTH
            wait(SP, S["d5_mm"], e)
            SP.dma_start(m["w2"][:, 0:2, :], a["W2"][l, 0:2 * P, :].rearrange("(j p) n -> p j n", p=P))\
                .then_inc(S["w2_in"], 16)
            SP.dma_start(m["w2"][0:DI - 2 * P, 2, :], a["W2"][l, 2 * P:DI, :]).then_inc(S["w2_in"], 16)
            SP.wait_ge(S["stream"], B + e)
            SP.dma_start(m["vec"][:, :], a["vectors"][l, :, :]).then_inc(S["vec_in"], 16)

        def sp_ffn(first):
            last = first + PHASE - 1
            sp_scales(first)
            if first == 0:
                for k in range(0, B + 1):
                    sp_weights(k)
            sp_wo(first)
            sp_w1(first)
            sp_w2(first)
            for u in range(2):
                sp_pairs(first, u)

            def body(it, mlp, ahead, more):
                for u in range(TILES):
                    if u == 0:
                        if ahead:
                            sp_scales(it + 1)
                        if more:
                            sp_weights(it + B + 1)
                    if ahead or u + 2 < TILES:
                        sp_pairs(it, u + 2)
                    if mlp and u == 1:
                        sp_wo(it)
                    if mlp and u == 3:
                        sp_w1(it)
                if mlp:
                    sp_w2(it)

            body(first, False, True, True)
            if first == 0:
                body(1, True, True, True)
            with nc.sync.Fori(max(first + 1, 2), last) as it:
                body(it, True, True, True)
            body(last, True, False, first == 0)

        def pe_ln(stage):
            for b in range(B):
                n = stage * B + b
                nc.tensor.wait_ge(x_ready, B * stage + B)
                wait(nc.tensor, lnx_ev, 2 * n)
                nc.tensor.matmul(o_ps[0], center[:, :], xm[:, b, :], start=True, stop=True).then_inc(lnc_mm, 1)
                nc.tensor.wait_ge(lnx_ev, 2 * n + 2)
                wait(nc.tensor, lnstd_done, n)
                nc.tensor.matmul(o_ps[1], mean[:, :], ln_sq[:, :], start=True, stop=True).then_inc(lnv_mm, 1)

        def act_ln(stage):
            for b in range(B):
                n = stage * B + b
                nc.scalar.wait_ge(lnc_mm, n + 1)
                wait(nc.scalar, ln_done[stage], b)
                nc.scalar.activation(ln_xc[:, :], o_ps[0], ACT.Copy).then_inc(lnx_ev, 1)
                wait(nc.scalar, lnv_mm, n)
                nc.scalar.activation(ln_sq[:, :], o_ps[0], ACT.Square).then_inc(lnx_ev, 1)
                nc.scalar.wait_ge(lnv_mm, n + 1)
                nc.scalar.activation(ln_std[:, :], o_ps[1], ACT.Sqrt, bias=eps_t[:, :]).then_inc(lnstd_done, 1)

        def dve_ln(stage):
            for b in range(B):
                n = stage * B + b
                V.wait_ge(lnstd_done, n + 1)
                V.reciprocal(ln_rstd[:, :], ln_std[:, :]).then_inc(ln_rs, 1)
                V.wait_ge(ln_rs, n + 1)
                V.tensor_tensor(xf[:, b, 1:1 + T], ln_xc[:, :], ln_rstd[:, :], ALU.mult).then_inc(ln_done[stage], 1)

        def dve_add(stage):
            V.wait_ge(S["stream"], B + PHASE * stage)
            for b in range(B):
                V.tensor_tensor(xm[:, b, :], xm[:, b, :], xf[:, b, 1:1 + T], ALU.add).then_inc(x_ready, 1)

        def sp_gla(sp):
            for dst, name in (("w", "gla_w"), ("b", "gla_b"), ("wo", "gla_wo"), ("bo", "gla_bo"), ("pick", "gla_pick")):
                sp.dma_start(gb[dst][:], a[name]).then_inc(gs["in"], 16)

        def pe_gla():
            nc.tensor.wait_ge(gs["in"], 5 * 16)
            nc.tensor.wait_ge(ln_done[0], B)
            banks = [proj_ps[0], proj_ps[1], tr_ps[0], tr_ps[1]]
            for j in range(4):
                for b in range(B):
                    last = nc.tensor.matmul(banks[j][GK * b:GK * b + GK, :], gb["w"][:, j, :], xf[:, b, 1:1 + T],
                                            start=True, stop=True)
                last.then_inc(gs["proj_mm"], 1)
            nc.tensor.wait_ge(gs["zero"], 1)
            nc.tensor.wait_ge(gs["proj_ev"], 4)
            nc.tensor.matmul(s_ps[0], gb["zero"][:, :], gb["v"][:, :], start=True, stop=False)

            def gather(v, r):
                nc.tensor.wait_ge(gs["sq"], v + 1)
                nc.tensor.matmul(s_ps[0], gb["gather"][:, r, :], gb["sq"][:, r, :], start=False, stop=False)\
                    .then_inc(gs["sum_mm"], 1)

            def spread(v, r, first=False):
                nc.tensor.wait_ge(gs["sel"], v + 1)
                if not first:
                    nc.tensor.wait_ge(gs["kv"], v - 1)
                nc.tensor.matmul(proj_ps[r], gb["spread"][:, r, :, :].rearrange("p b k -> p (b k)"), gb["v"][:, :],
                                 start=True, stop=True).then_inc(gs["vb_mm"], 1)

            spread(0, 0, True)
            spread(1, 1, True)
            with nc.tensor.Fori(0, GK // 2 - 1) as i:
                for r in range(2):
                    gather(2 * i + r, r)
                    spread(2 * i + (r + 2), r)
            for r in range(2):
                gather(GK - 2 + r, r)
            nc.tensor.matmul(s_ps[0], gb["zero"][:, :], gb["v"][:, :], start=False, stop=True).then_inc(gs["sum_mm"], 1)
            nc.tensor.wait_ge(gs["o_ev"], 1)
            for b in range(B):
                if b >= 2:
                    nc.tensor.wait_ge(x_ready, B + b - 1)
                nc.tensor.matmul(tr_ps[b % 2], gb["wo"][:, b, :], gb["o"][:, :], start=True, stop=True)\
                    .then_inc(gs["out_mm"], 1)

        def act_gla():
            nc.scalar.wait_ge(gs["in"], 5 * 16)
            banks = [proj_ps[0], proj_ps[1], tr_ps[0], tr_ps[1]]
            for j, (dst, func) in enumerate((("q", ACT.Identity), ("k", ACT.Sigmoid), ("g", ACT.Sigmoid),
                                             ("v", ACT.Identity))):
                nc.scalar.wait_ge(gs["proj_mm"], j + 1)
                nc.scalar.activation(gb[dst][:, :], banks[j], func, bias=gb["b"][:, j:j + 1]).then_inc(gs["proj_ev"], 1)

            def select(v, r, first=False):
                if not first:
                    nc.scalar.wait_ge(gs["sum_mm"], v - 1)
                nc.scalar.activation(gb["spread"][:, r, :, :],
                                     ident[:, :].rearrange("p (b v) -> p b v", v=GK)[:, :, bass.ds(v, 1)]
                                     .to_broadcast([P, B, GK]), ACT.Copy)
                nc.scalar.activation(gb["gather"][:, r, :], gb["pick"][:, bass.ds(4 * (GK - 1) - 4 * v, P)], ACT.Copy)\
                    .then_inc(gs["sel"], 1)

            nc.scalar.wait_ge(consts, 5 * 16)
            select(0, 0, True)
            select(1, 1, True)
            with nc.scalar.Fori(1, GK // 2) as i:
                for r in range(2):
                    select(2 * i + r, r)
            nc.scalar.wait_ge(gs["sum_mm"], GK + 1)
            nc.scalar.activation(gb["o"][:, :], s_ps[0], ACT.Copy).then_inc(gs["o_ev"], 1)

        def dve_gla():
            V.memset(gb["zero"][:, :], 0.0).then_inc(gs["zero"], 1)
            V.wait_ge(gs["proj_ev"], 4)

            def one(v, r, first=False):
                V.wait_ge(gs["vb_mm"], v + 1)
                if not first:
                    V.wait_ge(gs["st"], v - 1)
                V.tensor_tensor(gb["kv"][:, r, :], proj_ps[r], gb["k"][:, :], ALU.mult).then_inc(gs["kv"], 1)
                V.wait_ge(gs["kv"], v + 1)
                if not first:
                    V.wait_ge(gs["sq"], v - 1)
                V.tensor_tensor_scan(gb["st"][:, r, :], gb["g"][:, :], gb["kv"][:, r, :], 0.0, ALU.mult, ALU.add)\
                    .then_inc(gs["st"], 1)

            one(0, 0, True)
            one(1, 1, True)
            with nc.vector.Fori(1, GK // 2) as i:
                for r in range(2):
                    one(2 * i + r, r)
            for b in range(B):
                V.wait_ge(gs["out_mm"], b + 1)
                V.scalar_tensor_tensor(xm[:, b, :], tr_ps[b % 2], gb["bo"][:, :], xm[:, b, :], ALU.add, ALU.add)\
                    .then_inc(x_ready, 1)

        def pool_gla():
            G.wait_ge(gs["proj_ev"], 4)

            def one(v, r, first=False):
                G.wait_ge(gs["st"], v + 1)
                if not first:
                    G.wait_ge(gs["sum_mm"], v - 1)
                G.tensor_tensor(gb["sq"][:, r, :], gb["st"][:, r, :], gb["q"][:, :], ALU.mult).then_inc(gs["sq"], 1)

            one(0, 0, True)
            one(1, 1, True)
            with nc.gpsimd.Fori(1, GK // 2) as i:
                for r in range(2):
                    one(2 * i + r, r)

        MB_IN = (("win", "mb_in_w"), ("conv", "mb_conv"), ("cols", "mb_cols"), ("xw", "mb_x_w"), ("dtw", "mb_dt_w"),
                 ("alog", "mb_alog"), ("wout", "mb_out_w"), ("part", "mb_part"), ("bc", "mb_bc_pick"))

        def sp_mamba(sp):
            sp.wait_ge(x_ready, 3 * B)
            for dst, name in MB_IN:
                sp.dma_start(mb[dst][:], a[name]).then_inc(ms["in"], 16)

        def pe_mamba():
            T_ = nc.tensor
            T_.wait_ge(ms["in"], len(MB_IN) * 16)
            T_.wait_ge(ln_done[2], B)

            def batch(b, first):
                if not first:
                    T_.wait_ge(ms["bu"], 32 * b)
                    T_.wait_ge(ms["c_ev"], 16 * b)
                for j in range(4):
                    last = T_.matmul(psum[:, j, :], mb["win"][:, P * j:P * j + P], xf[:, b, 1:1 + T],
                                     start=True, stop=True)
                    last.then_inc(ms["in_mm"], 1)
                T_.wait_ge(ms["u_ev"], b + 1)
                for j in range(2):
                    last = T_.matmul(psum[0:3 * XPW, 6, :], mb["xw"][:, j, :], mb["u"][:, j, :],
                                     start=(j == 0), stop=(j == 1))
                last.then_inc(ms["xd_mm"], 1)
                T_.wait_ge(ms["xd_ev"], b + 1)
                T_.wait_ge(ms["x_ev"], b + 1)
                for j in range(2):
                    last = T_.matmul(psum[:, j, :], mb["dtw"][:, P * j:P * j + P], mb["xd"][0:RANK, :],
                                     start=True, stop=True)
                last.then_inc(ms["dt_mm"], 1)
                T_.wait_ge(ms["split"], 6 * b + 6)
                T_.wait_ge(ms["dt_ev"], b + 1)
                T_.wait_ge(ms["z_ev"], b + 1)

                def spread(n):
                    if n >= 2:
                        T_.wait_ge(ms["bu"], 32 * b + 2 * (n - 1))
                        T_.wait_ge(ms["c_ev"], 16 * b + (n - 1))
                    T_.matmul(psum[:, n % 2, :], mb["bc"][:, n, :], mb["parts"][:, :], start=True, stop=True)\
                        .then_inc(ms["b_mm"], 1)
                    T_.matmul(psum[:, 2 + n % 2, :], mb["bc"][:, NST + n, :], mb["parts"][:, :], start=True, stop=True)\
                        .then_inc(ms["c_mm"], 1)

                spread(0)
                for n in range(NST):
                    if n + 1 < NST:
                        spread(n + 1)
                    for j in range(2):
                        T_.wait_ge(ms["hc"], 32 * b + 2 * n + j + 1)
                        if n == 0 and not first:
                            T_.wait_ge(ms["yo"], 4 * b)
                        T_.matmul(psum[:, 4 + j, :], ident[:, :], mb["hc"][:, j, :], start=(n == 0), stop=(n == NST - 1))\
                            .then_inc(ms["y_mm"], 1)
                T_.wait_ge(ms["yo"], 4 * b + 4)
                if not first:
                    T_.wait_ge(x_ready, b + 3 * B)
                for j in range(2):
                    last = T_.matmul(psum[:, 7, :], mb["wout"][:, j, :], mb["yo"][:, j, :], start=(j == 0), stop=(j == 1))
                last.then_inc(ms["out_mm"], 1)

            batch(0, True)
            with T_.Fori(1, B) as b:
                batch(b, False)

        def act_mamba():
            A_ = nc.scalar
            A_.wait_ge(ms["in"], len(MB_IN) * 16)
            A_.activation(mb["a"][:, :, :], mb["alog"][:, :, :], ACT.Exp).then_inc(ms["a1"], 1)

            def batch(b, first):
                A_.wait_ge(ms["in_mm"], 4 * b + 2)
                if not first:
                    A_.wait_ge(ms["conv"], 8 * b)
                A_.activation(mb["xp"][:, :, SHIFT:], psum[:, 0:2, :], ACT.Copy).then_inc(ms["x_ev"], 1)
                A_.wait_ge(ms["in_mm"], 4 * b + 4)
                if not first:
                    A_.wait_ge(ms["yo"], 4 * b)
                A_.activation(mb["zs"][:, :, :], psum[:, 2:4, :], ACT.Silu).then_inc(ms["z_ev"], 1)
                A_.wait_ge(ms["conv"], 8 * b + 8)
                for j in range(2):
                    last = A_.activation(mb["u"][:, j, :], mb["cv"][:, j, :], ACT.Silu, bias=mb["cols"][:, j, 0:1])
                last.then_inc(ms["u_ev"], 1)
                A_.wait_ge(ms["xd_mm"], b + 1)
                if not first:
                    A_.wait_ge(ms["dt_mm"], b)
                    A_.wait_ge(ms["split"], 6 * b)
                A_.activation(mb["xd"][:, :], psum[0:3 * XPW, 6, :], ACT.Copy).then_inc(ms["xd_ev"], 1)
                A_.wait_ge(ms["dt_ev"], b + 1)
                A_.activation(mb["ab"][:, :, :], mb["y"][:, :, :], ACT.Abs).then_inc(ms["abs"], 1)
                A_.wait_ge(ms["abs"], b + 1)
                A_.activation(mb["e"][:, :, :], mb["ab"][:, :, :], ACT.Exp, scale=-1.0).then_inc(ms["exp"], 1)
                A_.wait_ge(ms["poly"], (len(LOG1P) + 2) * b + (len(LOG1P) + 2))
                A_.wait_ge(ms["a2"], 1)
                for n in range(NST):
                    for j in range(2):
                        if not (first and n == 0):
                            A_.wait_ge(ms["h"], 32 * b + 2 * n + j - 1)
                        A_.activation(mb["da"][:, j, :], mb["dl"][:, j, :], ACT.Exp, scale=mb["a"][:, j, n:n + 1])\
                            .then_inc(ms["da"], 1)
                    A_.wait_ge(ms["c_mm"], 16 * b + n + 1)
                    if not (first and n < 2):
                        A_.wait_ge(ms["hc"], 32 * b + 2 * (n - 1))
                    A_.activation(mb["c"][:, n % 2, :], psum[:, 2 + n % 2, :], ACT.Copy).then_inc(ms["c_ev"], 1)

            batch(0, True)
            with A_.Fori(1, B) as b:
                batch(b, False)

        def dve_mamba():
            V.wait_ge(ms["in"], len(MB_IN) * 16)
            V.memset(mb["xp"][:, :, 0:SHIFT], 0.0).then_inc(ms["zero"], 1)
            V.wait_ge(ms["a1"], 1)
            V.tensor_scalar(mb["a"][:, :, :], mb["a"][:, :, :], -1.0, None, ALU.mult).then_inc(ms["a2"], 1)
            V.wait_ge(ms["zero"], 1)
            NP_ = len(LOG1P) + 2

            def batch(b, first):
                V.wait_ge(ms["x_ev"], b + 1)
                if not first:
                    V.wait_ge(ms["u_ev"], b)
                for k in range(CONV):
                    for j in range(2):
                        src, tap = mb["xp"][:, j, k:k + T], mb["conv"][:, j, k:k + 1]
                        if k == 0:
                            V.tensor_scalar(mb["cv"][:, j, :], src, tap, None, ALU.mult).then_inc(ms["conv"], 1)
                        else:
                            V.wait_ge(ms["conv"], 8 * b + (2 * (k - 1) + j + 1))
                            V.scalar_tensor_tensor(mb["cv"][:, j, :], src, tap, mb["cv"][:, j, :], ALU.mult, ALU.add)\
                                .then_inc(ms["conv"], 1)
                V.wait_ge(ms["xd_ev"], b + 1)
                part = mb["part"]
                if not first:
                    V.wait_ge(ms["c_mm"], 16 * b)
                V.tensor_copy(mb["hi"][:, :], mb["xd"][:, :]).then_inc(ms["split"], 1)
                V.wait_ge(ms["split"], 6 * b + 1)
                V.tensor_tensor(mb["r1"][:, :], mb["xd"][:, :], mb["hi"][:, :], ALU.subtract).then_inc(ms["split"], 1)
                V.wait_ge(ms["split"], 6 * b + 2)
                V.tensor_copy(mb["mid"][:, :], mb["r1"][:, :]).then_inc(ms["split"], 1)
                V.tensor_scalar(mb["pa"][:, :], mb["hi"][:, :], part[:, 0:1], None, ALU.mult)
                V.wait_ge(ms["split"], 6 * b + 3)
                V.tensor_tensor(mb["r2"][:, :], mb["r1"][:, :], mb["mid"][:, :], ALU.subtract).then_inc(ms["split"], 1)
                V.wait_ge(ms["split"], 6 * b + 4)
                V.scalar_tensor_tensor(mb["pb"][:, :], mb["mid"][:, :], part[:, 1:2], mb["pa"][:, :], ALU.mult, ALU.add)\
                    .then_inc(ms["split"], 1)
                V.wait_ge(ms["split"], 6 * b + 5)
                V.scalar_tensor_tensor(mb["parts"][:, :], mb["r2"][:, :], part[:, 2:3], mb["pb"][:, :],
                                       ALU.mult, ALU.add).then_inc(ms["split"], 1)
                V.wait_ge(ms["dt_mm"], b + 1)
                for j in range(2):
                    bias = mb["cols"][:, j, 1:2]
                    last = V.tensor_scalar(mb["y"][:, j, :], psum[:, j, :], bias, bias, ALU.add, ALU.add)
                last.then_inc(ms["dt_ev"], 1)
                V.wait_ge(ms["exp"], b + 1)
                if not first:
                    V.wait_ge(ms["da"], 32 * b)
                e, pl = mb["e"][:, :, :], mb["pl"][:, :, :]
                V.tensor_scalar(pl, e, LOG1P[-1], None, ALU.mult).then_inc(ms["poly"], 1)
                for i, c in enumerate(LOG1P[-2::-1]):
                    V.wait_ge(ms["poly"], NP_ * b + (i + 1))
                    V.scalar_tensor_tensor(pl, pl, c, e, ALU.add, ALU.mult).then_inc(ms["poly"], 1)
                V.wait_ge(ms["poly"], NP_ * b + (NP_ - 2))
                V.scalar_tensor_tensor(mb["dl"][:, :, :], mb["y"][:, :, :], 0.0, pl, ALU.max, ALU.add)\
                    .then_inc(ms["poly"], 1)
                V.wait_ge(ms["poly"], NP_ * b + (NP_ - 1))
                V.tensor_tensor(mb["du"][:, :, :], mb["dl"][:, :, :], mb["u"][:, :, :], ALU.mult).then_inc(ms["poly"], 1)
                V.wait_ge(ms["poly"], NP_ * b + NP_)
                for n in range(NST):
                    V.wait_ge(ms["b_mm"], 16 * b + n + 1)
                    for j in range(2):
                        k = 2 * n + j
                        if not (first and n == 0):
                            V.wait_ge(ms["h"], 32 * b + k - 1)
                        V.tensor_tensor(mb["bu"][:, j, :], psum[:, n % 2, :], mb["du"][:, j, :], ALU.mult)\
                            .then_inc(ms["bu"], 1)
                    for j in range(2):
                        k = 2 * n + j
                        V.wait_ge(ms["bu"], 32 * b + k + 1)
                        V.wait_ge(ms["da"], 32 * b + k + 1)
                        if not (first and n == 0):
                            V.wait_ge(ms["hc"], 32 * b + k - 1)
                        V.tensor_tensor_scan(mb["h"][:, j, :], mb["da"][:, j, :], mb["bu"][:, j, :], 0.0,
                                             ALU.mult, ALU.add).then_inc(ms["h"], 1)
                V.wait_ge(ms["y_mm"], 32 * b + 32)
                if not first:
                    V.wait_ge(ms["out_mm"], b)
                for j in range(2):
                    V.scalar_tensor_tensor(mb["yo"][:, j, :], mb["u"][:, j, :], mb["cols"][:, j, 2:3],
                                           psum[:, 4 + j, :], ALU.mult, ALU.add).then_inc(ms["yo"], 1)
                V.wait_ge(ms["z_ev"], b + 1)
                for j in range(2):
                    V.wait_ge(ms["yo"], 4 * b + (j + 1))
                    V.tensor_tensor(mb["yo"][:, j, :], mb["yo"][:, j, :], mb["zs"][:, j, :], ALU.mult)\
                        .then_inc(ms["yo"], 1)
                V.wait_ge(ms["out_mm"], b + 1)
                V.tensor_tensor(xm[:, b, :], xm[:, b, :], psum[:, 7, :], ALU.add).then_inc(x_ready, 1)

            batch(0, True)
            with nc.vector.Fori(1, B) as b:
                batch(b, False)

        def pool_mamba():
            def batch(b, first):
                for n in range(NST):
                    G.wait_ge(ms["c_ev"], 16 * b + n + 1)
                    for j in range(2):
                        k = 2 * n + j
                        G.wait_ge(ms["h"], 32 * b + k + 1)
                        if not (first and n == 0):
                            G.wait_ge(ms["y_mm"], 32 * b + k - 1)
                        G.tensor_tensor(mb["hc"][:, j, :], mb["h"][:, j, :], mb["c"][:, n % 2, :], ALU.mult)\
                            .then_inc(ms["hc"], 1)

            batch(0, True)
            with nc.gpsimd.Fori(1, B) as b:
                batch(b, False)

        block = ctx.enter_context(nc.Block())
        xin = a["x"].rearrange("b (t p) c -> p (b t) c", p=P)
        xout = a["out"].rearrange("b (t p) c -> p (b t) c", p=P)
        xrows = m["qk"][:, :, :].rearrange("p u n -> p (u n)")[:, 0:2 * 1024].rearrange("p (n c) -> p n c", c=D)

        @block.sync
        def _(sp):
            sp.dma_start(xrows, xin).then_inc(x_in, 16)
            for dst, name in CONSTS:
                sp.dma_start(dst[:], a[name]).then_inc(consts, 16)
            sp_gla(sp)
            sp.wait_ge(x_ready, 2 * B)
            sp.dma_start(m["rot"][:], a["rot"]).then_inc(rot_in, 16)
            sp_ffn(0)
            sp_mamba(sp)
            sp.wait_ge(x_ready, 4 * B)
            sp.dma_start(m["rot"][:], a["rot"]).then_inc(rot_in, 16)
            sp_ffn(PHASE)
            sp.wait_ge(out_ev, 4)
            sp.dma_start(xout, xrows).then_inc(out_st, 16)
            sp.wait_ge(out_st, 16)

        @block.tensor
        def _(pe):
            pe.wait_ge(consts, 16 * len(CONSTS))
            pe.wait_ge(x_in, 16)
            for g in range(B):
                if g >= 2:
                    pe.wait_ge(x_ready, g - 1)
                for i in range(4):
                    last = nc.tensor.transpose(tr_ps[g % 2][:, i * P:(i + 1) * P], xrows[:, 4 * g + i, :], ident[:, :])
                last.then_inc(x_tr, 1)
            pe_ln(0)
            pe_gla()
            pe_ln(1)
            pe_ffn(0)
            pe_ln(2)
            pe_mamba()
            pe_ln(3)
            pe_ffn(PHASE)
            for g in range(B):
                pe.wait_ge(x_ready, 4 * B + g + 1)
                if g >= 2:
                    pe.wait_ge(out_ev, g - 1)
                for i in range(4):
                    last = nc.tensor.transpose(tr_ps[g % 2][:, i * P:(i + 1) * P], xm[:, g, i * P:(i + 1) * P], ident[:, :])
                last.then_inc(out_tr, 1)

        @block.scalar
        def _(act):
            act.wait_ge(zeroed, 3)
            act_ln(0)
            act_gla()
            act_ln(1)
            act_ffn(0)
            act_ln(2)
            act_mamba()
            act_ln(3)
            act_ffn(PHASE)
            for g in range(B):
                act.wait_ge(out_tr, g + 1)
                nc.scalar.activation(xrows[:, 4 * g:4 * g + 4, :], tr_ps[g % 2].rearrange("p (i c) -> p i c", i=4),
                                     ACT.Copy).then_inc(out_ev, 1)

        def dve_ffn_start(n, stage):
            V.memset(m["kt"][:, :, 0:WIN], 0.0).then_inc(zeroed, 1)
            V.wait_ge(rot_in, 16 * n)
            V.wait_ge(ln_done[stage], B)
            V.wait_ge(zeroed, 3 + n)

        @block.vector
        def _(dve):
            V.memset(xf[:, :, 0:1], 0.0).then_inc(zeroed, 1)
            V.memset(eps_t[:, :], EPS).then_inc(zeroed, 1)
            V.memset(three_halves[:, :], 1.5).then_inc(zeroed, 1)
            for g in range(B):
                V.wait_ge(x_tr, g + 1)
                V.tensor_copy(xm[:, g, :], tr_ps[g % 2]).then_inc(x_ready, 1)
            dve_ln(0)
            dve_gla()
            dve_ln(1)
            dve_ffn_start(1, 1)
            dve_ffn(0)
            dve_add(1)
            dve_ln(2)
            dve_mamba()
            dve_ln(3)
            dve_ffn_start(2, 3)
            dve_ffn(PHASE)
            dve_add(2)

        @block.gpsimd
        def _(pool):
            pool_gla()
            pool_ffn(0)
            pool_mamba()
            pool_ffn(PHASE)


def constants():
    half = np.arange(0, DH, 2, dtype=np.float32)
    inv_freq = (1.0 / np.power(np.float32(10000.0), half / np.float32(DH))).astype(np.float32)
    t = np.arange(T, dtype=np.float32)
    freqs = t[:, None] * inv_freq[None, :]
    base = (half + np.float32(0.4 * DH)) / np.float32(1.4 * DH)
    power = (t - T // 2) / np.float32(WIN // 2)
    scale = np.power(base[None, :], power[:, None]).astype(np.float32)
    cos, sin = np.cos(freqs), np.sin(freqs)
    inv = np.float32(1.0) / scale

    def two(x, y):
        return np.concatenate([x, y], -1)

    rot = np.concatenate([two(cos * scale, cos * scale), two(-sin * scale, sin * scale),
                          two(cos * inv, cos * inv), two(-sin * inv, sin * inv)], -1).astype(np.float32)
    rot = rot.reshape(TILES, P, 4 * DH).transpose(1, 0, 2)
    tau = np.arange(WIN)
    prev = np.where(tau[:, None] > tau[None, :], MASKED, 0.0)
    own = np.where(tau[:, None] < tau[None, :], MASKED, 0.0)
    maskrow = np.zeros((64, HC, 2 * WIN), np.float32)
    maskrow[:WIN] = np.concatenate([prev, own], 1)[:, None, :]
    maskrow[WIN, :, :WIN] = MASKED
    onehot = np.zeros((64, 2, P), np.float32)
    onehot[:WIN] = np.tile(np.eye(WIN), (1, WPT))[:, None, :]
    onehot[WIN, 1, :WIN] = 1.0
    bf = mybir.dt.np(BF16)
    pick = np.zeros((P, 4 * (2 * GK - 1)), np.float32)
    pick[np.arange(P), 4 * (GK - 1) + np.arange(P) // GK] = 1.0
    bc = np.zeros((3 * XPW, 2 * NST, P), np.float32)
    part = np.zeros((3 * XPW, 3), np.float32)
    for i in range(3):
        part[i * XPW:(i + 1) * XPW, i] = 1.0
        for n in range(2 * NST):
            bc[i * XPW + RANK + n, n, :] = 1.0
    return {"gla_pick": pick, "mb_part": part, "mb_bc_pick": bc.astype(bf), "rot": np.ascontiguousarray(rot), "maskrow": maskrow.reshape(64, CH).astype(bf),
            "onehot": onehot.astype(bf), "ident": np.eye(P, dtype=np.float32),
            "center": (np.eye(P) - 1.0 / P).astype(np.float32), "mean": np.full((P, P), 1.0 / P, np.float32)}


def layout(inputs):
    f = {k: np.asarray(v) for k, v in inputs.items()}
    r = {"x": f["L0_attn_a_hidden_state"], "Wqkv": f["L0_ffn_Wqkv"], "Wo": f["L0_ffn_Wo"], "W1": f["L0_ffn_W1"],
         "W2": f["L0_ffn_W2"]}
    qs, ks = f["L0_ffn_q_scale"], f["L0_ffn_k_scale"]
    swap = np.concatenate([np.arange(DH // 2, DH), np.arange(DH // 2)])
    r["qk_scale"] = np.concatenate([qs, qs[:, swap], ks, ks[:, swap]], -1)[:, None, :]
    vec = np.zeros((DEPTH, P, NVEC), np.float32)
    vec[:, :, 0] = f["L0_ffn_ln_g"]
    vec[:, :, 1] = f["L0_ffn_ln_b"]
    for j, (at, n) in enumerate(DT_TILES):
        vec[:, :n, 2 + j] = f["L0_ffn_b1"][:, at:at + n]
        vec[:, :n, 5 + j] = f["L0_ffn_b1"][:, DI + at:DI + at + n]
    vec[:, :, 8] = f["L0_ffn_b2"]
    r["vectors"] = vec

    def chan(x):
        return x.reshape(2, P, -1).transpose(1, 0, 2)

    g = {n: f["L0_attn_a_" + n] for n in ("Wq", "bq", "Wk", "bk", "Wv", "bv", "Wg", "bg", "Wo", "bo")}
    r["gla_w"] = np.stack([g["Wq"], g["Wk"], g["Wg"], g["Wv"]], 1)
    r["gla_b"] = np.tile(np.stack([g["bq"], g["bk"], g["bg"], g["bv"]], 1), (B, 1))
    wo = np.zeros((GK, B, B, D), np.float32)
    for b in range(B):
        wo[:, b, b, :] = g["Wo"]
    r["gla_wo"] = wo.reshape(P, B, D)
    r["gla_bo"] = g["bo"][:, None]
    h = {n: f["L0_attn_b_" + n] for n in ("in_proj_w", "conv_w", "conv_b", "x_proj_w", "dt_proj_w", "dt_proj_b",
                                          "A_log", "D_skip", "out_proj_w")}
    r["mb_in_w"] = h["in_proj_w"]
    r["mb_conv"] = chan(h["conv_w"])
    r["mb_cols"] = chan(np.stack([h["conv_b"], h["dt_proj_b"], h["D_skip"]], 1))
    r["mb_x_w"] = chan(np.concatenate([h["x_proj_w"]] * 3, 1))
    r["mb_dt_w"] = h["dt_proj_w"]
    r["mb_alog"] = chan(h["A_log"])
    r["mb_out_w"] = chan(h["out_proj_w"])
    return {k: np.ascontiguousarray(v) for k, v in (r | constants()).items()}


def kernel(**inputs):
    import numpy as np
    import concourse.bacc as bacc
    from concourse import mybir
    from concourse.bass_utils import run_bass_kernel_spmd

    arrays = {"in_" + name: value for name, value in layout(inputs).items()}
    nc = bacc.Bacc("TRN2", target_bir_lowering=False, num_devices=1)
    tensors = {name[3:]: nc.dram_tensor(name, value.shape, mybir.dt.from_np(value.dtype), kind="ExternalInput").ap()
               for name, value in arrays.items()}
    tensors["out"] = nc.dram_tensor("out_x", (B, T, D), F32, kind="ExternalOutput").ap()
    build(nc, tensors)
    result = run_bass_kernel_spmd(nc, [arrays], core_ids=[0])
    return result.results[0]["out_x"]
```

```python
import numpy as np
import concourse.bass as bass
from concourse import mybir
from contextlib import ExitStack

F32 = mybir.dt.float32
F32R = mybir.dt.float32r
BF16 = mybir.dt.bfloat16
I32 = mybir.dt.int32
ALU = mybir.AluOpType
ACT = mybir.ActivationFunctionType
AX = mybir.AxisListType

P = 128
B, T, D = 4, 512, 128
EPS = 1e-5
DEPTH, HEADS, DH, WIN = 6, 16, 64, 32
INNER = HEADS * DH
HP = HEADS // 2
QK_SCALE = 8.0
DI = int(D * 4 * 2 / 3)
DT_TILES = [(0, 128), (128, 128), (256, DI - 256)]
TILES = T // P
WPT = P // WIN
CH = 512
NCH = 3 * INNER // CH
HC = CH // DH
QKC = 2 * INNER // CH
WQ = 3 * INNER // 4
PHASE = DEPTH * B
NEWTON, NEWTON_DVE = 3, 2
MAGIC = 0x5F3759DF
MASKED = -1e30
NVEC = 9
GK = 32
RING = 4
NST, DIN, RANK, CONV = 16, 256, 8, 4
XPW = RANK + 2 * NST
SHIFT = 2 * (CONV - 1)
LOG1P = [float(c) for c in np.polynomial.chebyshev.Chebyshev.interpolate(
    lambda e: np.log1p(e) / e, 9, domain=[0, 1]).convert(kind=np.polynomial.Polynomial).coef]


def cnt(it, per_unit, j, k=0):
    return it * (TILES * per_unit) + (per_unit * j + k)


def wait(eng, sem, value):
    if isinstance(value, int) and value <= 0:
        return
    eng.wait_ge(sem, value)


def build(nc, a):
    ctx = ExitStack()
    with ctx:
        def sb(name, shape, dt=F32):
            return ctx.enter_context(nc.sbuf_tensor(name, shape, dt))

        def sem(name):
            return ctx.enter_context(nc.semaphore(name))

        xm = sb("x_main", [P, B, T])
        xf = sb("x_ffn", [P, B, T + 1])
        ident = sb("ident", [P, P])
        center = sb("center", [P, P])
        mean = sb("mean", [P, P])
        onehot = sb("onehot", [P, 2, P], BF16)
        maskrow = sb("maskrow", [P, CH], BF16)
        eps_t = sb("eps_t", [P, 1])
        three_halves = sb("three_halves", [P, 2 * HEADS])
        CONSTS = ((ident, "ident"), (center, "center"), (mean, "mean"), (onehot, "onehot"), (maskrow, "maskrow"))
        ln_xc = sb("ln_xc", [P, T])
        hidden = sb("hidden", [P, 3, T])
        gelu = sb("gelu", [P, 2, T])
        mlp_xs = hidden[:, 0, :]
        ln_sq = hidden[:, 1, :]
        ln_rstd = gelu[:, 1, :]
        ln_diag = gelu[:, 1, :].rearrange("p (t q) -> p t q", t=TILES)
        ln_cols = sb("ln_cols", [P, 2, B, TILES])
        ln_col_std = sb("ln_col_std", [P, TILES])
        ln_col_rstd = sb("ln_col_rstd", [P, TILES])

        psum = ctx.enter_context(nc.psum_tensor("psum", [P, 8, CH], F32))
        proj_ps = [psum[:, 0, :], psum[:, 1, :]]
        tr_ps = [psum[:, 2, :], psum[:, 3, :]]
        s_ps = [psum[:, 4, :], psum[:, 5, :]]
        o_ps = [psum[:, 6, :], psum[:, 7, :]]

        consts = sem("consts")
        rot_in = sem("rot_in")
        zeroed = sem("zeroed")
        x_in = sem("x_in")
        x_tr = sem("x_tr")
        x_ready = sem("x_ready")
        lnc_mm, lnx_ev, lnv_mm, lnstd_done, ln_rs, ln_diag_done, ln_spread = (
            sem(n) for n in ("lnc_mm", "lnx_ev", "lnv_mm", "lnstd_done", "ln_rs", "ln_diag_done", "ln_spread"))
        out_tr, out_ev, out_st = sem("out_tr"), sem("out_ev"), sem("out_st")
        added = sem("added")

        wqkv_hi = sb("wqkv_hi", [P, 2, 3 * INNER], F32R)
        wqkv_lo = sb("wqkv_lo", [P, 2, 3 * INNER], F32R)
        wqkv_staged = sb("wqkv_staged", [P, 1, WQ])
        fctx = ctx.enter_context(ExitStack())

        def fsb(name, shape, dt=F32):
            return fctx.enter_context(nc.sbuf_tensor(name, shape, dt))

        def ffn_buffers():
            m = {}
            m["wh"], m["wl"], m["wst"] = wqkv_hi, wqkv_lo, wqkv_staged
            m["wo"] = fsb("wo", [P, HP, D])
            m["w1"] = fsb("w1", [P, 2 * DI])
            m["w2"] = fsb("w2", [P, 3, D])
            m["vec"] = fsb("layer_vectors", [P, NVEC])
            m["rot"] = fsb("rot_base", [P, TILES, 4 * DH])
            m["rots"] = fsb("rot_scaled", [P, TILES, 4 * DH])
            m["qks"] = fsb("qk_scale", [P, 4 * DH])
            m["xh"] = fsb("xs_hi", [P, 2, P], F32R)
            m["xl"] = fsb("xs_lo", [P, 2, P], F32R)
            m["sq"] = fsb("squares", [P, 2, CH])
            m["ma"] = fsb("rot_cos", [P, 2, CH])
            m["mb"] = fsb("rot_sin", [P, 2, CH])
            m["qk"] = fsb("qk_rows", [P, 2, 2 * INNER])
            m["ss"] = fsb("sumsq", [P, 2 * HEADS])
            m["ny"] = fsb("newton_y", [P, 2 * HEADS])
            m["nt"] = fsb("newton_t", [P, 2 * HEADS])
            m["hs"] = fsb("minus_half_sumsq", [P, 2 * HEADS])
            m["rn"] = fsb("rnorm", [P, 2, 2 * HEADS])
            m["v"] = fsb("v_rows", [P, 2, 2, HP * DH])
            m["vp"] = fsb("v_pairs", [P, 2, WPT, HP * DH])
            m["qt"] = fsb("q_t", [P, HP, P])
            m["kt"] = fsb("k_t", [P, HP, WIN + T])
            m["mx"] = fsb("row_max", [P, 2, HP])
            m["nmax"] = fsb("row_max_scaled", [P, HP])
            m["p"] = fsb("probs", [P, HP, 2, 2 * WIN])
            m["pt"] = fsb("probs_t", [P, HP, P])
            m["den"] = fsb("den", [P, 2, HP])
            m["rden"] = fsb("rden", [P, 2, 2, HP])
            m["o"] = fsb("o_rows", [P, HP, 2, DH])
            m["ot"] = fsb("o_t", [P, HP, T])
            m["xn"] = fsb("xn_mlp", [P, T])
            m["gl"], m["h"], m["xs"] = gelu, hidden, mlp_xs
            return m

        m = ffn_buffers()
        fctx.close()

        def gla_buffers():
            gb = {}
            gb["w"] = fsb("gla_w", [P, 4, GK])
            gb["b"] = fsb("gla_b", [P, 4])
            gb["wo"] = fsb("gla_wo", [P, B, D])
            gb["bo"] = fsb("gla_bo", [P, 1])
            gb["pick"] = fsb("gla_pick", [P, 4 * (2 * GK - 1)])
            gb["q"] = fsb("gla_q", [P, T])
            gb["k"] = fsb("gla_k", [P, T])
            gb["g"] = fsb("gla_g", [P, T])
            gb["v"] = fsb("gla_v", [P, T])
            gb["zero"] = fsb("gla_zero", [P, P])
            gb["spread"] = fsb("gla_spread", [P, RING, B, GK])
            gb["gather"] = fsb("gla_gather", [P, RING, P])
            gb["kv"] = fsb("gla_kv", [P, RING, T])
            gb["st"] = fsb("gla_state", [P, RING, T])
            gb["sq"] = fsb("gla_state_q", [P, RING, T])
            gb["o"] = fsb("gla_out", [P, T])
            return gb

        gb = gla_buffers()
        fctx.close()

        def mamba_buffers():
            mb = {}
            mb["win"] = fsb("mb_in_w", [P, 2 * DIN])
            mb["conv"] = fsb("mb_conv", [P, 2, CONV])
            mb["cols"] = fsb("mb_cols", [P, 2, 3])
            mb["xw"] = fsb("mb_x_w", [P, 2, 3 * XPW])
            mb["dtw"] = fsb("mb_dt_w", [RANK, DIN])
            mb["alog"] = fsb("mb_alog", [P, 2, NST])
            mb["a"] = fsb("mb_a", [P, 2, NST])
            mb["wout"] = fsb("mb_out_w", [P, 2, D])
            mb["part"] = fsb("mb_part", [3 * XPW, 3])
            mb["bc"] = fsb("mb_bc_pick", [3 * XPW, 2 * NST, P], BF16)
            mb["xp"] = fsb("mb_x", [P, 2, SHIFT + T])
            mb["zs"] = fsb("mb_z", [P, 2, T])
            mb["cv"] = fsb("mb_conv_out", [P, 2, T])
            mb["u"] = fsb("mb_u", [P, 2, T])
            mb["xd"] = fsb("mb_xdbl", [3 * XPW, T])
            mb["hi"] = fsb("mb_hi", [3 * XPW, T], BF16)
            mb["mid"] = fsb("mb_mid", [3 * XPW, T], BF16)
            mb["r1"] = fsb("mb_rest", [3 * XPW, T])
            mb["r2"] = fsb("mb_rest2", [3 * XPW, T])
            mb["pa"] = fsb("mb_parts_a", [3 * XPW, T])
            mb["pb"] = fsb("mb_parts_b", [3 * XPW, T])
            mb["parts"] = fsb("mb_parts", [3 * XPW, T], BF16)
            mb["y"] = fsb("mb_dt", [P, 2, T])
            mb["ab"] = fsb("mb_dt_abs", [P, 2, T])
            mb["e"] = fsb("mb_dt_exp", [P, 2, T])
            mb["pl"] = fsb("mb_poly", [P, 2, T])
            mb["dl"] = fsb("mb_delta", [P, 2, T])
            mb["du"] = fsb("mb_du", [P, 2, T])
            mb["da"] = fsb("mb_decay", [P, 2, 2, T])
            mb["bu"] = fsb("mb_bu", [P, 2, 2, T])
            mb["h"] = fsb("mb_h", [P, 2, 2, T])
            mb["c"] = fsb("mb_c", [P, 2, T])
            mb["hc"] = fsb("mb_hc", [P, 2, 2, T])
            mb["yo"] = fsb("mb_y", [P, 2, T])
            return mb

        mb = mamba_buffers()
        gs = {n: sem("g_" + n) for n in (
            "in", "zero", "proj_mm", "proj_ev", "spread_sel", "gather_sel", "vb_mm", "kv", "st", "sq", "sum_mm", "o_ev",
            "out_mm")}
        ms = {n: sem("m_" + n) for n in (
            "in", "zero", "a1", "a2", "in_mm", "x_ev", "z_ev", "conv", "u_ev", "xd_mm", "xd_ev", "split", "dt_mm",
            "dt_ev", "abs", "exp", "poly", "du", "da", "b_mm", "c_mm", "bu", "h", "c_ev", "hc", "y_mm", "yo",
            "out_mm", "added")}
        S = {n: sem(n) for n in (
            "xs_hi", "xs_lo", "wstaged", "whi_done", "wconv", "qkv_mm", "sq_done", "m_done", "red_done",
            "seed", "newton", "add_done", "rot_done", "v_ev", "vp0", "vp1", "oT_mm", "oT_ev", "qkT_mm",
            "qkT_ev", "s_mm", "max_done", "bias_done", "sub_done", "den_sum", "exp1_done", "exp0_done", "den_done", "pT_mm", "pT_ev",
            "o_mm", "o_ev", "wo_in", "w1_in", "w2_in", "vec_in", "qks_in", "rots_done", "d1_mm", "d1_ev",
            "mlp_xs", "d2_mm", "xc_ev", "d3_mm", "std_done", "rstd_done", "diag_done", "d6_mm", "xn1", "xn2", "d4_mm",
            "gelu_done", "h_done", "hidden_done", "d5_mm", "stream")}
        ln_done = [sem("ln0_done"), S["stream"], sem("ln2_done"), sem("ln3_done")]
        vp_sem = [S["vp0"], S["vp1"]]

        def pe_proj(it, u, c):
            layer = (it + u // TILES) // B
            if c == 0:
                nc.tensor.wait_ge(S["xs_lo"], cnt(it, 1, u, 1))
                nc.tensor.wait_ge(S["wconv"], layer * B + B)
            if c < 2:
                wait(nc.tensor, S["v_ev"], cnt(it, 2, u, c - 1))
            else:
                wait(nc.tensor, S["sq_done"], cnt(it, QKC, u, c - 1))
                wait(nc.tensor, S["m_done"], cnt(it, QKC, u, c - 1))
            cols = slice(c * CH, (c + 1) * CH)
            xh, xl = m["xh"][:, u % 2, :], m["xl"][:, u % 2, :]
            wh, wl = m["wh"][:, layer % 2, cols], m["wl"][:, layer % 2, cols]
            nc.tensor.matmul(proj_ps[c % 2], xh, wh, start=True, stop=False)
            nc.tensor.matmul(proj_ps[c % 2], xh, wl, start=False, stop=False)
            nc.tensor.matmul(proj_ps[c % 2], xl, wh, start=False, stop=True).then_inc(S["qkv_mm"], 1)

        def pe_out_t(it, u, qk_after):
            for g in range(2):
                nc.tensor.wait_ge(S["o_ev"], cnt(it, 2, u, 2))
                if qk_after:
                    nc.tensor.wait_ge(S["qkT_ev"], cnt(it, 4, u + 2, g + 3))
                else:
                    nc.tensor.wait_ge(S["pT_ev"], cnt(it, 2, u, g + 1))
                for i in range(4):
                    hp = 4 * g + i
                    last = nc.tensor.transpose(tr_ps[g][:, i * P:(i + 1) * P],
                                               m["o"][:, hp, :, :].rearrange("p a e -> p (a e)"),
                                               ident[:, :])
                last.then_inc(S["oT_mm"], 1)

        def pe_qk_t(it, u, after, groups):
            for g in groups:
                nc.tensor.wait_ge(S["rot_done"], cnt(it, QKC, u, g + 1))
                if g >= 2:
                    nc.tensor.wait_ge(S["qkT_ev"], cnt(it, 4, u, g - 1))
                elif after:
                    nc.tensor.wait_ge(S["pT_ev"], cnt(it, 2, u - 2, g + 1))
                for i in range(4):
                    last = nc.tensor.transpose(tr_ps[g % 2][:, i * P:(i + 1) * P],
                                               m["qk"][:, u % 2, (4 * g + i) * P:(4 * g + i + 1) * P],
                                               ident[:, :])
                last.then_inc(S["qkT_mm"], 1)

        def pe_probs_t(it, u, qk_after, out_before):
            for g in range(2):
                nc.tensor.wait_ge(S["exp0_done"], cnt(it, 1, u, 1))
                nc.tensor.wait_ge(S["exp1_done"], cnt(it, 1, u, 1))
                if out_before:
                    nc.tensor.wait_ge(S["oT_ev"], cnt(it, 2, u - 1, g + 1))
                elif qk_after:
                    nc.tensor.wait_ge(S["qkT_ev"], cnt(it, 4, u + 1, g + 3))
                for i in range(4):
                    hp = 4 * g + i
                    last = nc.tensor.transpose(tr_ps[g][:, i * P:(i + 1) * P],
                                               m["p"][:, hp, :, :].rearrange("p a k -> p (a k)"),
                                               ident[:, :])
                last.then_inc(S["pT_mm"], 1)

        def pe_scores(it, u, half):
            t = u % TILES
            if half == 0:
                nc.tensor.wait_ge(S["qkT_ev"], cnt(it, 4, u, 4))
                for g in range(2):
                    wait(nc.tensor, S["exp1_done" if g else "sub_done"], cnt(it, 1, u))
                    nc.tensor.matmul(s_ps[g], onehot[64 * g:64 * g + 64, 1 if t == 0 else 0, :],
                                     maskrow[64 * g:64 * g + 64, :], start=True, stop=False,
                                     skip_group_check=True)
            for hp in range(4 * half, 4 * half + 4):
                for par in range(2):
                    rows = slice(64 * par, 64 * par + 64)
                    for w in range(WPT):
                        last = nc.tensor.matmul(
                            s_ps[par][WIN * w:WIN * w + WIN, 64 * hp:64 * hp + 64],
                            m["qt"][rows, hp, WIN * w:WIN * w + WIN],
                            m["kt"][rows, hp, t * P + WIN * w:t * P + WIN * w + 2 * WIN],
                            start=False, stop=True, skip_group_check=True)
                    if hp == HP - 1:
                        last.then_inc(S["s_mm"], 1)

        def pe_pv(it, u, half):
            for hp in range(4 * half, 4 * half + 4):
                for par in range(2):
                    rows = slice(64 * par, 64 * par + 64)
                    for w in range(WPT):
                        last = nc.tensor.matmul(
                            o_ps[par][WIN * w:WIN * w + WIN, 64 * hp:64 * hp + 64],
                            m["pt"][rows, hp, WIN * w:WIN * w + WIN],
                            m["vp"][rows, u % 2, w, DH * hp:DH * hp + DH],
                            start=True, stop=True)
                    if hp == HP - 1:
                        last.then_inc(S["o_mm"], 1)

        def pe_pv_ready(it, u, mlp):
            nc.tensor.wait_ge(vp_sem[u % 2], it * 512 + 256 * (u // 2 + 1))
            nc.tensor.wait_ge(S["pT_ev"], cnt(it, 2, u, 2))
            wait(nc.tensor, S["o_ev"], cnt(it, 2, u))
            if mlp:
                pe_pv_banks(it - 1, u)

        def pe_wo(e, half):
            if half == 0:
                nc.tensor.wait_ge(S["wo_in"], (e + 1) * 16)
                nc.tensor.wait_ge(S["oT_ev"], (e + 1) * 8)
                nc.tensor.wait_ge(S["o_ev"], (e + 1) * 8 - 1)
            for hp in range(4 * half, 4 * half + 4):
                last = nc.tensor.matmul(o_ps[0], m["wo"][:, hp, :], m["ot"][:, hp, :],
                                        start=(hp == 0), stop=(hp == HP - 1))
            if half == 1:
                last.then_inc(S["d1_mm"], 1)

        def pe_center(e, o_free):
            wait(nc.tensor, S["o_ev"], o_free)
            nc.tensor.wait_ge(S["mlp_xs"], e + 1)
            nc.tensor.matmul(o_ps[0], center[:, :], m["xs"][:, :], start=True, stop=True).then_inc(S["d2_mm"], 1)

        def pe_var(e, o_free):
            wait(nc.tensor, S["o_ev"], o_free)
            nc.tensor.wait_ge(S["xc_ev"], 2 * (e + 1))
            for t in range(TILES):
                last = nc.tensor.matmul(o_ps[1][:, t:t + 1], ln_sq[:, t * P:(t + 1) * P], mean[:, 0:1],
                                        start=True, stop=True)
            last.then_inc(S["d3_mm"], 1)

        def pe_rstd(e, o_free):
            wait(nc.tensor, S["o_ev"], o_free)
            nc.tensor.wait_ge(S["diag_done"], e + 1)
            nc.tensor.matmul(o_ps[1], mean[:, :], ln_rstd[:, :], start=True, stop=True).then_inc(S["d6_mm"], 1)

        def pe_up(e, j, o_free):
            if j < 2:
                wait(nc.tensor, S["o_ev"], o_free)
            if j == 0:
                nc.tensor.wait_ge(S["w1_in"], (e + 1) * 16)
                nc.tensor.wait_ge(S["xn2"], e + 1)
            if j > 0:
                nc.tensor.wait_ge(S["h_done"], 2 * e + j)
                nc.tensor.wait_ge(S["gelu_done"], 3 * e + j)
            at, n = DT_TILES[j]
            nc.tensor.matmul(o_ps[1][:n, :], m["w1"][:, DI + at:DI + at + n], m["xn"][:, :], start=True, stop=True)
            nc.tensor.matmul(o_ps[0][:n, :], m["w1"][:, at:at + n], m["xn"][:, :],
                             start=True, stop=True).then_inc(S["d4_mm"], 1)

        def pe_down(e, o_free):
            wait(nc.tensor, S["o_ev"], o_free)
            nc.tensor.wait_ge(S["w2_in"], (e + 1) * 32)
            nc.tensor.wait_ge(S["hidden_done"], e + 1)
            for j, (_, n) in enumerate(DT_TILES):
                last = nc.tensor.matmul(o_ps[0], m["w2"][:n, j, :], m["h"][:n, j, :], start=(j == 0), stop=(j == 2))
            last.then_inc(S["d5_mm"], 1)

        def pe_pv_banks(e, u):
            if u == 0:
                nc.tensor.wait_ge(S["d1_ev"], e + 1)
            elif u == 1:
                nc.tensor.wait_ge(S["xc_ev"], 2 * (e + 1))
                nc.tensor.wait_ge(S["std_done"], e + 1)
            elif u == 2:
                nc.tensor.wait_ge(S["h_done"], 2 * e + 1)
            else:
                nc.tensor.wait_ge(S["stream"], B + e + 1)

        def pe_body(it, mlp, ahead):
            for u in range(TILES):
                o_free = cnt(it, 2, u)
                proj, nxt, prev = ahead or u + 2 < TILES, ahead or u + 1 < TILES, mlp or u > 0
                if nxt:
                    pe_qk_t(it, u + 1, prev, (0, 1))
                if proj:
                    pe_proj(it, u + 2, 1)
                if mlp and u == 1:
                    pe_center(it - 1, o_free)
                if mlp and u == 3:
                    pe_up(it - 1, 1, o_free)
                if nxt:
                    pe_qk_t(it, u + 1, prev, (2, 3))
                if mlp and u == 2:
                    pe_rstd(it - 1, o_free)
                if proj:
                    pe_proj(it, u + 2, 2)
                if prev:
                    pe_out_t(it, u - 1, nxt)
                if mlp and u == 3:
                    pe_up(it - 1, 2, o_free)
                if proj:
                    pe_proj(it, u + 2, 3)
                if mlp and u == 0:
                    pe_wo(it - 1, 0)
                if mlp and u == 1:
                    pe_var(it - 1, o_free)
                if mlp and u == 2:
                    pe_up(it - 1, 0, o_free)
                pe_probs_t(it, u, nxt, prev)
                if nxt:
                    pe_scores(it, u + 1, 0)
                if proj:
                    pe_proj(it, u + 2, 4)
                if mlp and u == 0:
                    pe_wo(it - 1, 1)
                if mlp and u == 3:
                    pe_down(it - 1, o_free)
                if nxt:
                    pe_scores(it, u + 1, 1)
                pe_pv_ready(it, u, mlp)
                if proj:
                    pe_proj(it, u + 2, 5)
                pe_pv(it, u, 0)
                if ahead or u + 3 < TILES:
                    pe_proj(it, u + 3, 0)
                pe_pv(it, u, 1)

        def pe_ffn(first):
            last = first + PHASE - 1
            for u in range(2):
                for c in range(NCH):
                    pe_proj(first, u, c)
            pe_qk_t(first, 0, False, range(4))
            pe_scores(first, 0, 0)
            pe_scores(first, 0, 1)
            pe_proj(first, 2, 0)
            pe_body(first, False, True)
            if first == 0:
                pe_body(1, True, True)
            with nc.tensor.Fori(max(first + 1, 2), last) as it:
                pe_body(it, True, True)
            pe_body(last, True, False)
            pe_out_t(last, 3, False)
            pe_wo(last, 0)
            pe_wo(last, 1)
            pe_center(last, 0)
            pe_var(last, 0)
            nc.tensor.wait_ge(S["std_done"], last + 1)
            pe_rstd(last, 0)
            for j in range(3):
                pe_up(last, j, 0)
            pe_down(last, 0)

        def act_square(it, u, c):
            nc.scalar.wait_ge(S["qkv_mm"], cnt(it, NCH, u, c + 1))
            wait(nc.scalar, S["red_done"], cnt(it, QKC, u, c - 1))
            nc.scalar.activation(m["sq"][:, c % 2, :], proj_ps[c % 2], ACT.Square).then_inc(S["sq_done"], 1)

        def act_v(it, u, c):
            nc.scalar.wait_ge(S["qkv_mm"], cnt(it, NCH, u, QKC + c + 1))
            if c == 0:
                wait(nc.scalar, vp_sem[u % 2], it * 512 + 256 * (u // 2))
                wait(nc.scalar, vp_sem[(u + 1) % 2], it * 512 + 256 * ((u - 1) // 2 + 1))
            nc.scalar.activation(
                m["v"][:, u % 2, :, 256 * c:256 * c + 256].rearrange("p a (i e) -> p i a e", e=DH),
                proj_ps[c % 2].rearrange("p (i a e) -> p i a e", a=2, e=DH), ACT.Copy).then_inc(S["v_ev"], 1)

        def act_out_t(it, u):
            t = u % TILES
            for g in range(2):
                nc.scalar.wait_ge(S["oT_mm"], cnt(it, 2, u, g + 1))
                if t == 0:
                    wait(nc.scalar, S["d1_mm"], it + u // TILES)
                nc.scalar.activation(m["ot"][:, 4 * g:4 * g + 4, t * P:(t + 1) * P],
                                     tr_ps[g].rearrange("p (i q) -> p i q", i=4), ACT.Copy).then_inc(S["oT_ev"], 1)

        def act_qk_t(it, u, groups):
            t = u % TILES
            wait(nc.scalar, S["s_mm"], cnt(it, 2, u))
            for g in groups:
                nc.scalar.wait_ge(S["qkT_mm"], cnt(it, 4, u, g + 1))
                hp = 4 * (g % 2)
                out = (m["qt"][:, hp:hp + 4, :] if g < 2
                       else m["kt"][:, hp:hp + 4, WIN + t * P:WIN + (t + 1) * P])
                nc.scalar.activation(out, tr_ps[g % 2].rearrange("p (i q) -> p i q", i=4), ACT.Copy)\
                    .then_inc(S["qkT_ev"], 1)

        def act_probs_t(it, u):
            for g in range(2):
                nc.scalar.wait_ge(S["pT_mm"], cnt(it, 2, u, g + 1))
                wait(nc.scalar, S["o_mm"], cnt(it, 2, u - 1, g + 1))
                nc.scalar.activation(m["pt"][:, 4 * g:4 * g + 4, :], tr_ps[g].rearrange("p (i q) -> p i q", i=4),
                                     ACT.Copy).then_inc(S["pT_ev"], 1)

        def act_exp_odd(it, u):
            nc.scalar.wait_ge(S["bias_done"], cnt(it, 1, u, 1))
            wait(nc.scalar, S["pT_mm"], cnt(it, 2, u))
            wait(nc.scalar, S["den_done"], cnt(it, 1, u))
            for hp in range(HP):
                last = nc.scalar.activation(m["p"][:, hp, 1, :], s_ps[1][:, 2 * WIN * hp:2 * WIN * (hp + 1)], ACT.Exp,
                                            scale=QK_SCALE, bias=m["nmax"][:, hp:hp + 1],
                                            accum_out=m["den"][:, 1, hp:hp + 1])
            last.then_inc(S["exp1_done"], 1)

        def act_exp_even(it, u):
            nc.scalar.wait_ge(S["sub_done"], cnt(it, 1, u, 1))
            nc.scalar.activation(m["p"][:, :, 0, :], m["p"][:, :, 0, :], ACT.Exp, scale=QK_SCALE)\
                .then_inc(S["exp0_done"], 1)

        def act_center(e):
            nc.scalar.wait_ge(S["d2_mm"], e + 1)
            wait(nc.scalar, S["xn1"], e)
            nc.scalar.activation(ln_xc[:, :], o_ps[0], ACT.Copy).then_inc(S["xc_ev"], 1)
            wait(nc.scalar, S["d3_mm"], e)
            nc.scalar.activation(ln_sq[:, :], o_ps[0], ACT.Square).then_inc(S["xc_ev"], 1)

        def act_std(e):
            nc.scalar.wait_ge(S["d3_mm"], e + 1)
            wait(nc.scalar, S["rstd_done"], e)
            nc.scalar.activation(ln_col_std[:, :], o_ps[1][:, 0:TILES], ACT.Sqrt, bias=eps_t[:, :])\
                .then_inc(S["std_done"], 1)

        def act_gelu(e, j):
            n = DT_TILES[j][1]
            nc.scalar.wait_ge(S["d4_mm"], 3 * e + j + 1)
            if j == 0:
                nc.scalar.wait_ge(S["vec_in"], (e + 1) * 16)
            if j == 0:
                wait(nc.scalar, S["hidden_done"], e)
            if j == 2:
                nc.scalar.wait_ge(S["h_done"], 2 * e + 1)
            nc.scalar.activation(m["gl"][:n, j % 2, :], o_ps[1][:n, :], ACT.Gelu,
                                 bias=m["vec"][:n, 5 + j:6 + j]).then_inc(S["gelu_done"], 1)

        def act_body(it, mlp, ahead):
            for u in range(TILES):
                proj, nxt, prev = ahead or u + 2 < TILES, ahead or u + 1 < TILES, mlp or u > 0
                if nxt:
                    act_qk_t(it, u + 1, (0, 1))
                if proj:
                    act_square(it, u + 2, 1)
                if mlp and u == 3:
                    act_gelu(it - 1, 1)
                if nxt:
                    act_qk_t(it, u + 1, (2, 3))
                if mlp and u == 1:
                    act_center(it - 1)
                if proj:
                    act_square(it, u + 2, 2)
                if prev:
                    act_out_t(it, u - 1)
                if proj:
                    act_square(it, u + 2, 3)
                if mlp and u == 1:
                    act_std(it - 1)
                if mlp and u == 2:
                    act_gelu(it - 1, 0)
                if mlp and u == 3:
                    act_gelu(it - 1, 2)
                act_probs_t(it, u)
                if proj:
                    act_v(it, u + 2, 0)
                if proj:
                    act_v(it, u + 2, 1)
                if nxt:
                    act_exp_odd(it, u + 1)
                if ahead or u + 3 < TILES:
                    act_square(it, u + 3, 0)
                if nxt:
                    act_exp_even(it, u + 1)

        def act_ffn(first):
            last = first + PHASE - 1
            for u in range(2):
                for c in range(QKC):
                    act_square(first, u, c)
                for c in range(2):
                    act_v(first, u, c)
            act_qk_t(first, 0, range(4))
            act_exp_odd(first, 0)
            act_square(first, 2, 0)
            act_exp_even(first, 0)
            act_body(first, False, True)
            if first == 0:
                act_body(1, True, True)
            with nc.scalar.Fori(max(first + 1, 2), last) as it:
                act_body(it, True, True)
            act_body(last, True, False)
            act_out_t(last, 3)
            act_center(last)
            act_std(last)
            for j in range(3):
                act_gelu(last, j)

        V = nc.vector

        def dve_xs(it, u):
            t, b = u % TILES, (it + u // TILES) % B
            wait(V, S["qkv_mm"], cnt(it, NCH, u - 1))
            V.wait_ge(S["stream"], it + u // TILES + 1)
            halves = [(slice(0, 64), xf[0:64, b, 1 + t * P:1 + (t + 1) * P]),
                      (slice(64, 128), xf[64:128, b, t * P:(t + 1) * P])]
            for rows, src in halves:
                V.tensor_scalar(m["xh"][rows, u % 2, :], src, 1.0, None, ALU.mult).then_inc(S["xs_hi"], 1)
            V.wait_ge(S["xs_hi"], cnt(it, 2, u, 2))
            for rows, src in halves:
                last_ = V.tensor_tensor(m["xl"][rows, u % 2, :], src, m["xh"][rows, u % 2, :].bitcast(F32), ALU.subtract)
            last_.then_inc(S["xs_lo"], 1)

        def dve_tables(e, half):
            V.wait_ge(S["qks_in"], (e + 1) * 16)
            tiles = slice(2 * half, 2 * half + 2)
            wait(V, S["m_done"], (e - 1) * (TILES * QKC) + (2 * half + 2) * QKC)
            V.tensor_tensor(m["rots"][:, tiles, :], m["rot"][:, tiles, :],
                            m["qks"][:, :].unsqueeze(1).to_broadcast([P, 2, 4 * DH]), ALU.mult)\
                .then_inc(S["rots_done"], 1)

        def dve_rotate(it, u, chunks):
            t = u % TILES
            if t % 2 == 0 and chunks[0] == 0:
                V.wait_ge(S["rots_done"], 2 * it + (2 * (u // TILES) + t // 2 + 1))
            for c in chunks:
                o = 2 * DH * (c // 2)
                ps = proj_ps[c % 2].rearrange("p (h e) -> p h e", e=DH)
                ma = m["ma"][:, c % 2, :].rearrange("p (h e) -> p h e", e=DH)
                mb = m["mb"][:, c % 2, :].rearrange("p (h e) -> p h e", e=DH)
                cos = m["rots"][:, t, o:o + DH].unsqueeze(1).to_broadcast([P, HC, DH])
                sin = m["rots"][:, t, o + DH:o + 2 * DH].unsqueeze(1).to_broadcast([P, HC, DH])
                V.wait_ge(S["sq_done"], cnt(it, QKC, u, c + 1))
                wait(V, S["add_done"], cnt(it, QKC, u, c - 1))
                V.tensor_tensor(ma, ps, cos, ALU.mult)
                V.tensor_tensor(mb[:, :, 0:32], ps[:, :, 32:64], sin[:, :, 0:32], ALU.mult)
                V.tensor_tensor(mb[:, :, 32:64], ps[:, :, 0:32], sin[:, :, 32:64], ALU.mult).then_inc(S["m_done"], 1)
                V.tensor_reduce(m["ss"][:, HC * c:HC * c + HC],
                                m["sq"][:, c % 2, :].rearrange("p (h e) -> p h e", e=DH), AX.X, ALU.add)\
                    .then_inc(S["red_done"], 1)

        SEED, STEPS = 4 + 3 * NEWTON_DVE, 4 * (NEWTON - NEWTON_DVE)

        def dve_rnorm(it, u):
            n = [0]

            def link(ins):
                n[0] += 1
                ins.then_inc(S["seed"], 1)
                V.wait_ge(S["seed"], cnt(it, SEED, u, n[0]))

            ss, y, t_ = m["ss"][:, :], m["ny"][:, :], m["nt"][:, :]
            V.wait_ge(S["red_done"], cnt(it, QKC, u, QKC))
            wait(V, S["newton"], cnt(it, STEPS, u))
            link(V.tensor_scalar(ss, ss, 1e-24, None, ALU.max))
            link(V.tensor_scalar(t_.bitcast(I32), ss.bitcast(I32), 1, None, ALU.logical_shift_right))
            link(V.tensor_scalar(m["hs"][:, :], ss, -0.5, None, ALU.mult))
            link(V.tensor_scalar(y.bitcast(I32), t_.bitcast(I32), -1.0, float(MAGIC), ALU.mult, ALU.add))
            for i in range(NEWTON_DVE):
                link(V.tensor_tensor(t_, y, y, ALU.mult))
                link(V.tensor_tensor(t_, t_, m["hs"][:, :], ALU.mult))
                step = V.scalar_tensor_tensor(y, t_, 1.5, y, ALU.add, ALU.mult)
                if i < NEWTON_DVE - 1:
                    link(step)
                else:
                    step.then_inc(S["seed"], 1)

        def dve_softmax_in(it, u):
            for n, g in enumerate((1, 0)):
                V.wait_ge(S["s_mm"], cnt(it, 2, u, g + 1))
                s = s_ps[g].rearrange("p (h k) -> p h k", k=2 * WIN)
                V.tensor_reduce(m["mx"][:, g, :], s, AX.X, ALU.max).then_inc(S["max_done"], 1)
                V.wait_ge(S["max_done"], cnt(it, 2, u, n + 1))
                if g == 1:
                    wait(V, S["exp1_done"], cnt(it, 1, u))
                    V.tensor_scalar(m["nmax"][:, :], m["mx"][:, 1, :], -QK_SCALE, None, ALU.mult)\
                        .then_inc(S["bias_done"], 1)
                else:
                    wait(V, S["pT_mm"], cnt(it, 2, u))
                    wait(V, S["den_sum"], cnt(it, 1, u))
                    V.tensor_tensor(m["p"][:, :, 0, :], s, m["mx"][:, 0, :].unsqueeze(2).to_broadcast([P, HP, 2 * WIN]),
                                    ALU.subtract).then_inc(S["sub_done"], 1)

        def dve_den(it, u):
            V.wait_ge(S["exp0_done"], cnt(it, 1, u, 1))
            wait(V, S["den_done"], cnt(it, 1, u))
            V.tensor_reduce(m["den"][:, 0, :], m["p"][:, :, 0, :], AX.X, ALU.add).then_inc(S["den_sum"], 1)
            V.wait_ge(S["den_sum"], cnt(it, 1, u, 1))
            V.wait_ge(S["exp1_done"], cnt(it, 1, u, 1))
            wait(V, S["o_ev"], cnt(it, 2, u - 1))
            V.reciprocal(m["rden"][:, u % 2, :, :], m["den"][:, :, :]).then_inc(S["den_done"], 1)

        def dve_out(it, u):
            V.wait_ge(S["den_done"], cnt(it, 1, u, 1))
            for g in range(2):
                V.wait_ge(S["o_mm"], cnt(it, 2, u, g + 1))
                wait(V, S["oT_mm"], cnt(it, 2, u))
                V.tensor_tensor(m["o"][:, :, g, :], o_ps[g].rearrange("p (h e) -> p h e", e=DH),
                                m["rden"][:, u % 2, g, :].unsqueeze(2).to_broadcast([P, 8, DH]),
                                ALU.mult).then_inc(S["o_ev"], 1)

        def dve_wo(e):
            b = e % B
            V.wait_ge(S["d1_mm"], e + 1)
            V.tensor_tensor(xf[:, b, 1:1 + T], o_ps[0], xf[:, b, 1:1 + T], ALU.add).then_inc(S["d1_ev"], 1)
            V.wait_ge(S["d1_ev"], e + 1)
            wait(V, S["d2_mm"], e)
            V.tensor_scalar(m["xs"][0:64, :], xf[0:64, b, 1:1 + T], 1.0, None, ALU.mult)
            V.tensor_scalar(m["xs"][64:128, :], xf[64:128, b, 0:T], 1.0, None, ALU.mult).then_inc(S["mlp_xs"], 1)

        def dve_rstd(e):
            V.wait_ge(S["std_done"], e + 1)
            wait(V, S["diag_done"], e)
            V.reciprocal(ln_col_rstd[:, :], ln_col_std[:, :]).then_inc(S["rstd_done"], 1)
            V.wait_ge(S["rstd_done"], e + 1)
            wait(V, S["hidden_done"], e)
            V.scalar_tensor_tensor(ln_diag, ident[:, :].unsqueeze(1).to_broadcast([P, TILES, P]), float(P),
                                   ln_col_rstd[:, :].unsqueeze(2).to_broadcast([P, TILES, P]), ALU.mult, ALU.mult)\
                .then_inc(S["diag_done"], 1)

        def dve_norm(e):
            V.wait_ge(S["vec_in"], (e + 1) * 16)
            V.wait_ge(S["d6_mm"], e + 1)
            wait(V, S["d4_mm"], 3 * e)
            V.scalar_tensor_tensor(m["xn"][:, :], ln_xc[:, :], m["vec"][:, 0:1], o_ps[1], ALU.mult, ALU.mult)\
                .then_inc(S["xn1"], 1)
            V.wait_ge(S["xn1"], e + 1)
            V.tensor_scalar(m["xn"][:, :], m["xn"][:, :], m["vec"][:, 1:2], None, ALU.add).then_inc(S["xn2"], 1)

        def dve_hidden(e, j):
            n = DT_TILES[j][1]
            V.wait_ge(S["gelu_done"], 3 * e + j + 1)
            wait(V, S["d5_mm"], e)
            V.scalar_tensor_tensor(m["h"][:n, j, :], o_ps[0][:n, :], m["vec"][:n, 2 + j:3 + j], m["gl"][:n, j % 2, :],
                                   ALU.add, ALU.mult).then_inc(S["hidden_done" if j == 2 else "h_done"], 1)

        def dve_down(e):
            b = e % B
            V.wait_ge(S["d5_mm"], e + 1)
            V.wait_ge(S["d1_ev"], e + 1)
            V.scalar_tensor_tensor(xf[:, b, 1:1 + T], o_ps[0], m["vec"][:, 8:9], xf[:, b, 1:1 + T], ALU.add, ALU.add)\
                .then_inc(S["stream"], 1)

        def dve_body(it, mlp, ahead, more):
            for u in range(TILES):
                proj, nxt = ahead or u + 2 < TILES, ahead or u + 1 < TILES
                if proj:
                    dve_rotate(it, u + 2, (0, 1))
                if mlp and u == 3:
                    dve_hidden(it - 1, 1)
                if mlp and u == 2:
                    dve_norm(it - 1)
                dve_den(it, u)
                if ahead or u + 3 < TILES:
                    dve_xs(it, u + 3)
                if proj:
                    dve_rotate(it, u + 2, (2,))
                if mlp and u == 3:
                    dve_hidden(it - 1, 2)
                if proj:
                    dve_rotate(it, u + 2, (3,))
                if mlp and u == 2:
                    dve_hidden(it - 1, 0)
                if proj:
                    dve_rnorm(it, u + 2)
                if mlp and u == 3:
                    dve_down(it - 1)
                if u == 0 and more:
                    dve_weights(it)
                if u == 0 and ahead:
                    dve_tables(it + 1, 0)
                if mlp and u == 0:
                    dve_wo(it - 1)
                if u == 3 and ahead:
                    dve_tables(it + 1, 1)
                if nxt:
                    dve_softmax_in(it, u + 1)
                if mlp and u == 1:
                    dve_rstd(it - 1)
                dve_out(it, u)

        def dve_weights(it):
            k = it + B
            par, at = (k // 4) % 2, (k % 4) * WQ
            V.wait_ge(S["wstaged"], (k + 1) * 16)
            hi = m["wh"][:, par, bass.ds(at, WQ)]
            V.tensor_scalar(hi, m["wst"][:, 0, :], 1.0, None, ALU.mult).then_inc(S["whi_done"], 1)
            V.wait_ge(S["whi_done"], k + 1)
            V.tensor_tensor(m["wl"][:, par, bass.ds(at, WQ)], m["wst"][:, 0, :], hi.bitcast(F32), ALU.subtract)\
                .then_inc(S["wconv"], 1)

        def dve_ffn(first):
            last = first + PHASE - 1
            dve_tables(first, 0)
            dve_tables(first, 1)
            dve_xs(first, 0)
            dve_xs(first, 1)
            dve_rotate(first, 0, range(QKC))
            dve_rnorm(first, 0)
            dve_xs(first, 2)
            dve_rotate(first, 1, range(QKC))
            dve_rnorm(first, 1)
            dve_softmax_in(first, 0)
            dve_body(first, False, True, True)
            if first == 0:
                dve_body(1, True, True, True)
            with nc.vector.Fori(max(first + 1, 2), last) as it:
                dve_body(it, True, True, True)
            dve_body(last, True, False, first == 0)
            dve_wo(last)
            dve_rstd(last)
            dve_norm(last)
            for j in range(3):
                dve_hidden(last, j)
            dve_down(last)

        G = nc.gpsimd

        def pool_newton(it, u):
            n = [0]

            def link(out, in0, in1, op):
                n[0] += 1
                G.tensor_tensor(out, in0, in1, op).then_inc(S["newton"], 1)
                G.wait_ge(S["newton"], cnt(it, STEPS, u, n[0]))

            y, t_ = m["ny"][:, :], m["nt"][:, :]
            G.wait_ge(S["seed"], cnt(it, SEED, u, SEED))
            wait(G, S["rot_done"], cnt(it, QKC, u - 1))
            for i in range(NEWTON_DVE, NEWTON):
                link(t_, y, y, ALU.mult)
                link(t_, t_, m["hs"][:, :], ALU.mult)
                link(t_, t_, three_halves[:, :], ALU.add)
                link(m["rn"][:, u % 2, :] if i == NEWTON - 1 else y, y, t_, ALU.mult)

        def pool_rotate(it, u):
            qk = m["qk"][:, u % 2, :]
            wait(G, S["qkT_mm"], cnt(it, 4, u - 1))
            for c in range(QKC):
                G.wait_ge(S["m_done"], cnt(it, QKC, u, c + 1))
                G.tensor_tensor(qk[:, c * CH:(c + 1) * CH], m["ma"][:, c % 2, :], m["mb"][:, c % 2, :], ALU.add)\
                    .then_inc(S["add_done"], 1)
            pool_newton(it, u)
            for c in range(QKC):
                G.wait_ge(S["add_done"], cnt(it, QKC, u, c + 1))
                part = qk[:, c * CH:(c + 1) * CH].rearrange("p (h e) -> p h e", e=DH)
                G.tensor_tensor(part, part, m["rn"][:, u % 2, HC * c:HC * c + HC].unsqueeze(2)
                                .to_broadcast([P, HC, DH]), ALU.mult).then_inc(S["rot_done"], 1)

        def pool_ffn(first):
            last = first + PHASE - 1
            G.wait_ge(zeroed, 3)
            for u in range(2):
                pool_rotate(first, u)
            with nc.gpsimd.Fori(first, last) as it:
                for u in range(TILES):
                    pool_rotate(it, u + 2)
            for u in range(2):
                pool_rotate(last, u + 2)

        SP = nc.sync

        def sp_pairs(it, u):
            t = u % TILES
            SP.wait_ge(S["v_ev"], cnt(it, 2, u, 2))
            wait(SP, S["o_mm"], (it * TILES + (u - 1)) * 2)
            for par in range(2):
                for half in range(2):
                    for w in range(WPT):
                        slot, src_w = u % 2, w if half else w - 1
                        if src_w < 0:
                            slot, src_w = ((u - 1) % 2, WPT - 1) if t else (slot, 0)
                        at = 64 * par + 32 * half
                        SP.dma_start(m["vp"][at:at + WIN, u % 2, w, :],
                                     m["v"][WIN * src_w:WIN * src_w + WIN, slot, par, :])\
                            .then_inc(vp_sem[u % 2], 16)

        def sp_weights(k):
            wait(SP, S["wconv"], k)
            SP.dma_start(m["wst"][:, 0, :], a["Wqkv"][(k // 4) % DEPTH, :, bass.ds((k % 4) * WQ, WQ)])\
                .then_inc(S["wstaged"], 16)

        def sp_scales(e):
            wait(SP, S["rots_done"], 2 * e)
            SP.dma_start(m["qks"][:, :], a["qk_scale"][(e // B) % DEPTH, :, :].to_broadcast([P, 4 * DH]))\
                .then_inc(S["qks_in"], 16)

        def sp_wo(e):
            wait(SP, S["d1_mm"], e)
            SP.dma_start(m["wo"][:, :, :], a["Wo"][(e // B) % DEPTH, :, :].rearrange("(h p) n -> p h n", p=P))\
                .then_inc(S["wo_in"], 16)

        def sp_w1(e):
            wait(SP, S["d4_mm"], 3 * e)
            SP.dma_start(m["w1"][:, :], a["W1"][(e // B) % DEPTH, :, :]).then_inc(S["w1_in"], 16)

        def sp_w2(e):
            l = (e // B) % DEPTH
            wait(SP, S["d5_mm"], e)
            SP.dma_start(m["w2"][:, 0:2, :], a["W2"][l, 0:2 * P, :].rearrange("(j p) n -> p j n", p=P))\
                .then_inc(S["w2_in"], 16)
            SP.dma_start(m["w2"][0:DI - 2 * P, 2, :], a["W2"][l, 2 * P:DI, :]).then_inc(S["w2_in"], 16)
            SP.wait_ge(S["stream"], B + e)
            SP.dma_start(m["vec"][:, :], a["vectors"][l, :, :]).then_inc(S["vec_in"], 16)

        def sp_ffn(first):
            last = first + PHASE - 1
            sp_scales(first)
            sp_wo(first)
            sp_w1(first)
            sp_w2(first)
            for u in range(2):
                sp_pairs(first, u)

            def body(it, mlp, ahead, more):
                for u in range(TILES):
                    if u == 0:
                        if ahead:
                            sp_scales(it + 1)
                        if more:
                            sp_weights(it + B + 1)
                    if ahead or u + 2 < TILES:
                        sp_pairs(it, u + 2)
                    if mlp and u == 1:
                        sp_wo(it)
                    if mlp and u == 3:
                        sp_w1(it)
                if mlp:
                    sp_w2(it)

            body(first, False, True, True)
            if first == 0:
                body(1, True, True, True)
            with nc.sync.Fori(max(first + 1, 2), last) as it:
                body(it, True, True, True)
            body(last, True, False, first == 0)

        def pe_ln(stage):
            n = stage * B
            nc.tensor.wait_ge(x_ready, n + B)
            for b in range(B):
                nc.tensor.matmul(psum[:, b, :], center[:, :], xm[:, b, :], start=True, stop=True).then_inc(lnc_mm, 1)
            for b in range(B):
                nc.tensor.wait_ge(lnx_ev, 2 * (n + b + 1))
                for t in range(TILES):
                    last = nc.tensor.matmul(psum[:, B + b, t:t + 1], hidden[:, b % 3, t * P:(t + 1) * P], mean[:, 0:1],
                                            start=True, stop=True)
                last.then_inc(lnv_mm, 1)
            for b in range(B):
                nc.tensor.wait_ge(lnstd_done, n + b + 1)
                nc.tensor.wait_ge(ln_diag_done, n + b + 1)
                nc.tensor.matmul(psum[:, B + b, :], mean[:, :], gelu[:, b % 2, :], start=True, stop=True)\
                    .then_inc(ln_spread, 1)

        def act_ln(stage):
            n = stage * B
            for b in range(B):
                nc.scalar.wait_ge(lnc_mm, n + b + 1)
                nc.scalar.activation(xf[:, b, 1:1 + T], psum[:, b, :], ACT.Copy).then_inc(lnx_ev, 1)
                if b >= 3:
                    nc.scalar.wait_ge(lnv_mm, n + b - 2)
                nc.scalar.activation(hidden[:, b % 3, :], psum[:, b, :], ACT.Square).then_inc(lnx_ev, 1)
            for b in range(B):
                nc.scalar.wait_ge(lnv_mm, n + b + 1)
                nc.scalar.activation(ln_cols[:, 0, b, :], psum[:, B + b, 0:TILES], ACT.Sqrt, bias=eps_t[:, :])\
                    .then_inc(lnstd_done, 1)

        def dve_ln(stage):
            n = stage * B

            def scale(b):
                V.wait_ge(ln_spread, n + b + 1)
                V.tensor_tensor(xf[:, b, 1:1 + T], xf[:, b, 1:1 + T], psum[:, B + b, :], ALU.mult)\
                    .then_inc(ln_done[stage], 1)

            for b in range(B):
                V.wait_ge(lnstd_done, n + b + 1)
                V.reciprocal(ln_cols[:, 1, b, :], ln_cols[:, 0, b, :]).then_inc(ln_rs, 1)
                if b >= 2:
                    scale(b - 2)
                V.wait_ge(ln_rs, n + b + 1)
                V.scalar_tensor_tensor(gelu[:, b % 2, :].rearrange("p (t q) -> p t q", t=TILES),
                                       ident[:, :].unsqueeze(1).to_broadcast([P, TILES, P]), float(P),
                                       ln_cols[:, 1, b, :].unsqueeze(2).to_broadcast([P, TILES, P]),
                                       ALU.mult, ALU.mult).then_inc(ln_diag_done, 1)
            scale(B - 2)
            scale(B - 1)

        def dve_add(stage):
            V.wait_ge(S["stream"], B + PHASE * stage)
            for b in range(B):
                V.tensor_tensor(xm[:, b, :], xm[:, b, :], xf[:, b, 1:1 + T], ALU.add).then_inc(x_ready, 1)

        GLA_IN = (("w", "gla_w"), ("b", "gla_b"), ("wo", "gla_wo"), ("bo", "gla_bo"), ("pick", "gla_pick"))

        def sp_gla(sp):
            for dst, name in GLA_IN:
                sp.dma_start(gb[dst][:], a[name]).then_inc(gs["in"], 16)

        def pe_gla():
            nc.tensor.wait_ge(gs["in"], 16 * len(GLA_IN))
            nc.tensor.wait_ge(ln_done[0], B)
            banks = [proj_ps[0], proj_ps[1], tr_ps[0], tr_ps[1]]
            for j in range(4):
                for b in range(B):
                    last = nc.tensor.matmul(banks[j][GK * b:GK * b + GK, :], gb["w"][:, j, :], xf[:, b, 1:1 + T],
                                            start=True, stop=True)
                last.then_inc(gs["proj_mm"], 1)
            nc.tensor.wait_ge(gs["zero"], 1)
            nc.tensor.wait_ge(gs["proj_ev"], 4)
            nc.tensor.matmul(s_ps[0], gb["zero"][:, :], gb["v"][:, :], start=True, stop=False)

            def gather(v, r):
                nc.tensor.wait_ge(gs["sq"], v + 1)
                nc.tensor.wait_ge(gs["gather_sel"], v + 1)
                nc.tensor.matmul(s_ps[0], gb["gather"][:, r, :], gb["sq"][:, r, :], start=False, stop=False)\
                    .then_inc(gs["sum_mm"], 1)

            def spread(v, r, first=False):
                nc.tensor.wait_ge(gs["spread_sel"], v + 1)
                if not first:
                    nc.tensor.wait_ge(gs["kv"], v - 1)
                nc.tensor.matmul(proj_ps[r % 2], gb["spread"][:, r, :, :].rearrange("p b k -> p (b k)"), gb["v"][:, :],
                                 start=True, stop=True).then_inc(gs["vb_mm"], 1)

            spread(0, 0, True)
            spread(1, 1, True)
            with nc.tensor.Fori(0, GK // RING - 1) as i:
                for r in range(RING):
                    spread(RING * i + (r + 2), (r + 2) % RING)
                    gather(RING * i + r, r)
            for v in range(GK - RING, GK):
                if v + 2 < GK:
                    spread(v + 2, (v + 2) % RING)
                gather(v, v % RING)
            nc.tensor.matmul(s_ps[0], gb["zero"][:, :], gb["v"][:, :], start=False, stop=True).then_inc(gs["sum_mm"], 1)
            nc.tensor.wait_ge(gs["o_ev"], 1)
            for b in range(B):
                if b >= 2:
                    nc.tensor.wait_ge(x_ready, B + b - 1)
                nc.tensor.matmul(tr_ps[b % 2], gb["wo"][:, b, :], gb["o"][:, :], start=True, stop=True)\
                    .then_inc(gs["out_mm"], 1)

        def act_gla():
            nc.scalar.wait_ge(gs["in"], 16 * len(GLA_IN))
            banks = [proj_ps[0], proj_ps[1], tr_ps[0], tr_ps[1]]
            for j, (dst, func) in enumerate((("q", ACT.Identity), ("k", ACT.Sigmoid), ("g", ACT.Sigmoid),
                                             ("v", ACT.Identity))):
                nc.scalar.wait_ge(gs["proj_mm"], j + 1)
                nc.scalar.activation(gb[dst][:, :], banks[j], func, bias=gb["b"][:, j:j + 1]).then_inc(gs["proj_ev"], 1)

            def select(v, r, first=False):
                if not first:
                    nc.scalar.wait_ge(gs["vb_mm"], v - (RING - 1))
                nc.scalar.activation(gb["spread"][:, r, :, :],
                                     ident[:, :].rearrange("p (b v) -> p b v", v=GK)[:, :, bass.ds(v, 1)]
                                     .to_broadcast([P, B, GK]), ACT.Copy).then_inc(gs["spread_sel"], 1)
                if not first:
                    nc.scalar.wait_ge(gs["sum_mm"], v - (RING - 1))
                nc.scalar.activation(gb["gather"][:, r, :], gb["pick"][:, bass.ds(4 * (GK - 1) - 4 * v, P)], ACT.Copy)\
                    .then_inc(gs["gather_sel"], 1)

            nc.scalar.wait_ge(consts, 16 * len(CONSTS))
            for r in range(RING):
                select(r, r, True)
            with nc.scalar.Fori(1, GK // RING) as i:
                for r in range(RING):
                    select(RING * i + r, r)
            nc.scalar.wait_ge(gs["sum_mm"], GK + 1)
            nc.scalar.activation(gb["o"][:, :], s_ps[0], ACT.Copy).then_inc(gs["o_ev"], 1)

        def dve_gla():
            V.memset(gb["zero"][:, :], 0.0).then_inc(gs["zero"], 1)
            V.wait_ge(gs["proj_ev"], 4)

            def one(v, r, first=False):
                V.wait_ge(gs["vb_mm"], v + 1)
                if not first:
                    V.wait_ge(gs["st"], v - (RING - 1))
                V.tensor_tensor(gb["kv"][:, r, :], proj_ps[r % 2], gb["k"][:, :], ALU.mult).then_inc(gs["kv"], 1)
                V.wait_ge(gs["kv"], v + 1)
                if not first:
                    V.wait_ge(gs["sq"], v - (RING - 1))
                V.tensor_tensor_scan(gb["st"][:, r, :], gb["g"][:, :], gb["kv"][:, r, :], 0.0, ALU.mult, ALU.add)\
                    .then_inc(gs["st"], 1)

            for r in range(RING):
                one(r, r, True)
            with nc.vector.Fori(1, GK // RING) as i:
                for r in range(RING):
                    one(RING * i + r, r)
            for b in range(B):
                V.wait_ge(gs["out_mm"], b + 1)
                V.scalar_tensor_tensor(xm[:, b, :], tr_ps[b % 2], gb["bo"][:, :], xm[:, b, :], ALU.add, ALU.add)\
                    .then_inc(x_ready, 1)

        def pool_gla():
            G.wait_ge(gs["proj_ev"], 4)

            def one(v, r, first=False):
                G.wait_ge(gs["st"], v + 1)
                if not first:
                    G.wait_ge(gs["sum_mm"], v - (RING - 1))
                G.tensor_tensor(gb["sq"][:, r, :], gb["st"][:, r, :], gb["q"][:, :], ALU.mult).then_inc(gs["sq"], 1)

            for r in range(RING):
                one(r, r, True)
            with nc.gpsimd.Fori(1, GK // RING) as i:
                for r in range(RING):
                    one(RING * i + r, r)

        MB_IN = (("win", "mb_in_w"), ("conv", "mb_conv"), ("cols", "mb_cols"), ("xw", "mb_x_w"), ("dtw", "mb_dt_w"),
                 ("alog", "mb_alog"), ("wout", "mb_out_w"), ("part", "mb_part"), ("bc", "mb_bc_pick"))

        def sp_mamba(sp):
            sp.wait_ge(x_ready, 3 * B)
            for dst, name in MB_IN:
                sp.dma_start(mb[dst][:], a[name]).then_inc(ms["in"], 16)

        def pe_mamba():
            T_ = nc.tensor
            T_.wait_ge(ms["in"], len(MB_IN) * 16)
            T_.wait_ge(ln_done[2], B)

            def batch(b, first):
                if not first:
                    T_.wait_ge(ms["bu"], 32 * b)
                    T_.wait_ge(ms["c_ev"], 16 * b)
                for j in range(4):
                    last = T_.matmul(psum[:, j, :], mb["win"][:, P * j:P * j + P], xf[:, b, 1:1 + T],
                                     start=True, stop=True)
                    last.then_inc(ms["in_mm"], 1)
                T_.wait_ge(ms["u_ev"], b + 1)
                for j in range(2):
                    last = T_.matmul(psum[0:3 * XPW, 6, :], mb["xw"][:, j, :], mb["u"][:, j, :],
                                     start=(j == 0), stop=(j == 1))
                last.then_inc(ms["xd_mm"], 1)
                T_.wait_ge(ms["xd_ev"], b + 1)
                T_.wait_ge(ms["x_ev"], b + 1)
                for j in range(2):
                    last = T_.matmul(psum[:, j, :], mb["dtw"][:, P * j:P * j + P], mb["xd"][0:RANK, :],
                                     start=True, stop=True)
                last.then_inc(ms["dt_mm"], 1)
                T_.wait_ge(ms["split"], 6 * b + 6)
                T_.wait_ge(ms["dt_ev"], b + 1)
                T_.wait_ge(ms["z_ev"], b + 1)

                def spread(n):
                    if n >= 2:
                        T_.wait_ge(ms["bu"], 32 * b + 2 * (n - 1))
                        T_.wait_ge(ms["c_ev"], 16 * b + (n - 1))
                    T_.matmul(psum[:, n % 2, :], mb["bc"][:, n, :], mb["parts"][:, :], start=True, stop=True)\
                        .then_inc(ms["b_mm"], 1)
                    T_.matmul(psum[:, 2 + n % 2, :], mb["bc"][:, NST + n, :], mb["parts"][:, :], start=True, stop=True)\
                        .then_inc(ms["c_mm"], 1)

                spread(0)
                spread(1)
                for n in range(NST):
                    if n + 2 < NST:
                        spread(n + 2)
                    for j in range(2):
                        T_.wait_ge(ms["hc"], 32 * b + 2 * n + j + 1)
                        if n == 0 and not first:
                            T_.wait_ge(ms["yo"], 4 * b)
                        T_.matmul(psum[:, 4 + j, :], ident[:, :], mb["hc"][:, n % 2, j, :], start=(n == 0), stop=(n == NST - 1))\
                            .then_inc(ms["y_mm"], 1)
                T_.wait_ge(ms["yo"], 4 * b + 4)
                if not first:
                    T_.wait_ge(x_ready, b + 3 * B)
                for j in range(2):
                    last = T_.matmul(psum[:, 7, :], mb["wout"][:, j, :], mb["yo"][:, j, :], start=(j == 0), stop=(j == 1))
                last.then_inc(ms["out_mm"], 1)

            batch(0, True)
            with T_.Fori(1, B) as b:
                batch(b, False)

        def act_mamba():
            A_ = nc.scalar
            A_.wait_ge(ms["in"], len(MB_IN) * 16)
            A_.activation(mb["a"][:, :, :], mb["alog"][:, :, :], ACT.Exp).then_inc(ms["a1"], 1)

            def batch(b, first):
                A_.wait_ge(ms["in_mm"], 4 * b + 2)
                if not first:
                    A_.wait_ge(ms["conv"], 8 * b)
                A_.activation(mb["xp"][:, :, SHIFT:], psum[:, 0:2, :], ACT.Copy).then_inc(ms["x_ev"], 1)
                A_.wait_ge(ms["in_mm"], 4 * b + 4)
                if not first:
                    A_.wait_ge(ms["yo"], 4 * b)
                A_.activation(mb["zs"][:, :, :], psum[:, 2:4, :], ACT.Silu).then_inc(ms["z_ev"], 1)
                A_.wait_ge(ms["conv"], 8 * b + 8)
                for j in range(2):
                    last = A_.activation(mb["u"][:, j, :], mb["cv"][:, j, :], ACT.Silu, bias=mb["cols"][:, j, 0:1])
                last.then_inc(ms["u_ev"], 1)
                A_.wait_ge(ms["xd_mm"], b + 1)
                if not first:
                    A_.wait_ge(ms["dt_mm"], b)
                    A_.wait_ge(ms["split"], 6 * b)
                A_.activation(mb["xd"][:, :], psum[0:3 * XPW, 6, :], ACT.Copy).then_inc(ms["xd_ev"], 1)
                A_.wait_ge(ms["dt_ev"], b + 1)
                A_.activation(mb["ab"][:, :, :], mb["y"][:, :, :], ACT.Abs).then_inc(ms["abs"], 1)
                A_.wait_ge(ms["abs"], b + 1)
                A_.activation(mb["e"][:, :, :], mb["ab"][:, :, :], ACT.Exp, scale=-1.0).then_inc(ms["exp"], 1)
                A_.wait_ge(ms["poly"], (len(LOG1P) + 2) * b + (len(LOG1P) + 2))
                A_.wait_ge(ms["a2"], 1)
                for n in range(NST):
                    for j in range(2):
                        if not (first and n < 2):
                            A_.wait_ge(ms["h"], 32 * b + 2 * n + j - 3)
                        A_.activation(mb["da"][:, n % 2, j, :], mb["dl"][:, j, :], ACT.Exp, scale=mb["a"][:, j, n:n + 1])\
                            .then_inc(ms["da"], 1)
                    A_.wait_ge(ms["c_mm"], 16 * b + n + 1)
                    if not (first and n < 2):
                        A_.wait_ge(ms["hc"], 32 * b + 2 * (n - 1))
                    A_.activation(mb["c"][:, n % 2, :], psum[:, 2 + n % 2, :], ACT.Copy).then_inc(ms["c_ev"], 1)

            batch(0, True)
            with A_.Fori(1, B) as b:
                batch(b, False)

        def dve_mamba():
            V.wait_ge(ms["in"], len(MB_IN) * 16)
            V.memset(mb["xp"][:, :, 0:SHIFT], 0.0).then_inc(ms["zero"], 1)
            V.wait_ge(ms["a1"], 1)
            V.tensor_scalar(mb["a"][:, :, :], mb["a"][:, :, :], -1.0, None, ALU.mult).then_inc(ms["a2"], 1)
            V.wait_ge(ms["zero"], 1)
            NP_ = len(LOG1P) + 2

            def batch(b, first):
                V.wait_ge(ms["x_ev"], b + 1)
                if not first:
                    V.wait_ge(ms["u_ev"], b)
                for k in range(CONV):
                    for j in range(2):
                        src, tap = mb["xp"][:, j, k:k + T], mb["conv"][:, j, k:k + 1]
                        if k == 0:
                            V.tensor_scalar(mb["cv"][:, j, :], src, tap, None, ALU.mult).then_inc(ms["conv"], 1)
                        else:
                            V.wait_ge(ms["conv"], 8 * b + (2 * (k - 1) + j + 1))
                            V.scalar_tensor_tensor(mb["cv"][:, j, :], src, tap, mb["cv"][:, j, :], ALU.mult, ALU.add)\
                                .then_inc(ms["conv"], 1)
                V.wait_ge(ms["dt_mm"], b + 1)
                for j in range(2):
                    bias = mb["cols"][:, j, 1:2]
                    last = V.tensor_scalar(mb["y"][:, j, :], psum[:, j, :], bias, bias, ALU.add, ALU.add)
                last.then_inc(ms["dt_ev"], 1)
                V.wait_ge(ms["xd_ev"], b + 1)
                part = mb["part"]
                if not first:
                    V.wait_ge(ms["c_mm"], 16 * b)
                V.tensor_copy(mb["hi"][:, :], mb["xd"][:, :]).then_inc(ms["split"], 1)
                V.wait_ge(ms["split"], 6 * b + 1)
                V.tensor_tensor(mb["r1"][:, :], mb["xd"][:, :], mb["hi"][:, :], ALU.subtract).then_inc(ms["split"], 1)
                V.wait_ge(ms["split"], 6 * b + 2)
                V.tensor_copy(mb["mid"][:, :], mb["r1"][:, :]).then_inc(ms["split"], 1)
                V.tensor_scalar(mb["pa"][:, :], mb["hi"][:, :], part[:, 0:1], None, ALU.mult)
                V.wait_ge(ms["split"], 6 * b + 3)
                V.tensor_tensor(mb["r2"][:, :], mb["r1"][:, :], mb["mid"][:, :], ALU.subtract).then_inc(ms["split"], 1)
                V.wait_ge(ms["split"], 6 * b + 4)
                V.scalar_tensor_tensor(mb["pb"][:, :], mb["mid"][:, :], part[:, 1:2], mb["pa"][:, :], ALU.mult, ALU.add)\
                    .then_inc(ms["split"], 1)
                V.wait_ge(ms["split"], 6 * b + 5)
                V.scalar_tensor_tensor(mb["parts"][:, :], mb["r2"][:, :], part[:, 2:3], mb["pb"][:, :],
                                       ALU.mult, ALU.add).then_inc(ms["split"], 1)
                V.wait_ge(ms["exp"], b + 1)
                if not first:
                    V.wait_ge(ms["da"], 32 * b)
                e, pl = mb["e"][:, :, :], mb["pl"][:, :, :]
                V.tensor_scalar(pl, e, LOG1P[-1], None, ALU.mult).then_inc(ms["poly"], 1)
                for i, c in enumerate(LOG1P[-2::-1]):
                    V.wait_ge(ms["poly"], NP_ * b + (i + 1))
                    V.scalar_tensor_tensor(pl, pl, c, e, ALU.add, ALU.mult).then_inc(ms["poly"], 1)
                V.wait_ge(ms["poly"], NP_ * b + (NP_ - 2))
                V.scalar_tensor_tensor(mb["dl"][:, :, :], mb["y"][:, :, :], 0.0, pl, ALU.max, ALU.add)\
                    .then_inc(ms["poly"], 1)
                V.wait_ge(ms["poly"], NP_ * b + (NP_ - 1))
                V.tensor_tensor(mb["du"][:, :, :], mb["dl"][:, :, :], mb["u"][:, :, :], ALU.mult).then_inc(ms["poly"], 1)
                V.wait_ge(ms["poly"], NP_ * b + NP_)
                for n in range(NST):
                    V.wait_ge(ms["b_mm"], 16 * b + n + 1)
                    for j in range(2):
                        k = 2 * n + j
                        if not (first and n < 2):
                            V.wait_ge(ms["h"], 32 * b + k - 3)
                        V.tensor_tensor(mb["bu"][:, n % 2, j, :], psum[:, n % 2, :], mb["du"][:, j, :], ALU.mult)\
                            .then_inc(ms["bu"], 1)
                    for j in range(2):
                        k = 2 * n + j
                        V.wait_ge(ms["bu"], 32 * b + k + 1)
                        V.wait_ge(ms["da"], 32 * b + k + 1)
                        if not (first and n < 2):
                            V.wait_ge(ms["hc"], 32 * b + k - 3)
                        V.tensor_tensor_scan(mb["h"][:, n % 2, j, :], mb["da"][:, n % 2, j, :],
                                             mb["bu"][:, n % 2, j, :], 0.0,
                                             ALU.mult, ALU.add).then_inc(ms["h"], 1)
                V.wait_ge(ms["y_mm"], 32 * b + 32)
                if not first:
                    V.wait_ge(ms["out_mm"], b)
                for j in range(2):
                    V.scalar_tensor_tensor(mb["yo"][:, j, :], mb["u"][:, j, :], mb["cols"][:, j, 2:3],
                                           psum[:, 4 + j, :], ALU.mult, ALU.add).then_inc(ms["yo"], 1)
                V.wait_ge(ms["z_ev"], b + 1)
                for j in range(2):
                    V.wait_ge(ms["yo"], 4 * b + (j + 1))
                    V.tensor_tensor(mb["yo"][:, j, :], mb["yo"][:, j, :], mb["zs"][:, j, :], ALU.mult)\
                        .then_inc(ms["yo"], 1)
                V.wait_ge(ms["out_mm"], b + 1)
                V.tensor_tensor(xm[:, b, :], xm[:, b, :], psum[:, 7, :], ALU.add).then_inc(x_ready, 1)

            batch(0, True)
            with nc.vector.Fori(1, B) as b:
                batch(b, False)

        def pool_mamba():
            def batch(b, first):
                for n in range(NST):
                    G.wait_ge(ms["c_ev"], 16 * b + n + 1)
                    for j in range(2):
                        k = 2 * n + j
                        G.wait_ge(ms["h"], 32 * b + k + 1)
                        if not (first and n < 2):
                            G.wait_ge(ms["y_mm"], 32 * b + k - 3)
                        G.tensor_tensor(mb["hc"][:, n % 2, j, :], mb["h"][:, n % 2, j, :], mb["c"][:, n % 2, :], ALU.mult)\
                            .then_inc(ms["hc"], 1)

            batch(0, True)
            with nc.gpsimd.Fori(1, B) as b:
                batch(b, False)

        block = ctx.enter_context(nc.Block())
        xin = a["x"].rearrange("b (t p) c -> p (b t) c", p=P)
        xout = a["out"].rearrange("b (t p) c -> p (b t) c", p=P)
        xrows = m["qk"][:, :, :].rearrange("p u n -> p (u n)")[:, 0:2 * 1024].rearrange("p (n c) -> p n c", c=D)

        @block.sync
        def _(sp):
            sp.dma_start(xrows, xin).then_inc(x_in, 16)
            for dst, name in CONSTS:
                sp.dma_start(dst[:], a[name]).then_inc(consts, 16)
            sp_gla(sp)
            for k in range(B + 1):
                sp_weights(k)
            sp.wait_ge(x_ready, 2 * B)
            sp.dma_start(m["rot"][:], a["rot"]).then_inc(rot_in, 16)
            sp_ffn(0)
            sp_mamba(sp)
            sp.wait_ge(x_ready, 4 * B)
            sp.dma_start(m["rot"][:], a["rot"]).then_inc(rot_in, 16)
            sp_ffn(PHASE)
            sp.wait_ge(out_ev, 4)
            sp.dma_start(xout, xrows).then_inc(out_st, 16)
            sp.wait_ge(out_st, 16)

        @block.tensor
        def _(pe):
            pe.wait_ge(consts, 16 * len(CONSTS))
            pe.wait_ge(x_in, 16)
            for g in range(B):
                if g >= 2:
                    pe.wait_ge(x_ready, g - 1)
                for i in range(4):
                    last = nc.tensor.transpose(tr_ps[g % 2][:, i * P:(i + 1) * P], xrows[:, 4 * g + i, :], ident[:, :])
                last.then_inc(x_tr, 1)
            pe_ln(0)
            pe_gla()
            pe_ln(1)
            pe_ffn(0)
            pe_ln(2)
            pe_mamba()
            pe_ln(3)
            pe_ffn(PHASE)
            for g in range(B):
                pe.wait_ge(x_ready, 4 * B + g + 1)
                if g >= 2:
                    pe.wait_ge(out_ev, g - 1)
                for i in range(4):
                    last = nc.tensor.transpose(tr_ps[g % 2][:, i * P:(i + 1) * P], xm[:, g, i * P:(i + 1) * P], ident[:, :])
                last.then_inc(out_tr, 1)

        @block.scalar
        def _(act):
            act.wait_ge(zeroed, 3)
            act_ln(0)
            act_gla()
            act_ln(1)
            act_ffn(0)
            act_ln(2)
            act_mamba()
            act_ln(3)
            act_ffn(PHASE)
            for g in range(B):
                act.wait_ge(out_tr, g + 1)
                nc.scalar.activation(xrows[:, 4 * g:4 * g + 4, :], tr_ps[g % 2].rearrange("p (i c) -> p i c", i=4),
                                     ACT.Copy).then_inc(out_ev, 1)

        def dve_ffn_start(n, stage):
            V.memset(m["kt"][:, :, 0:WIN], 0.0).then_inc(zeroed, 1)
            V.wait_ge(rot_in, 16 * n)
            V.wait_ge(ln_done[stage], B)
            V.wait_ge(zeroed, 3 + n)

        @block.vector
        def _(dve):
            V.memset(xf[:, :, 0:1], 0.0).then_inc(zeroed, 1)
            V.memset(eps_t[:, :], EPS).then_inc(zeroed, 1)
            V.memset(three_halves[:, :], 1.5).then_inc(zeroed, 1)
            for g in range(B):
                V.wait_ge(x_tr, g + 1)
                V.tensor_copy(xm[:, g, :], tr_ps[g % 2]).then_inc(x_ready, 1)
            dve_weights(-4)
            dve_weights(-3)
            dve_ln(0)
            dve_weights(-2)
            dve_weights(-1)
            dve_gla()
            dve_ln(1)
            dve_ffn_start(1, 1)
            dve_ffn(0)
            dve_add(1)
            dve_ln(2)
            dve_mamba()
            dve_ln(3)
            dve_ffn_start(2, 3)
            dve_ffn(PHASE)
            dve_add(2)

        @block.gpsimd
        def _(pool):
            pool_gla()
            pool_ffn(0)
            pool_mamba()
            pool_ffn(PHASE)


def constants():
    half = np.arange(0, DH, 2, dtype=np.float32)
    inv_freq = (1.0 / np.power(np.float32(10000.0), half / np.float32(DH))).astype(np.float32)
    t = np.arange(T, dtype=np.float32)
    freqs = t[:, None] * inv_freq[None, :]
    base = (half + np.float32(0.4 * DH)) / np.float32(1.4 * DH)
    power = (t - T // 2) / np.float32(WIN // 2)
    scale = np.power(base[None, :], power[:, None]).astype(np.float32)
    cos, sin = np.cos(freqs), np.sin(freqs)
    inv = np.float32(1.0) / scale

    def two(x, y):
        return np.concatenate([x, y], -1)

    rot = np.concatenate([two(cos * scale, cos * scale), two(-sin * scale, sin * scale),
                          two(cos * inv, cos * inv), two(-sin * inv, sin * inv)], -1).astype(np.float32)
    rot = rot.reshape(TILES, P, 4 * DH).transpose(1, 0, 2)
    tau = np.arange(WIN)
    prev = np.where(tau[:, None] > tau[None, :], MASKED, 0.0)
    own = np.where(tau[:, None] < tau[None, :], MASKED, 0.0)
    maskrow = np.zeros((64, HC, 2 * WIN), np.float32)
    maskrow[:WIN] = np.concatenate([prev, own], 1)[:, None, :]
    maskrow[WIN, :, :WIN] = MASKED
    onehot = np.zeros((64, 2, P), np.float32)
    onehot[:WIN] = np.tile(np.eye(WIN), (1, WPT))[:, None, :]
    onehot[WIN, 1, :WIN] = 1.0
    bf = mybir.dt.np(BF16)
    pick = np.zeros((P, 4 * (2 * GK - 1)), np.float32)
    pick[np.arange(P), 4 * (GK - 1) + np.arange(P) // GK] = 1.0
    bc = np.zeros((3 * XPW, 2 * NST, P), np.float32)
    part = np.zeros((3 * XPW, 3), np.float32)
    for i in range(3):
        part[i * XPW:(i + 1) * XPW, i] = 1.0
        for n in range(2 * NST):
            bc[i * XPW + RANK + n, n, :] = 1.0
    return {"gla_pick": pick, "mb_part": part, "mb_bc_pick": bc.astype(bf), "rot": np.ascontiguousarray(rot), "maskrow": np.tile(maskrow.reshape(64, CH), (2, 1)).astype(bf),
            "onehot": np.tile(onehot, (2, 1, 1)).astype(bf), "ident": np.eye(P, dtype=np.float32),
            "center": (np.eye(P) - 1.0 / P).astype(np.float32), "mean": np.full((P, P), 1.0 / P, np.float32)}


def layout(inputs):
    f = {k: np.asarray(v) for k, v in inputs.items()}
    r = {"x": f["L0_attn_a_hidden_state"], "Wqkv": f["L0_ffn_Wqkv"], "Wo": f["L0_ffn_Wo"], "W1": f["L0_ffn_W1"],
         "W2": f["L0_ffn_W2"]}
    qs, ks = f["L0_ffn_q_scale"], f["L0_ffn_k_scale"]
    swap = np.concatenate([np.arange(DH // 2, DH), np.arange(DH // 2)])
    r["qk_scale"] = np.concatenate([qs, qs[:, swap], ks, ks[:, swap]], -1)[:, None, :]
    vec = np.zeros((DEPTH, P, NVEC), np.float32)
    vec[:, :, 0] = f["L0_ffn_ln_g"]
    vec[:, :, 1] = f["L0_ffn_ln_b"]
    for j, (at, n) in enumerate(DT_TILES):
        vec[:, :n, 2 + j] = f["L0_ffn_b1"][:, at:at + n]
        vec[:, :n, 5 + j] = f["L0_ffn_b1"][:, DI + at:DI + at + n]
    vec[:, :, 8] = f["L0_ffn_b2"]
    r["vectors"] = vec

    def chan(x):
        return x.reshape(2, P, -1).transpose(1, 0, 2)

    g = {n: f["L0_attn_a_" + n] for n in ("Wq", "bq", "Wk", "bk", "Wv", "bv", "Wg", "bg", "Wo", "bo")}
    r["gla_w"] = np.stack([g["Wq"], g["Wk"], g["Wg"], g["Wv"]], 1)
    r["gla_b"] = np.tile(np.stack([g["bq"], g["bk"], g["bg"], g["bv"]], 1), (B, 1))
    wo = np.zeros((GK, B, B, D), np.float32)
    for b in range(B):
        wo[:, b, b, :] = g["Wo"]
    r["gla_wo"] = wo.reshape(P, B, D)
    r["gla_bo"] = g["bo"][:, None]
    h = {n: f["L0_attn_b_" + n] for n in ("in_proj_w", "conv_w", "conv_b", "x_proj_w", "dt_proj_w", "dt_proj_b",
                                          "A_log", "D_skip", "out_proj_w")}
    r["mb_in_w"] = h["in_proj_w"]
    r["mb_conv"] = chan(h["conv_w"])
    r["mb_cols"] = chan(np.stack([h["conv_b"], h["dt_proj_b"], h["D_skip"]], 1))
    r["mb_x_w"] = chan(np.concatenate([h["x_proj_w"]] * 3, 1))
    r["mb_dt_w"] = h["dt_proj_w"]
    r["mb_alog"] = chan(h["A_log"])
    r["mb_out_w"] = chan(h["out_proj_w"])
    return {k: np.ascontiguousarray(v) for k, v in (r | constants()).items()}


def kernel(**inputs):
    import numpy as np
    import concourse.bacc as bacc
    from concourse import mybir
    from concourse.bass_utils import run_bass_kernel_spmd

    arrays = {"in_" + name: value for name, value in layout(inputs).items()}
    nc = bacc.Bacc("TRN2", target_bir_lowering=False, num_devices=1)
    tensors = {name[3:]: nc.dram_tensor(name, value.shape, mybir.dt.from_np(value.dtype), kind="ExternalInput").ap()
               for name, value in arrays.items()}
    tensors["out"] = nc.dram_tensor("out_x", (B, T, D), F32, kind="ExternalOutput").ap()
    build(nc, tensors)
    result = run_bass_kernel_spmd(nc, [arrays], core_ids=[0])
    return result.results[0]["out_x"]
```
